# Optimizing a Trainium2 kernel written in Bass

```python
import numpy as np
import jax
import jax.numpy as jnp

def _softmax(x, axis=-1):
    return jax.nn.softmax(x, axis=axis)

def _gelu(x):
    return jax.nn.gelu(x, approximate=True)

def _silu(x):
    return jax.nn.silu(x)

def _sigmoid(x):
    return jax.nn.sigmoid(x)

def _layernorm(x, axis=-1, eps=1e-05):
    m = jnp.mean(x, axis=axis, keepdims=True)
    v = jnp.var(x, axis=axis, keepdims=True)
    return (x - m) / jnp.sqrt(v + eps)

def _scatter_add(tgt, idx, src, axis=0):
    return tgt.at[idx].add(src)

def _segment_sum(src, seg, n):
    return jax.ops.segment_sum(src, seg, n)
kernel_name = 'mk_seq_preln_d1_jaxref_r8_70b7c2'

def setup_inputs(seed: int=0):
    np.random.seed(seed)
    _w = jnp.asarray

    def _L0_attn_setup():
        import jax, jax.numpy as jnp
        import numpy as np
        from jax import lax
        B, T, D_MODEL = (4, 256, 256)
        EXPAND, D_CONV = (2, 4)
        D_INNER = D_MODEL * EXPAND

        def _forward(x, w_in, w_out, conv_w, conv_b, D):
            x_proj = jnp.einsum('btc,dc->btd', x, w_in)
            xi, gate = jnp.split(x_proj, 2, axis=-1)
            xc = jnp.transpose(xi, (0, 2, 1))
            xc = lax.conv_general_dilated(xc, conv_w, window_strides=(1,), padding=[(D_CONV - 1, 0)], dimension_numbers=('NCH', 'OIH', 'NCH'), feature_group_count=D_INNER) + conv_b[None, :, None]
            xc = jnp.transpose(xc, (0, 2, 1))
            h = jax.nn.silu(xc) * D[None, None, :] * jax.nn.silu(gate)
            return jnp.einsum('btd,cd->btc', h, w_out)
        key = jax.random.key(seed)
        ks = jax.random.split(key, 5)
        x = jax.random.normal(ks[0], (B, T, D_MODEL), dtype=jnp.float32)
        w_in = jax.random.normal(ks[1], (2 * D_INNER, D_MODEL), dtype=jnp.float32) * D_MODEL ** (-0.5)
        w_out = jax.random.normal(ks[2], (D_MODEL, D_INNER), dtype=jnp.float32) * D_INNER ** (-0.5)
        conv_w = jax.random.normal(ks[3], (D_INNER, 1, D_CONV), dtype=jnp.float32) * D_CONV ** (-0.5)
        conv_b = jax.random.normal(ks[4], (D_INNER,), dtype=jnp.float32) * 0.02
        D = jnp.ones((D_INNER,), dtype=jnp.float32)
        return {'x': x, 'w_in': w_in, 'w_out': w_out, 'conv_w': conv_w, 'conv_b': conv_b, 'D': D}
    _L0_attn_in = _L0_attn_setup()

    def _L0_ffn_setup():
        import jax, jax.numpy as jnp
        import numpy as np
        import math
        B, S, D = (2, 256, 256)
        H, HD = (16, 128)
        E, I = (4, 256)
        TOP_K = 2
        ROPE_THETA = 10000.0

        def _layernorm(x, w, b):
            mu = jnp.mean(x, axis=-1, keepdims=True)
            var = jnp.mean(jnp.square(x - mu), axis=-1, keepdims=True)
            return (x - mu) * jax.lax.rsqrt(var + 1e-05) * w + b

        def _rotate_half(x):
            x1, x2 = jnp.split(x, 2, axis=-1)
            return jnp.concatenate((-x2, x1), axis=-1)

        def _attention(h, wq, bq, wk, bk, wv, bv, wo, bo):
            b, s, _ = h.shape
            q = (h @ wq + bq).reshape(b, s, H, HD).transpose(0, 2, 1, 3)
            k = (h @ wk + bk).reshape(b, s, H, HD).transpose(0, 2, 1, 3)
            v = (h @ wv + bv).reshape(b, s, H, HD).transpose(0, 2, 1, 3)
            inv_freq = 1.0 / ROPE_THETA ** (jnp.arange(0, HD, 2, dtype=jnp.float32) / HD)
            freqs = jnp.arange(s, dtype=jnp.float32)[:, None] * inv_freq[None, :]
            emb = jnp.concatenate((freqs, freqs), axis=-1)
            cos = jnp.cos(emb)[None, None]
            sin = jnp.sin(emb)[None, None]
            q = q * cos + _rotate_half(q) * sin
            k = k * cos + _rotate_half(k) * sin
            scores = jnp.einsum('bhqd,bhkd->bhqk', q, k) / math.sqrt(HD)
            causal = jnp.tril(jnp.ones((s, s), bool))
            scores = jnp.where(causal[None, None], scores, jnp.finfo(jnp.float32).min)
            probs = jax.nn.softmax(scores.astype(jnp.float32), axis=-1).astype(q.dtype)
            out = jnp.einsum('bhqk,bhkd->bhqd', probs, v)
            out = out.transpose(0, 2, 1, 3).reshape(b, s, H * HD)
            return out @ wo + bo

        def _moe(h, w_gate, we1, be1, we2, be2):
            b, s, d = h.shape
            x = h.reshape(-1, d)
            t = x.shape[0]
            raw = jax.nn.softmax(x @ w_gate, axis=-1)
            top_vals, top_idx = jax.lax.top_k(raw, TOP_K)
            w = jax.nn.softmax(top_vals, axis=-1)
            comb = jnp.zeros((t, E), x.dtype).at[jnp.arange(t)[:, None], top_idx].add(w)
            hmid = jax.nn.gelu(jnp.einsum('td,edi->tei', x, we1) + be1[None], approximate=False)
            eout = jnp.einsum('tei,eid->ted', hmid, we2) + be2[None]
            out = jnp.einsum('te,ted->td', comb, eout)
            return out.reshape(b, s, d)
        key = jax.random.key(seed)
        ks = jax.random.split(key, 20)
        s = 0.02
        p = {'hidden_states': jax.random.normal(ks[0], (B, S, D), jnp.float32), 'wq': jax.random.normal(ks[1], (D, H * HD), jnp.float32) * s, 'bq': jnp.zeros((H * HD,), jnp.float32), 'wk': jax.random.normal(ks[2], (D, H * HD), jnp.float32) * s, 'bk': jnp.zeros((H * HD,), jnp.float32), 'wv': jax.random.normal(ks[3], (D, H * HD), jnp.float32) * s, 'bv': jnp.zeros((H * HD,), jnp.float32), 'wo': jax.random.normal(ks[4], (H * HD, D), jnp.float32) * s, 'bo': jnp.zeros((D,), jnp.float32), 'ln1_w': jnp.ones((D,), jnp.float32), 'ln1_b': jnp.zeros((D,), jnp.float32), 'ln2_w': jnp.ones((D,), jnp.float32), 'ln2_b': jnp.zeros((D,), jnp.float32), 'w_gate': jax.random.normal(ks[5], (D, E), jnp.float32) * s, 'we1': jax.random.normal(ks[6], (E, D, I), jnp.float32) * s, 'be1': jnp.zeros((E, I), jnp.float32), 'we2': jax.random.normal(ks[7], (E, I, D), jnp.float32) * s, 'be2': jnp.zeros((E, D), jnp.float32)}
        return p
    _L0_ffn_in = _L0_ffn_setup()
    _d = {'L0_attn_x': _L0_attn_in['x'], 'L0_attn_w_in': _L0_attn_in['w_in'], 'L0_attn_w_out': _L0_attn_in['w_out'], 'L0_attn_conv_w': _L0_attn_in['conv_w'], 'L0_attn_conv_b': _L0_attn_in['conv_b'], 'L0_attn_D': _L0_attn_in['D'], 'L0_ffn_wq': _L0_ffn_in['wq'], 'L0_ffn_bq': _L0_ffn_in['bq'], 'L0_ffn_wk': _L0_ffn_in['wk'], 'L0_ffn_bk': _L0_ffn_in['bk'], 'L0_ffn_wv': _L0_ffn_in['wv'], 'L0_ffn_bv': _L0_ffn_in['bv'], 'L0_ffn_wo': _L0_ffn_in['wo'], 'L0_ffn_bo': _L0_ffn_in['bo'], 'L0_ffn_ln1_w': _L0_ffn_in['ln1_w'], 'L0_ffn_ln1_b': _L0_ffn_in['ln1_b'], 'L0_ffn_ln2_w': _L0_ffn_in['ln2_w'], 'L0_ffn_ln2_b': _L0_ffn_in['ln2_b'], 'L0_ffn_w_gate': _L0_ffn_in['w_gate'], 'L0_ffn_we1': _L0_ffn_in['we1'], 'L0_ffn_be1': _L0_ffn_in['be1'], 'L0_ffn_we2': _L0_ffn_in['we2'], 'L0_ffn_be2': _L0_ffn_in['be2']}
    _x0 = _d['L0_attn_x']
    _d['L0_attn_x'] = jax.random.normal(jax.random.fold_in(jax.random.key(seed), 1), (2, 1024, 256), dtype=_x0.dtype)
    del _x0
    return _d

def reference(L0_attn_x, L0_attn_w_in, L0_attn_w_out, L0_attn_conv_w, L0_attn_conv_b, L0_attn_D, L0_ffn_wq, L0_ffn_bq, L0_ffn_wk, L0_ffn_bk, L0_ffn_wv, L0_ffn_bv, L0_ffn_wo, L0_ffn_bo, L0_ffn_ln1_w, L0_ffn_ln1_b, L0_ffn_ln2_w, L0_ffn_ln2_b, L0_ffn_w_gate, L0_ffn_we1, L0_ffn_be1, L0_ffn_we2, L0_ffn_be2):

    def _L0_attn_ref(x, w_in, w_out, conv_w, conv_b, D):
        import jax, jax.numpy as jnp
        import numpy as np
        from jax import lax
        B, T, D_MODEL = (4, 256, 256)
        EXPAND, D_CONV = (2, 4)
        D_INNER = D_MODEL * EXPAND

        def _forward(x, w_in, w_out, conv_w, conv_b, D):
            x_proj = jnp.einsum('btc,dc->btd', x, w_in)
            xi, gate = jnp.split(x_proj, 2, axis=-1)
            xc = jnp.transpose(xi, (0, 2, 1))
            xc = lax.conv_general_dilated(xc, conv_w, window_strides=(1,), padding=[(D_CONV - 1, 0)], dimension_numbers=('NCH', 'OIH', 'NCH'), feature_group_count=D_INNER) + conv_b[None, :, None]
            xc = jnp.transpose(xc, (0, 2, 1))
            h = jax.nn.silu(xc) * D[None, None, :] * jax.nn.silu(gate)
            return jnp.einsum('btd,cd->btc', h, w_out)
        return _forward(x, w_in, w_out, conv_w, conv_b, D)

    def _L0_ffn_ref(hidden_states, wq, bq, wk, bk, wv, bv, wo, bo, ln1_w, ln1_b, ln2_w, ln2_b, w_gate, we1, be1, we2, be2):
        import jax, jax.numpy as jnp
        import numpy as np
        import math
        B, S, D = (2, 256, 256)
        H, HD = (16, 128)
        E, I = (4, 256)
        TOP_K = 2
        ROPE_THETA = 10000.0

        def _layernorm(x, w, b):
            mu = jnp.mean(x, axis=-1, keepdims=True)
            var = jnp.mean(jnp.square(x - mu), axis=-1, keepdims=True)
            return (x - mu) * jax.lax.rsqrt(var + 1e-05) * w + b

        def _rotate_half(x):
            x1, x2 = jnp.split(x, 2, axis=-1)
            return jnp.concatenate((-x2, x1), axis=-1)

        def _attention(h, wq, bq, wk, bk, wv, bv, wo, bo):
            b, s, _ = h.shape
            q = (h @ wq + bq).reshape(b, s, H, HD).transpose(0, 2, 1, 3)
            k = (h @ wk + bk).reshape(b, s, H, HD).transpose(0, 2, 1, 3)
            v = (h @ wv + bv).reshape(b, s, H, HD).transpose(0, 2, 1, 3)
            inv_freq = 1.0 / ROPE_THETA ** (jnp.arange(0, HD, 2, dtype=jnp.float32) / HD)
            freqs = jnp.arange(s, dtype=jnp.float32)[:, None] * inv_freq[None, :]
            emb = jnp.concatenate((freqs, freqs), axis=-1)
            cos = jnp.cos(emb)[None, None]
            sin = jnp.sin(emb)[None, None]
            q = q * cos + _rotate_half(q) * sin
            k = k * cos + _rotate_half(k) * sin
            scores = jnp.einsum('bhqd,bhkd->bhqk', q, k) / math.sqrt(HD)
            causal = jnp.tril(jnp.ones((s, s), bool))
            scores = jnp.where(causal[None, None], scores, jnp.finfo(jnp.float32).min)
            probs = jax.nn.softmax(scores.astype(jnp.float32), axis=-1).astype(q.dtype)
            out = jnp.einsum('bhqk,bhkd->bhqd', probs, v)
            out = out.transpose(0, 2, 1, 3).reshape(b, s, H * HD)
            return out @ wo + bo

        def _moe(h, w_gate, we1, be1, we2, be2):
            b, s, d = h.shape
            x = h.reshape(-1, d)
            t = x.shape[0]
            raw = jax.nn.softmax(x @ w_gate, axis=-1)
            top_vals, top_idx = jax.lax.top_k(raw, TOP_K)
            w = jax.nn.softmax(top_vals, axis=-1)
            comb = jnp.zeros((t, E), x.dtype).at[jnp.arange(t)[:, None], top_idx].add(w)
            hmid = jax.nn.gelu(jnp.einsum('td,edi->tei', x, we1) + be1[None], approximate=False)
            eout = jnp.einsum('tei,eid->ted', hmid, we2) + be2[None]
            out = jnp.einsum('te,ted->td', comb, eout)
            return out.reshape(b, s, d)
        a = _attention(_layernorm(hidden_states, ln1_w, ln1_b), wq, bq, wk, bk, wv, bv, wo, bo)
        h = hidden_states + a
        m = _moe(_layernorm(h, ln2_w, ln2_b), w_gate, we1, be1, we2, be2)
        return h + m
    x = L0_attn_x
    x = x + _L0_attn_ref(_layernorm(x, axis=-1), L0_attn_w_in, L0_attn_w_out, L0_attn_conv_w, L0_attn_conv_b, L0_attn_D)
    x = x + _L0_ffn_ref(_layernorm(x, axis=-1), L0_ffn_wq, L0_ffn_bq, L0_ffn_wk, L0_ffn_bk, L0_ffn_wv, L0_ffn_bv, L0_ffn_wo, L0_ffn_bo, L0_ffn_ln1_w, L0_ffn_ln1_b, L0_ffn_ln2_w, L0_ffn_ln2_b, L0_ffn_w_gate, L0_ffn_we1, L0_ffn_be1, L0_ffn_we2, L0_ffn_be2)
    return x

_drawn_inputs = setup_inputs


def setup_inputs(seed=0):
    import zlib

    import numpy as np

    out = dict(_drawn_inputs(seed))
    spreads = {'L0_attn_D': (1.0, 0.2),
     'L0_ffn_bq': (0.0, 0.8),
     'L0_ffn_bk': (0.0, 0.8),
     'L0_ffn_bv': (0.0, 0.1),
     'L0_ffn_bo': (0.0, 0.1),
     'L0_ffn_ln1_w': (1.0, 0.6),
     'L0_ffn_ln1_b': (0.0, 0.556),
     'L0_ffn_ln2_w': (1.0, 0.6),
     'L0_ffn_ln2_b': (0.0, 0.8),
     'L0_ffn_be1': (0.0, 0.8),
     'L0_ffn_be2': (0.0, 0.304)}
    factors = {'L0_attn_conv_b': 7.123,
     'L0_ffn_wq': 8.0,
     'L0_ffn_wk': 8.0,
     'L0_ffn_wv': 2.677,
     'L0_ffn_we1': 2.884,
     'L0_ffn_we2': 2.677}
    for name, (base, spread) in spreads.items():
        noise = np.random.default_rng([zlib.crc32(name.encode()), seed]).standard_normal(out[name].shape)
        drawn = base * np.exp(spread * noise) if base else spread * noise
        out[name] = jnp.asarray(drawn.astype(out[name].dtype))
    for name, factor in factors.items():
        out[name] = (out[name] * factor).astype(out[name].dtype)
    return out
```

```python
from contextlib import ExitStack

import concourse.bass as bass
from concourse import mybir

F32 = mybir.dt.float32
F32R = mybir.dt.float32r
BF16 = mybir.dt.bfloat16
ALU = mybir.AluOpType
ACT = mybir.ActivationFunctionType
AX = mybir.AxisListType

P = 128
BATCH, SEQ, D = 2, 1024, 256
TOK = BATCH * SEQ
DC = D // P
DI = 512
IB = DI // P
TAPS = 4
HEADS, HD = 16, 128
EXPERTS, EI = 4, 256
IC = EI // P
HALF = SEQ // 2
TG = HALF // P
GROUPS = TOK // HALF
QB = SEQ // P
SCALE = float(HD) ** -0.5
EPS = 1e-5
BIG = -1e30

WQK = 4 * P + 2
WOV = D + 1


def scores_width(i):
    return max(256, (i + 1) * P)


def score_banks(i):
    return 1 if scores_width(i) <= 512 else 2


def spread(buf, i):
    nb = score_banks(i)
    return buf[:, 0:nb, 0:scores_width(i) // nb]


def packed(buf, i):
    return buf[:, 0:scores_width(i)].rearrange("p (a n) -> p a n", a=score_banks(i))


CHUNKS = [(i, j, min(4, i + 1 - j)) for i in range(QB) for j in range(0, i + 1, 4)]
NCH = len(CHUNKS)
FIRST_CHUNK = [min(c for c in range(NCH) if CHUNKS[c][0] == i) for i in range(QB)]
LAST_CHUNK = [max(c for c in range(NCH) if CHUNKS[c][0] == i) for i in range(QB)]
CHUNKS_TO_HALF = [LAST_CHUNK[3] + 1, NCH]

PE_STEPS = [
    [("S", 0), ("V", 0)],
    [("S", 1), ("V", 1)],
    [("S", 2)],
    [("S", 3), ("Q", 0)],
    [("T", 0), ("S", 4), ("Q", 1)],
    [("T", 1)],
    [("T", 2), ("S", 5)],
    [("T", 3), ("Q", 2)],
    [("T", 4), ("S", 6)],
    [("O", 0), ("T", 5)],
    [("S", 7), ("W", 0), ("W", 1)],
    [("T", 6)],
    [("Q", 3)],
    [("T", 7)],
    [("O", 1)],
    [("W", 2), ("W", 3)],
]
FOLLOW = {
    "S": [("max", 0), ("exp", 0), ("recip", 1), ("norm", 1)],
    "V": [("v_hi", 0), ("v_lo", 0)],
    "Q": [("q_cos", 0), ("q_swap", 0), ("q_sin", 0), ("q_rope", 1), ("q_hi", 2), ("q_lo", 2)],
    "O": [("o_hi", 0), ("o_lo", 0)],
    "W": [("acc", 0)],
    "C": [("p_hi", 0), ("p_lo", 0)],
}
MISC = [(op, k) for step in PE_STEPS for op, k in step if op in "VQOW"]


def unit_order():
    order, later = [], [[] for _ in range(len(PE_STEPS) + 4)]
    for n, step in enumerate(PE_STEPS):
        for op, k in step:
            parts = [("C", c) for c in range(FIRST_CHUNK[k], LAST_CHUNK[k] + 1)] if op == "T" else [(op, k)]
            for part, a in parts:
                order.append((part, a))
                for what, lag in FOLLOW[part]:
                    if lag:
                        later[n + lag].append((what, a))
                    else:
                        order.append((what, a))
        order += later[n]
    return order + [x for rest in later[len(PE_STEPS):] for x in rest]


UNIT = unit_order()


def wait(eng, sem, value):
    if not isinstance(value, int) or value > 0:
        eng.wait_ge(sem, value)


def conv_layer(nc, x, w_in_t, w_out_t, conv_par, ln1, ident_d, x2_d, h0_d, h1h, h1l, h1f):
    with ExitStack() as ctx:
        def sb(name, shape, dt=F32):
            return ctx.enter_context(nc.sbuf_tensor(name, shape, dt))

        def pb(name, shape, dt=F32):
            return ctx.enter_context(nc.psum_tensor(name, shape, dt))

        def sem(name):
            return ctx.enter_context(nc.semaphore("a_" + name))

        ident = sb("a_ident", [P, P])
        par = sb("a_par", [P, IB, TAPS + 2])
        lnp = sb("a_lnp", [P, 2, DC])
        wi = sb("wi", [P, DC, 2 * DI])
        wih = sb("wih", [P, DC, 2 * DI], F32R)
        wil = sb("wil", [P, DC, 2 * DI], F32R)
        wo = sb("wo", [P, IB, D])
        woh = sb("woh", [P, IB, D], F32R)
        wol = sb("wol", [P, IB, D], F32R)
        xt = [sb(f"xt{s}", [P, TG, D]) for s in range(2)]
        xn = [sb(f"xn{s}", [P, TG, D]) for s in range(2)]
        xth = [sb(f"xth{s}", [P, DC, HALF], F32R) for s in range(2)]
        xtl = [sb(f"xtl{s}", [P, DC, HALF], F32R) for s in range(2)]
        xi = sb("xi", [P, IB, TAPS - 1 + SEQ])
        sg = sb("sg", [P, IB, HALF])
        cv = sb("cv", [P, 2, HALF])
        sx = sb("sx", [P, 2, HALF])
        hh = sb("hh", [P, IB, HALF], F32R)
        hl = sb("hl", [P, IB, HALF], F32R)
        x2 = [sb(f"x2{s}", [P, TG, D]) for s in range(2)]
        h0 = [sb(f"h0{s}", [P, TG, D]) for s in range(2)]
        stats = sb("a_stats", [P, TG, 6])
        mv = sb("a_mv", [P, TG, 2])
        rstd = sb("a_rstd", [P, TG])
        vare = sb("a_vare", [P, TG])
        mark = sb("a_mark", [P, 1])
        power = sb("a_power", [P, TG])

        ps_t = pb("a_ps_t", [P, DC, HALF])
        ps_in = pb("a_ps_in", [P, 4, HALF])
        ps_out = pb("a_ps_out", [P, TG // 2, 2, D])

        const_loaded = sem("const_loaded")
        w_hi = sem("w_hi")
        w_lo = sem("w_lo")
        halo_zero = sem("halo_zero")
        x_loaded = [sem(f"x_loaded{s}") for s in range(2)]
        x2_stored = [sem(f"x2_stored{s}") for s in range(2)]
        h0_stored = [sem(f"h0_stored{s}") for s in range(2)]
        stat_done = sem("stat_done")
        rstd_done = sem("rstd_done")
        vare_done = sem("vare_done")
        power_set = sem("power_set")
        norm_done = sem("norm_done")
        tr_done = sem("tr_done")
        x_hi = sem("x_hi")
        x_lo = sem("x_lo")
        in_done = sem("in_done")
        evac = sem("evac")
        tap_done = sem("tap_done")
        silu_done = sem("silu_done")
        gated = sem("gated")
        h_hi = sem("h_hi")
        h_lo = sem("h_lo")
        out_done = sem("out_done")
        x2_done = sem("x2_done")
        h1_f = sem("h1_f")
        h1_h = sem("h1_h")
        h1_l = sem("h1_l")

        x_g = x.rearrange("(g t p) d -> g p t d", p=P, t=TG)
        x2_g = x2_d.rearrange("(g t p) d -> g p t d", p=P, t=TG)
        h0_g = h0_d.rearrange("(g t p) d -> g p t d", p=P, t=TG)
        block = ctx.enter_context(nc.Block())

        @block.sync
        def _(sp):
            for s in range(2):
                sp.dma_start(xt[s][:], x_g[s]).then_inc(x_loaded[s], 16)
            sp.dma_start(ident[:], ident_d).then_inc(const_loaded, 16)
            sp.dma_start(wi[:], w_in_t.rearrange("(c p) n -> p c n", p=P)).then_inc(const_loaded, 16)
            sp.dma_start(par[:], conv_par).then_inc(const_loaded, 16)
            sp.dma_start(lnp[:], ln1).then_inc(const_loaded, 16)
            sp.dma_start(wo[:], w_out_t.rearrange("(c p) n -> p c n", p=P)).then_inc(const_loaded, 16)
            with sp.Fori(0, BATCH) as b:
                for s in range(2):
                    sp.wait_ge(norm_done, b * 6 + 3 * s + 2)
                    sp.dma_start(x2_g[b * 2 + s], x2[s][:]).then_inc(x2_stored[s], 16)
                    sp.dma_start(h0_g[b * 2 + s], h0[s][:]).then_inc(h0_stored[s], 16)
                    if s == 1:
                        for r in range(2):
                            sp.dma_start(xt[r][:], x_g[2 + r]).then_inc(x_loaded[r], 16)
            for s in range(2):
                sp.wait_ge(x2_stored[s], 16 * BATCH)
                sp.wait_ge(h0_stored[s], 16 * BATCH)
                sp.wait_ge(x_loaded[s], 16 * (BATCH + 1))

        @block.gpsimd
        def _(pool):
            nc.gpsimd.memset(xi[:, :, 0:TAPS - 1], 0.0).then_inc(halo_zero, 1)
            nc.gpsimd.memset(power[:], -0.5).then_inc(power_set, 1)
            pool.wait_ge(power_set, 1)
            with pool.Fori(0, 6 * BATCH) as n:
                pool.wait_ge(vare_done, n + 1)
                nc.gpsimd.tensor_tensor(rstd[:], vare[:], power[:], ALU.pow).then_inc(rstd_done, 1)

        @block.scalar
        def _(act):
            act.wait_ge(const_loaded, 16 * 5)
            nc.scalar.activation(wih[:], wi[:], ACT.Copy).then_inc(w_hi, 1)
            nc.scalar.activation(woh[:], wo[:], ACT.Copy).then_inc(w_hi, 1)
            with act.Fori(0, BATCH) as b:
                for s in range(2):
                    act.wait_ge(tr_done, b * 4 + 2 * s + 1)
                    nc.scalar.activation(xth[s][:], ps_t[:], ACT.Copy).then_inc(x_hi, 1)
                    for m in range(IB):
                        act.wait_ge(in_done, b * 16 + 8 * s + 2 * m + 1)
                        lo = TAPS - 1 + s * HALF
                        nc.scalar.activation(xi[:, m, lo:lo + HALF], ps_in[:, 2 * m % 4, :], ACT.Copy).then_inc(evac, 1)
                        act.wait_ge(in_done, b * 16 + 8 * s + 2 * m + 2)
                        nc.scalar.activation(sg[:, m, :], ps_in[:, 2 * m % 4 + 1, :], ACT.Silu).then_inc(evac, 1)
                        act.wait_ge(tap_done, b * 32 + 16 * s + 4 * m + 4)
                        nc.scalar.activation(sx[:, m % 2, :], cv[:, m % 2, :], ACT.Silu).then_inc(silu_done, 1)
                        act.wait_ge(gated, b * 8 + 4 * s + m + 1)
                        nc.scalar.activation(hh[:, m, :], cv[:, m % 2, :], ACT.Copy).then_inc(h_hi, 1)
                    act.wait_ge(tr_done, b * 4 + 2 * s + 2)
                    for c in range(DC):
                        ins = nc.scalar.activation(h1f[:, c, bass.ds(b * SEQ + s * HALF, HALF)], ps_t[:, c, :],
                                                   ACT.Identity, bias=lnp[:, 1, c:c + 1], scale=lnp[:, 0, c:c + 1])
                    ins.then_inc(h1_f, 1)
                    act.wait_ge(h1_f, b * 2 + s + 1)
                    cols = bass.ds(b * SEQ + s * HALF, HALF)
                    nc.scalar.activation(h1h[:, :, cols], h1f[:, :, cols], ACT.Copy).then_inc(h1_h, 1)

        @block.vector
        def _(dve):
            def layernorm(b, s, which, src, dst):
                at = b * 24 + 12 * s + 4 * which
                for t in range(TG):
                    nc.vector.bn_stats(stats[:, t, :], src[:, t, :]).then_inc(stat_done, 1)
                dve.wait_ge(stat_done, at + TG)
                nc.vector.memset(mark[:], 0.0)
                for t in range(TG):
                    ins = nc.vector.bn_aggr(mv[:, t, :], stats[:, t, :])
                ins.then_inc(rstd_done, 1)
                n = b * 12 + 6 * s + 2 * which
                dve.wait_ge(rstd_done, n + 1)
                nc.vector.tensor_scalar(vare[:], mv[:, :, 1], EPS, None, ALU.add).then_inc(vare_done, 1)
                dve.wait_ge(rstd_done, n + 2)
                for t in range(TG):
                    ins = nc.vector.tensor_scalar(dst[:, t, :], src[:, t, :], mv[:, t, 0:1], rstd[:, t:t + 1],
                                                  ALU.subtract, ALU.mult)
                ins.then_inc(norm_done, 1)

            dve.wait_ge(w_hi, 2)
            nc.vector.tensor_tensor(wil[:], wi[:], wih[:], ALU.subtract).then_inc(w_lo, 1)
            nc.vector.tensor_tensor(wol[:], wo[:], woh[:], ALU.subtract).then_inc(w_lo, 1)
            dve.wait_ge(halo_zero, 1)
            with dve.Fori(0, BATCH) as b:
                for s in range(2):
                    dve.wait_ge(x_loaded[s], b * 16 + 16)
                    layernorm(b, s, 0, xt[s], xn[s])
                    dve.wait_ge(x_hi, b * 2 + s + 1)
                    nc.vector.tensor_tensor(xtl[s][:], ps_t[:], xth[s][:], ALU.subtract).then_inc(x_lo, 1)
                    for m in range(IB):
                        at = b * 32 + 16 * s + 4 * m
                        c = cv[:, m % 2, :]
                        dve.wait_ge(evac, b * 16 + 8 * s + 2 * m + 1)

                        def rows(j):
                            return xi[:, m, s * HALF + j:s * HALF + j + HALF]

                        nc.vector.tensor_scalar(c, rows(TAPS - 1), par[:, m, TAPS - 1:TAPS], par[:, m, TAPS:TAPS + 1],
                                                ALU.mult, ALU.add).then_inc(tap_done, 1)
                        for j in range(TAPS - 1):
                            dve.wait_ge(tap_done, at + j + 1)
                            nc.vector.scalar_tensor_tensor(out=c, in0=rows(j), scalar=par[:, m, j:j + 1], in1=c,
                                                           op0=ALU.mult, op1=ALU.add).then_inc(tap_done, 1)
                        n = b * 8 + 4 * s + m
                        dve.wait_ge(silu_done, n + 1)
                        dve.wait_ge(evac, b * 16 + 8 * s + 2 * m + 2)
                        nc.vector.scalar_tensor_tensor(out=c, in0=sx[:, m % 2, :], scalar=par[:, m, TAPS + 1:TAPS + 2],
                                                       in1=sg[:, m, :], op0=ALU.mult, op1=ALU.mult).then_inc(gated, 1)
                        dve.wait_ge(h_hi, n + 1)
                        nc.vector.tensor_tensor(hl[:, m, :], c, hh[:, m, :], ALU.subtract).then_inc(h_lo, 1)
                    for k in range(TG // 2):
                        dve.wait_ge(out_done, b * 4 + 2 * s + k + 1)
                        ins = nc.vector.tensor_tensor(x2[s][:, 2 * k:2 * k + 2, :], ps_out[:, k], xt[s][:, 2 * k:2 * k + 2, :],
                                                      ALU.add)
                    ins.then_inc(x2_done, 1)
                    dve.wait_ge(x2_done, b * 2 + s + 1)
                    layernorm(b, s, 1, x2[s], h0[s])
                    dve.wait_ge(norm_done, b * 6 + 3 * s + 2)
                    layernorm(b, s, 2, h0[s], xn[s])
                    dve.wait_ge(h1_h, b * 2 + s + 1)
                    cols = bass.ds(b * SEQ + s * HALF, HALF)
                    nc.vector.tensor_tensor(h1l[:, :, cols], h1f[:, :, cols], h1h[:, :, cols],
                                            ALU.subtract).then_inc(h1_l, 1)

        @block.tensor
        def _(pe):
            pe.wait_ge(const_loaded, 16 * 5)
            pe.wait_ge(w_lo, 2)
            with pe.Fori(0, BATCH) as b:
                for s in range(2):
                    def transposes():
                        for t in range(TG):
                            for c in range(DC):
                                ins = nc.tensor.transpose(ps_t[:, c, t * P:(t + 1) * P], xn[s][:, t, c * P:(c + 1) * P],
                                                          ident[:])
                        ins.then_inc(tr_done, 1)

                    pe.wait_ge(norm_done, b * 6 + 3 * s + 1)
                    transposes()
                    pe.wait_ge(x_lo, b * 2 + s + 1)
                    for k in range(2 * IB):
                        n = (k // 2) * P + (k % 2) * DI
                        if k >= 4:
                            pe.wait_ge(evac, b * 16 + 8 * s + k - 3)
                        for q, (w, r) in enumerate(((wih, xth), (wih, xtl), (wil, xth))):
                            for c in range(DC):
                                ins = nc.tensor.matmul(ps_in[:, k % 4, :], w[:, c, n:n + P], r[s][:, c, :],
                                                       start=(q + c == 0), stop=(q == 2 and c == DC - 1))
                        ins.then_inc(in_done, 1)
                    pe.wait_ge(h_lo, b * 8 + 4 * s + IB)
                    for t in range(TG):
                        for q, (l, w) in enumerate(((hh, woh), (hh, wol), (hl, woh))):
                            for m in range(IB):
                                ins = nc.tensor.matmul(ps_out[:, t // 2, t % 2, :], l[:, m, t * P:(t + 1) * P], w[:, m, :],
                                                       start=(q + m == 0), stop=(q == 2 and m == IB - 1))
                        if t % 2:
                            ins.then_inc(out_done, 1)
                    pe.wait_ge(norm_done, b * 6 + 3 * s + 3)
                    transposes()


def attention(nc, w_qk, w_v, w_ov, rope, ident_d, identb_d, mask_d, h1h, h1l, h1f, acc):
    with ExitStack() as ctx:
        def sb(name, shape, dt=F32):
            return ctx.enter_context(nc.sbuf_tensor(name, shape, dt))

        def pb(name, shape, dt=F32):
            return ctx.enter_context(nc.psum_tensor(name, shape, dt))

        def sem(name):
            return ctx.enter_context(nc.semaphore("b_" + name))

        ident = sb("b_ident", [P, P])
        identb = sb("b_identb", [P, P], BF16)
        mask = sb("b_mask", [P, 2 * P], BF16)
        cos_sin = sb("b_cos_sin", [P, 2, SEQ])
        wqk = sb("b_wqk", [P, WQK])
        wqkh = sb("b_wqkh", [P, 4, P], F32R)
        wqkl = sb("b_wqkl", [P, 4, P], F32R)
        bqk = sb("b_bqk", [P, 2])
        wv = sb("b_wv", [P, DC, P])
        wov = sb("b_wov", [P, WOV])
        woh = sb("b_woh", [P, D], F32R)
        wol = sb("b_wol", [P, D], F32R)
        bv = sb("b_bv", [P, 1])
        qkh = [sb(f"b_qkh{b}", [P, 2, SEQ], F32R) for b in range(BATCH)]
        qkl = [sb(f"b_qkl{b}", [P, 2, SEQ], F32R) for b in range(BATCH)]
        rot = sb("b_rot", [P, 2, HALF])
        swp = sb("b_swp", [P, 2, HALF])
        vh = sb("b_vh", [P, QB, HD], F32R)
        vl = sb("b_vl", [P, QB, HD], F32R)
        prob = [sb(f"b_prob{i}", [P, SEQ]) for i in range(4)]
        pth = [sb(f"b_pth{f}", [P, 4 * f + 4, HALF], F32R) for f in range(2)]
        ptl = [sb(f"b_ptl{f}", [P, 4 * f + 4, HALF], F32R) for f in range(2)]
        oh = [sb(f"b_oh{f}", [P, HALF], F32R) for f in range(2)]
        ol = [sb(f"b_ol{f}", [P, HALF], F32R) for f in range(2)]
        nmax = sb("b_nmax", [P, BATCH, QB])
        rsum = sb("b_rsum", [P, BATCH, QB])
        rinv = sb("b_rinv", [P, BATCH, QB])

        ps_s = [pb(f"b_ps_s{i}", [P, 2, HALF]) for i in range(2)]
        ps_t = pb("b_ps_t", [P, 2, HALF])
        ps_m = pb("b_ps_m", [P, 2, HALF])

        const_loaded = sem("const_loaded")
        qk_loaded = sem("qk_loaded")
        v_loaded = sem("v_loaded")
        ov_loaded = sem("ov_loaded")
        zeroed = sem("zeroed")
        wqk_hi, wqk_lo = sem("wqk_hi"), sem("wqk_lo")
        wo_hi, wo_lo = sem("wo_hi"), sem("wo_lo")
        s_done, max_done, exp_done = sem("s_done"), sem("max_done"), sem("exp_done")
        recip_done, norm_done = sem("recip_done"), sem("norm_done")
        t_done, p_hi, p_lo = sem("t_done"), sem("p_hi"), sem("p_lo")
        q_done, q_cos, q_swap, q_sin = sem("q_done"), sem("q_cos"), sem("q_swap"), sem("q_sin")
        q_rope, q_hi, q_lo = sem("q_rope"), sem("q_hi"), sem("q_lo")
        v_done, v_hi, v_lo = sem("v_done"), sem("v_hi"), sem("v_lo")
        o_done, o_hi, o_lo = sem("o_done"), sem("o_hi"), sem("o_lo")
        w_done, acc_done = sem("w_done"), sem("acc_done")

        EXP0, T0, P0, O0, W0, ACC0 = 2, NCH, 2, 2, 4, 4
        block = ctx.enter_context(nc.Block())

        @block.sync
        def _(sp):
            sp.sem_inc(exp_done, EXP0)
            sp.sem_inc(t_done, T0)
            sp.sem_inc(p_lo, P0)
            sp.sem_inc(o_done, O0)
            sp.sem_inc(w_done, W0)
            sp.sem_inc(acc_done, ACC0)
            sp.dma_start(wqk[:], w_qk[0]).then_inc(qk_loaded, 16)
            sp.dma_start(cos_sin[:], rope).then_inc(const_loaded, 16)
            sp.dma_start(wv[:], w_v[0].rearrange("p (c n) -> p c n", c=DC)).then_inc(v_loaded, 16)
            sp.dma_start(wov[:], w_ov[0]).then_inc(ov_loaded, 16)
            sp.dma_start(ident[:], ident_d).then_inc(const_loaded, 16)
            sp.dma_start(identb[:], identb_d).then_inc(const_loaded, 16)
            sp.dma_start(mask[:], mask_d).then_inc(const_loaded, 16)
            with sp.Fori(0, HEADS) as h:
                sp.wait_ge(wqk_lo, h + 1)
                sp.dma_start(wqk[:], w_qk[h + 1]).then_inc(qk_loaded, 16)
                sp.wait_ge(wo_lo, h + 1)
                sp.dma_start(wov[:], w_ov[h + 1]).then_inc(ov_loaded, 16)
                sp.wait_ge(v_done, h * 4 + 4)
                sp.dma_start(wv[:], w_v[h + 1].rearrange("p (c n) -> p c n", c=DC)).then_inc(v_loaded, 16)
            sp.wait_ge(qk_loaded, 16 * (HEADS + 1))
            sp.wait_ge(ov_loaded, 16 * (HEADS + 1))
            sp.wait_ge(v_loaded, 16 * (HEADS + 1))

        def piece(k):
            return k % 2, k // 2

        @block.gpsimd
        def _(pool):
            nc.gpsimd.memset(acc[:], 0.0).then_inc(zeroed, 1)
            for f in range(2):
                nc.gpsimd.memset(pth[f][:, 4 * f + 3, 2 * P:3 * P].bitcast(F32), 0.0).then_inc(zeroed, 1)
                nc.gpsimd.memset(ptl[f][:, 4 * f + 3, 2 * P:3 * P].bitcast(F32), 0.0).then_inc(zeroed, 1)
            pool.wait_ge(const_loaded, 16 * 4)

            def sin(k, n):
                half = piece(k)[1]
                pool.wait_ge(q_swap, n)
                nc.gpsimd.tensor_tensor(swp[:, k % 2, :], swp[:, k % 2, :], cos_sin[:, 1, half * HALF:(half + 1) * HALF],
                                        ALU.mult).then_inc(q_sin, 1)

            def rotate(k, n):
                pool.wait_ge(q_sin, n)
                nc.gpsimd.tensor_tensor(rot[:, k % 2, :], rot[:, k % 2, :], swp[:, k % 2, :], ALU.add).then_inc(q_rope, 1)

            for k in range(4):
                sin(k, k + 1)
                rotate(k, k + 1)
            with pool.Fori(0, HEADS) as h:
                for b in range(BATCH):
                    for op, k in UNIT:
                        if op == "norm":
                            pool.wait_ge(recip_done, h * 16 + 8 * b + k + 1)
                            row = prob[k % 4][:, 0:(k + 1) * P]
                            nc.gpsimd.tensor_tensor(row, row, rinv[:, b, k:k + 1].to_broadcast([P, (k + 1) * P]),
                                                    ALU.mult).then_inc(norm_done, 1)
                        elif op == "q_sin":
                            sin(k, h * 8 + 4 * b + k + 5)
                        elif op == "q_rope":
                            rotate(k, h * 8 + 4 * b + k + 5)

        @block.scalar
        def _(act):
            def split_qk(n):
                act.wait_ge(qk_loaded, 16 * n)
                nc.scalar.activation(wqkh[:, 0:2, :], wqk[:, 0:2 * P].rearrange("p (c n) -> p c n", c=2), ACT.Copy,
                                     scale=SCALE)
                nc.scalar.activation(wqkh[:, 2:4, :], wqk[:, 2 * P:4 * P].rearrange("p (c n) -> p c n", c=2),
                                     ACT.Copy).then_inc(wqk_hi, 1)

            def swap(k, n, free):
                which = piece(k)[0]
                act.wait_ge(q_cos, n)
                wait(act, q_rope, free)
                lo, hi = slice(0, HD // 2), slice(HD // 2, HD)
                for to, of in ((lo, hi), (hi, lo)):
                    ins = nc.scalar.activation(swp[to, k % 2, :], ps_m[of, q_bank(k), :], ACT.Identity,
                                               bias=bqk[of, which:which + 1])
                ins.then_inc(q_swap, 1)

            def high(k, n, dst):
                which, half = piece(k)
                act.wait_ge(q_rope, n)
                nc.scalar.activation(dst[:, which, half * HALF:(half + 1) * HALF], rot[:, k % 2, :],
                                     ACT.Copy).then_inc(q_hi, 1)

            q_bank = lambda k: k % 2
            split_qk(1)
            for k in range(4):
                swap(k, k + 1, k - 1)
                high(k, k + 1, qkh[0])
            q_bank = lambda k: MISC.index(("Q", k)) % 2
            with act.Fori(0, HEADS) as h:
                for b in range(BATCH):
                    if b == 0:
                        act.wait_ge(ov_loaded, h * 16 + 16)
                        act.wait_ge(w_done, h * 8 + 4)
                        nc.scalar.activation(woh[:], wov[:, 0:D], ACT.Copy).then_inc(wo_hi, 1)
                    else:
                        act.wait_ge(q_done, h * 8 + 8)
                        split_qk(h + 2)
                    for op, k in UNIT:
                        if op == "exp":
                            act.wait_ge(max_done, h * 16 + 8 * b + k + 1)
                            n = LAST_CHUNK[k - 4] + 1 + T0 if k >= 4 else LAST_CHUNK[k + 4] + 1
                            act.wait_ge(t_done, h * (2 * NCH) + NCH * b + n)
                            nc.scalar.activation(packed(prob[k % 4], k), spread(ps_s[k % 2], k), ACT.Exp,
                                                 bias=nmax[:, b, k:k + 1], accum_out=rsum[:, b, k:k + 1]).then_inc(exp_done, 1)
                        elif op == "p_hi":
                            i, j, n = CHUNKS[k]
                            f = i // 4
                            act.wait_ge(t_done, h * (2 * NCH) + NCH * b + k + 1 + T0)
                            act.wait_ge(o_done, h * 4 + 2 * b + f + 1)
                            nc.scalar.activation(pth[f][:, j:j + n, (i % 4) * P:(i % 4 + 1) * P],
                                                 ps_t[:, k % 2, 0:n * P].rearrange("p (n q) -> p n q", n=n),
                                                 ACT.Copy).then_inc(p_hi, 1)
                        elif op == "q_swap":
                            at = h * 8 + 4 * b + k + 5
                            swap(k, at, at - 2)
                        elif op == "q_hi":
                            high(k, h * 8 + 4 * b + k + 5, qkh[1 - b])
                        elif op == "v_hi":
                            act.wait_ge(v_done, h * 4 + 2 * b + k + 1)
                            act.wait_ge(o_done, h * 4 + 2 * b + 2)
                            nc.scalar.activation(vh[:, 4 * k:4 * k + 4, :],
                                                 ps_m[:, MISC.index(("V", k)) % 2, :].rearrange("p (n d) -> p n d", n=4),
                                                 ACT.Copy).then_inc(v_hi, 1)
                        elif op == "o_hi":
                            act.wait_ge(o_done, h * 4 + 2 * b + k + 1 + O0)
                            act.wait_ge(w_done, h * 8 + 4 * b + 2 * k + 2)
                            act.wait_ge(wo_lo, h + 1)
                            nc.scalar.activation(oh[k][:], ps_m[:, MISC.index(("O", k)) % 2, :], ACT.Identity,
                                                 bias=bv[:, 0:1]).then_inc(o_hi, 1)

        @block.vector
        def _(dve):
            def split_qk(n):
                dve.wait_ge(wqk_hi, n)
                nc.vector.scalar_tensor_tensor(out=wqkl[:, 0:2, :], in0=wqk[:, 0:2 * P].rearrange("p (c n) -> p c n", c=2),
                                               scalar=SCALE, in1=wqkh[:, 0:2, :], op0=ALU.mult, op1=ALU.subtract)
                nc.vector.tensor_tensor(wqkl[:, 2:4, :], wqk[:, 2 * P:4 * P].rearrange("p (c n) -> p c n", c=2),
                                        wqkh[:, 2:4, :], ALU.subtract)
                nc.vector.tensor_scalar(bqk[:, 0:1], wqk[:, 4 * P:4 * P + 1], SCALE, None, ALU.mult)
                nc.vector.tensor_copy(bqk[:, 1:2], wqk[:, 4 * P + 1:4 * P + 2]).then_inc(wqk_lo, 1)

            def times_cos(k, n, bank):
                which, half = piece(k)
                dve.wait_ge(q_done, n)
                nc.vector.scalar_tensor_tensor(out=rot[:, k % 2, :], in0=ps_m[:, bank, :], scalar=bqk[:, which:which + 1],
                                               in1=cos_sin[:, 0, half * HALF:(half + 1) * HALF],
                                               op0=ALU.add, op1=ALU.mult).then_inc(q_cos, 1)

            def low(k, n, hi, lo):
                which, half = piece(k)
                cols = slice(half * HALF, (half + 1) * HALF)
                dve.wait_ge(q_hi, n)
                nc.vector.tensor_tensor(lo[:, which, cols], rot[:, k % 2, :], hi[:, which, cols],
                                        ALU.subtract).then_inc(q_lo, 1)

            split_qk(1)
            dve.wait_ge(wqk_lo, 1)
            dve.wait_ge(const_loaded, 16 * 4)
            dve.wait_ge(zeroed, 1)
            for k in range(4):
                times_cos(k, k + 1, k % 2)
                low(k, k + 1, qkh[0], qkl[0])
            with dve.Fori(0, HEADS) as h:
                for b in range(BATCH):
                    if b == 0:
                        dve.wait_ge(wo_hi, h + 1)
                        nc.vector.tensor_tensor(wol[:], wov[:, 0:D], woh[:], ALU.subtract)
                        nc.vector.tensor_copy(bv[:], wov[:, D:D + 1]).then_inc(wo_lo, 1)
                    else:
                        dve.wait_ge(q_swap, h * 8 + 8)
                        split_qk(h + 2)
                        dve.wait_ge(wqk_lo, h + 2)
                    for op, k in UNIT:
                        if op == "max":
                            dve.wait_ge(s_done, h * 16 + 8 * b + k + 1)
                            nc.vector.tensor_reduce(nmax[:, b, k:k + 1], spread(ps_s[k % 2], k), AX.XY, ALU.max,
                                                    negate=True).then_inc(max_done, 1)
                        elif op == "recip":
                            dve.wait_ge(exp_done, h * 16 + 8 * b + k + 1 + EXP0)
                            nc.vector.reciprocal(rinv[:, b, k:k + 1], rsum[:, b, k:k + 1]).then_inc(recip_done, 1)
                        elif op == "p_lo":
                            i, j, n = CHUNKS[k]
                            f, q = i // 4, slice((i % 4) * P, (i % 4 + 1) * P)
                            dve.wait_ge(p_hi, h * (2 * NCH) + NCH * b + k + 1)
                            nc.vector.tensor_tensor(ptl[f][:, j:j + n, q],
                                                    ps_t[:, k % 2, 0:n * P].rearrange("p (n q) -> p n q", n=n),
                                                    pth[f][:, j:j + n, q], ALU.subtract).then_inc(p_lo, 1)
                        elif op == "q_cos":
                            times_cos(k, h * 8 + 4 * b + k + 5, MISC.index(("Q", k)) % 2)
                        elif op == "q_lo":
                            low(k, h * 8 + 4 * b + k + 5, qkh[1 - b], qkl[1 - b])
                        elif op == "v_lo":
                            dve.wait_ge(v_hi, h * 4 + 2 * b + k + 1)
                            nc.vector.tensor_tensor(vl[:, 4 * k:4 * k + 4, :],
                                                    ps_m[:, MISC.index(("V", k)) % 2, :].rearrange("p (n d) -> p n d", n=4),
                                                    vh[:, 4 * k:4 * k + 4, :], ALU.subtract).then_inc(v_lo, 1)
                        elif op == "o_lo":
                            dve.wait_ge(o_hi, h * 4 + 2 * b + k + 1)
                            nc.vector.scalar_tensor_tensor(out=ol[k][:], in0=ps_m[:, MISC.index(("O", k)) % 2, :],
                                                           scalar=bv[:, 0:1], in1=oh[k][:], op0=ALU.add,
                                                           op1=ALU.subtract).then_inc(o_lo, 1)
                        elif op == "acc":
                            dve.wait_ge(w_done, h * 8 + 4 * b + k + 1 + W0)
                            t = b * SEQ + (k // 2) * HALF
                            to = acc[:, k % 2, t:t + HALF]
                            nc.vector.tensor_tensor(to, ps_m[:, MISC.index(("W", k)) % 2, :], to, ALU.add).then_inc(acc_done, 1)

        @block.tensor
        def _(pe):
            def project(k, batch, bank):
                which, half = piece(k)
                t = batch * SEQ + half * HALF
                for q, (w, r) in enumerate(((wqkh, h1h), (wqkh, h1l), (wqkl, h1h))):
                    for c in range(DC):
                        ins = nc.tensor.matmul(ps_m[:, bank, :], w[:, 2 * which + c, :], r[:, c, t:t + HALF],
                                               start=(q + c == 0), stop=(q == 2 and c == DC - 1))
                ins.then_inc(q_done, 1)

            def bank_free(m, h, b):
                op, k = MISC[m - 2]
                if m < 2:
                    pe.wait_ge(acc_done, h * 8 + 4 * b + k + 1)
                    pe.wait_ge(q_swap, h * 8 + 4 * b + m + 3)
                elif op == "V":
                    pe.wait_ge(v_lo, h * 4 + 2 * b + k + 1)
                elif op == "Q":
                    pe.wait_ge(q_swap, h * 8 + 4 * b + k + 5)
                elif op == "O":
                    pe.wait_ge(o_lo, h * 4 + 2 * b + k + 1)
                else:
                    pe.wait_ge(acc_done, h * 8 + 4 * b + k + 1 + ACC0)

            pe.wait_ge(wqk_lo, 1)
            for k in range(4):
                if k >= 2:
                    pe.wait_ge(q_swap, k - 1)
                project(k, 0, k % 2)
            pe.wait_ge(const_loaded, 16 * 4)
            pe.wait_ge(zeroed, 5)
            with pe.Fori(0, HEADS) as h:
                for b in range(BATCH):
                    for op, k in UNIT:
                        if (op, k) in MISC:
                            m = MISC.index((op, k))
                            bank = m % 2
                        if op == "S":
                            pe.wait_ge(q_lo, h * 8 + 4 * b + (2 if k < 4 else 4))
                            pe.wait_ge(exp_done, h * 16 + 8 * b + k + 1)
                            nb = score_banks(k)
                            w = scores_width(k) // nb
                            q = slice(k * P, (k + 1) * P)
                            for n, (l, r) in enumerate(((qkh, qkh), (qkh, qkl), (qkl, qkh))):
                                for g in range(nb):
                                    nc.tensor.matmul(ps_s[k % 2][:, g, 0:w], l[b][:, 0, q], r[b][:, 1, g * w:(g + 1) * w],
                                                     start=(n == 0), stop=(n == 2 and g < nb - 1))
                            mw = 2 * P if k == 0 else P
                            nc.tensor.matmul(ps_s[k % 2][:, nb - 1, w - mw:w], identb[:], mask[:, 0:mw],
                                             start=False, stop=True).then_inc(s_done, 1)
                        elif op == "C":
                            i, j, n = CHUNKS[k]
                            pe.wait_ge(norm_done, h * 16 + 8 * b + i + 1)
                            pe.wait_ge(p_lo, h * (2 * NCH) + NCH * b + k + 1)
                            for a in range(n):
                                ins = nc.tensor.transpose(ps_t[:, k % 2, a * P:(a + 1) * P],
                                                          prob[i % 4][:, (j + a) * P:(j + a + 1) * P], ident[:])
                            ins.then_inc(t_done, 1)
                        elif op == "V":
                            pe.wait_ge(v_loaded, h * 16 + 16)
                            bank_free(m, h, b)
                            for a in range(4):
                                t = b * SEQ + (4 * k + a) * P
                                for c in range(DC):
                                    ins = nc.tensor.matmul(ps_m[:, bank, a * HD:(a + 1) * HD], h1f[:, c, t:t + P], wv[:, c, :],
                                                           start=(c == 0), stop=(c == DC - 1))
                            ins.then_inc(v_done, 1)
                        elif op == "Q":
                            bank_free(m, h, b)
                            pe.wait_ge(wqk_lo, h + 1 + b)
                            project(k, 1 - b, bank)
                        elif op == "O":
                            bank_free(m, h, b)
                            pe.wait_ge(p_lo, h * (2 * NCH) + NCH * b + CHUNKS_TO_HALF[k] + P0)
                            pe.wait_ge(v_lo, h * 4 + 2 * b + k + 1)
                            last = 4 * k + 3
                            for j in range(last + 1):
                                q0 = min(max(0, j - 4 * k) * P, HALF - 2 * P)
                                for n, (l, r) in enumerate(((vh, pth), (vh, ptl), (vl, pth))):
                                    ins = nc.tensor.matmul(ps_m[:, bank, q0:HALF], l[:, j, :], r[k][:, j, q0:HALF],
                                                           start=(j == 0 and n == 0), stop=(j == last and n == 2))
                            ins.then_inc(o_done, 1)
                        elif op == "W":
                            bank_free(m, h, b)
                            f, d = k // 2, slice((k % 2) * P, (k % 2 + 1) * P)
                            pe.wait_ge(o_lo, h * 4 + 2 * b + f + 1)
                            pe.wait_ge(wo_lo, h + 1)
                            for n, (l, r) in enumerate(((woh, oh), (woh, ol), (wol, oh))):
                                ins = nc.tensor.matmul(ps_m[:, bank, :], l[:, d], r[f][:], start=(n == 0), stop=(n == 2))
                            ins.then_inc(w_done, 1)


def experts(nc, ln2, w_gate, w1, b1, w2, b2, bo, ident_d, x2_d, h0_d, acc, out):
    with ExitStack() as ctx:
        def sb(name, shape, dt=F32):
            return ctx.enter_context(nc.sbuf_tensor(name, shape, dt))

        def pb(name, shape, dt=F32):
            return ctx.enter_context(nc.psum_tensor(name, shape, dt))

        def sem(name):
            return ctx.enter_context(nc.semaphore("c_" + name))

        E = EXPERTS
        TILES = TOK // P
        ident = sb("c_ident", [P, P])
        lnp = sb("c_lnp", [P, 2, DC])
        wg = sb("c_wg", [P, DC, E])
        bo_sb = sb("c_bo", [P, DC])
        b1_sb = sb("c_b1", [P, E, IC])
        b2_sb = sb("c_b2", [E, D])
        w1f = sb("c_w1f", [P, E, DC, EI])
        w1h = sb("c_w1h", [P, E, DC, EI], F32R)
        w1l = sb("c_w1l", [P, E, DC, EI], F32R)
        w2f = sb("c_w2f", [P, E, IC, D])
        w2h = sb("c_w2h", [P, E, IC, D], F32R)
        w2l = sb("c_w2l", [P, E, IC, D], F32R)
        att = sb("c_att", [P, DC, HALF])
        h0 = sb("c_h0", [P, TG, D])
        x2 = sb("c_x2", [P, TG, D])
        hg = sb("c_hg", [P, TG, D])
        zg = sb("c_zg", [P, TG, D])
        h2f = sb("c_h2f", [P, DC, HALF])
        h2h = sb("c_h2h", [P, DC, TOK], F32R)
        h2l = sb("c_h2l", [P, DC, TOK], F32R)
        total = sb("c_total", [P, TILES, D])
        stats = sb("c_stats", [P, TG, 6])
        mv = sb("c_mv", [P, TG, 2])
        rstd = sb("c_rstd", [P, TG])
        vare = sb("c_vare", [P, TG])
        mark = sb("c_mark", [P, 1])
        power = sb("c_power", [P, TG])
        logit = sb("c_logit", [P, TILES, E])
        raw = sb("c_raw", [P, TILES, E])
        rest = sb("c_rest", [P, TILES, E])
        eq = sb("c_eq", [P, TILES, E])
        seen = sb("c_seen", [P, TILES, 1])
        pick = [sb(f"c_pick{r}", [P, TILES, E]) for r in range(2)]
        top = [sb(f"c_top{r}", [P, TILES]) for r in range(2)]
        tmp = sb("c_tmp", [P, TILES])
        share = [sb(f"c_share{r}", [P, TILES]) for r in range(2)]
        comb = sb("c_comb", [P, TILES * E])
        comb_t = sb("c_comb_t", [E, TOK])
        comb_g = sb("c_comb_g", [E, HALF])
        hmf = [sb(f"c_hmf{i}", [P, HALF]) for i in range(2)]
        hmh = [sb(f"c_hmh{i}", [P, IC, HALF], F32R) for i in range(2)]
        hml = [sb(f"c_hml{i}", [P, IC, HALF], F32R) for i in range(2)]

        ps_a = pb("c_ps_a", [P, DC, HALF])
        ps_h = pb("c_ps_h", [P, 2, HALF])
        ps_o = [pb(f"c_ps_o{i}", [P, TG, D]) for i in range(2)]

        const_loaded, w_loaded = sem("const_loaded"), sem("w_loaded")
        rows_loaded = sem("rows_loaded")
        att_done, att_t = sem("att_done"), sem("att_t")
        h_done, stat_done, rstd_done, z_done = sem("h_done"), sem("stat_done"), sem("rstd_done"), sem("z_done")
        base_done, z_t = sem("base_done"), sem("z_t")
        vare_done, power_set = sem("vare_done"), sem("power_set")
        h2_f, h2_h, h2_l = sem("h2_f"), sem("h2_h"), sem("h2_l")
        gate_done, logit_done = sem("gate_done"), sem("logit_done")
        route, route_exp, comb_tr = sem("route"), sem("route_exp"), sem("comb_tr")
        comb_out, comb_cut = sem("comb_out"), sem("comb_cut")
        w_hi, w_lo = sem("w_hi"), sem("w_lo")
        hm_done, gelu_done, hm_hi, hm_lo = sem("hm_done"), sem("gelu_done"), sem("hm_hi"), sem("hm_lo")
        out_done, added = sem("out_done"), sem("added")
        stored = sem("stored")

        h0_g = h0_d.rearrange("(g t p) d -> g p t d", p=P, t=TG)
        x2_g = x2_d.rearrange("(g t p) d -> g p t d", p=P, t=TG)
        out_g = out.rearrange("(g t p) d -> g p t d", p=P, t=TG)
        HM = E * IC
        OUTS = 1 + E
        GROUP0 = 1
        GELU0 = 2
        ADD0 = 2
        block = ctx.enter_context(nc.Block())

        @block.sync
        def _(sp):
            sp.sem_inc(att_t, GROUP0)
            sp.sem_inc(base_done, GROUP0)
            sp.sem_inc(logit_done, GROUP0)
            sp.sem_inc(z_t, GROUP0)
            sp.sem_inc(gelu_done, GELU0)
            sp.sem_inc(hm_lo, GELU0)
            sp.sem_inc(added, ADD0)
            sp.sem_inc(out_done, OUTS)
            for dst, src in ((ident, ident_d), (lnp, ln2), (wg, w_gate.rearrange("(c p) e -> p c e", p=P)),
                             (bo_sb, bo), (b1_sb, b1), (b2_sb, b2)):
                sp.dma_start(dst[:], src).then_inc(const_loaded, 16)
            sp.dma_start(w1f[:], w1.rearrange("e (c p) i -> p e c i", p=P)).then_inc(w_loaded, 16)
            sp.dma_start(w2f[:], w2.rearrange("e (c p) d -> p e c d", p=P)).then_inc(w_loaded, 16)
            with sp.Fori(0, GROUPS) as g:
                sp.wait_ge(base_done, g + 1)
                sp.dma_start(h0[:], h0_g[g]).then_inc(rows_loaded, 16)
                sp.dma_start(x2[:], x2_g[g]).then_inc(rows_loaded, 16)
            with sp.Fori(0, GROUPS) as g:
                sp.wait_ge(added, g * OUTS + OUTS + ADD0)
                sp.dma_start(out_g[g], total[:, bass.ds(g * TG, TG), :]).then_inc(stored, 16)
            sp.wait_ge(stored, 16 * GROUPS)

        @block.gpsimd
        def _(pool):
            nc.gpsimd.memset(power[:], -0.5).then_inc(power_set, 1)
            pool.wait_ge(power_set, 1)
            with pool.Fori(0, GROUPS) as g:
                pool.wait_ge(vare_done, g + 1)
                nc.gpsimd.tensor_tensor(rstd[:], vare[:], power[:], ALU.pow).then_inc(rstd_done, 1)
                pool.wait_ge(h_done, g + 1)
                nc.gpsimd.tensor_tensor(total[:, bass.ds(g * TG, TG), :], x2[:], hg[:], ALU.add).then_inc(base_done, 1)

        @block.scalar
        def _(act):
            act.wait_ge(const_loaded, 16 * 6)
            with act.Fori(0, GROUPS) as g:
                act.wait_ge(att_t, g + GROUP0)
                for d in range(DC):
                    ins = nc.scalar.activation(att[:, d, :], acc[:, d, bass.ds(g * HALF, HALF)], ACT.Identity,
                                               bias=bo_sb[:, d:d + 1])
                ins.then_inc(att_done, 1)
                act.wait_ge(z_t, g + 1 + GROUP0)
                act.wait_ge(logit_done, g + GROUP0)
                for c in range(DC):
                    ins = nc.scalar.activation(h2f[:, c, :], ps_a[:, c, :], ACT.Identity, bias=lnp[:, 1, c:c + 1],
                                               scale=lnp[:, 0, c:c + 1])
                ins.then_inc(h2_f, 1)
                act.wait_ge(h2_f, g + 1)
                nc.scalar.activation(h2h[:, :, bass.ds(g * HALF, HALF)], h2f[:], ACT.Copy).then_inc(h2_h, 1)
            act.wait_ge(w_loaded, 32)
            nc.scalar.activation(w1h[:], w1f[:], ACT.Copy).then_inc(w_hi, 1)
            nc.scalar.activation(w2h[:], w2f[:], ACT.Copy).then_inc(w_hi, 1)
            act.wait_ge(route, 2)
            nc.scalar.activation(raw[:], rest[:], ACT.Exp).then_inc(route_exp, 1)
            act.wait_ge(route, 24)
            nc.scalar.activation(share[1][:], tmp[:], ACT.Exp).then_inc(route_exp, 1)
            with act.Fori(0, GROUPS) as g:
                for n in range(HM):
                    e, i = n // IC, n % IC
                    act.wait_ge(hm_done, g * HM + n + 1)
                    act.wait_ge(hm_lo, g * HM + n + GELU0 - 1)
                    nc.scalar.activation(hmf[n % 2][:], ps_h[:, n % 2, :], ACT.Gelu,
                                         bias=b1_sb[:, e, i:i + 1]).then_inc(gelu_done, 1)
                    act.wait_ge(gelu_done, g * HM + n + 1 + GELU0)
                    act.wait_ge(out_done, g * OUTS + e + (OUTS if e >= 2 else 4))
                    nc.scalar.activation(hmh[e % 2][:, i, :], hmf[n % 2][:], ACT.Copy).then_inc(hm_hi, 1)

        @block.vector
        def _(dve):
            with dve.Fori(0, GROUPS) as g:
                dve.wait_ge(rows_loaded, g * 32 + 32)
                dve.wait_ge(att_t, g + 1 + GROUP0)
                dve.wait_ge(base_done, g + GROUP0)
                for k in range(2):
                    rows = slice(2 * k, 2 * k + 2)
                    ins = nc.vector.tensor_tensor(hg[:, rows, :], ps_o[0][:, rows, :], h0[:, rows, :], ALU.add)
                ins.then_inc(h_done, 1)
                dve.wait_ge(h_done, g + 1)
                for t in range(TG):
                    nc.vector.bn_stats(stats[:, t, :], hg[:, t, :]).then_inc(stat_done, 1)
                dve.wait_ge(stat_done, g * TG + TG)
                nc.vector.memset(mark[:], 0.0)
                for t in range(TG):
                    ins = nc.vector.bn_aggr(mv[:, t, :], stats[:, t, :])
                ins.then_inc(rstd_done, 1)
                dve.wait_ge(rstd_done, g * 2 + 1)
                nc.vector.tensor_scalar(vare[:], mv[:, :, 1], EPS, None, ALU.add).then_inc(vare_done, 1)
                dve.wait_ge(rstd_done, g * 2 + 2)
                dve.wait_ge(z_t, g + GROUP0)
                for t in range(TG):
                    ins = nc.vector.tensor_scalar(zg[:, t, :], hg[:, t, :], mv[:, t, 0:1], rstd[:, t:t + 1],
                                                  ALU.subtract, ALU.mult)
                ins.then_inc(z_done, 1)
                dve.wait_ge(h2_h, g + 1)
                cols = bass.ds(g * HALF, HALF)
                nc.vector.tensor_tensor(h2l[:, :, cols], h2f[:], h2h[:, :, cols], ALU.subtract).then_inc(h2_l, 1)
                dve.wait_ge(gate_done, g + 1)
                nc.vector.tensor_copy(logit[:, bass.ds(g * TG, TG), :],
                                      ps_h[:, 0, 0:TG * E].rearrange("p (t e) -> p t e", e=E)).then_inc(logit_done, 1)
            dve.wait_ge(logit_done, GROUPS + GROUP0)

            steps = [0]

            def then(ins):
                steps[0] += 1
                ins.then_inc(route, 1)
                dve.wait_ge(route, steps[0])

            def bc(a):
                return a[:, :].unsqueeze(2).to_broadcast([P, TILES, E])

            def first(dst):
                then(nc.vector.tensor_copy(dst[:, :, 0:1], eq[:, :, 0:1]))
                then(nc.vector.tensor_copy(seen[:], eq[:, :, 0:1]))
                for e in range(1, E):
                    then(nc.vector.tensor_tensor(dst[:, :, e:e + 1], eq[:, :, e:e + 1], seen[:], ALU.is_gt))
                    if e < E - 1:
                        then(nc.vector.tensor_tensor(seen[:], seen[:], eq[:, :, e:e + 1], ALU.max))

            then(nc.vector.tensor_reduce(tmp[:], logit[:], AX.X, ALU.max))
            then(nc.vector.tensor_tensor(rest[:], logit[:], bc(tmp), ALU.subtract))
            dve.wait_ge(route_exp, 1)
            then(nc.vector.tensor_reduce(tmp[:], raw[:], AX.X, ALU.add))
            then(nc.vector.reciprocal(share[0][:], tmp[:]))
            then(nc.vector.tensor_tensor(raw[:], raw[:], bc(share[0]), ALU.mult))
            then(nc.vector.tensor_reduce(top[0][:], raw[:], AX.X, ALU.max))
            then(nc.vector.tensor_tensor(eq[:], raw[:], bc(top[0]), ALU.is_equal))
            first(pick[0])
            then(nc.vector.scalar_tensor_tensor(out=rest[:], in0=pick[0][:], scalar=-2.0, in1=raw[:],
                                                op0=ALU.mult, op1=ALU.add))
            then(nc.vector.tensor_reduce(top[1][:], rest[:], AX.X, ALU.max))
            then(nc.vector.tensor_tensor(tmp[:], top[1][:], top[0][:], ALU.subtract))
            gap = steps[0]
            then(nc.vector.tensor_tensor(eq[:], rest[:], bc(top[1]), ALU.is_equal))
            first(pick[1])
            assert gap <= 24 <= steps[0]
            dve.wait_ge(route_exp, 2)
            then(nc.vector.tensor_scalar(tmp[:], share[1][:], 1.0, None, ALU.add))
            then(nc.vector.reciprocal(share[0][:], tmp[:]))
            then(nc.vector.tensor_tensor(share[1][:], share[1][:], share[0][:], ALU.mult))
            then(nc.vector.tensor_tensor(pick[0][:], pick[0][:], bc(share[0]), ALU.mult))
            then(nc.vector.tensor_tensor(pick[1][:], pick[1][:], bc(share[1]), ALU.mult))
            nc.vector.tensor_tensor(comb[:].rearrange("p (t e) -> p t e", e=E), pick[0][:], pick[1][:],
                                    ALU.add).then_inc(comb_out, 1)
            dve.wait_ge(comb_tr, 1)
            nc.vector.tensor_copy(comb_t[:, 0:SEQ], ps_o[0][0:E, :, :].rearrange("p t d -> p (t d)"))
            nc.vector.tensor_copy(comb_t[:, SEQ:TOK], ps_o[1][0:E, :, :].rearrange("p t d -> p (t d)")).then_inc(comb_out, 1)
            dve.wait_ge(w_hi, 2)
            nc.vector.tensor_tensor(w1l[:], w1f[:], w1h[:], ALU.subtract).then_inc(w_lo, 1)
            nc.vector.tensor_tensor(w2l[:], w2f[:], w2h[:], ALU.subtract).then_inc(w_lo, 1)
            dve.wait_ge(comb_out, 2)
            dve.wait_ge(base_done, GROUPS + GROUP0)
            with dve.Fori(0, GROUPS) as g:
                dve.wait_ge(out_done, g * OUTS + 1)
                nc.vector.tensor_copy(comb_g[:], comb_t[:, bass.ds(g * HALF, HALF)]).then_inc(comb_cut, 1)

                def add(o):
                    dve.wait_ge(out_done, g * OUTS + o + 1 + OUTS)
                    dve.wait_ge(added, g * OUTS + o + ADD0)
                    ps = ps_o[0] if o == 0 else ps_o[o % 2]
                    for t in range(TG):
                        to = total[:, bass.ds(g * TG + t, 1), :].rearrange("p a d -> p (a d)")
                        if o == 0:
                            ins = nc.vector.tensor_tensor(to, ps[:, t, :], to, ALU.add)
                        else:
                            ins = nc.vector.scalar_tensor_tensor(
                                out=to, in0=ps[:, t, :], scalar=comb[:, bass.ds(g * TG * E + t * E + o - 1, 1)], in1=to,
                                op0=ALU.mult, op1=ALU.add)
                    ins.then_inc(added, 1)

                def low(n):
                    e, i = n // IC, n % IC
                    dve.wait_ge(hm_hi, g * HM + n + 1)
                    nc.vector.tensor_tensor(hml[e % 2][:, i, :], hmf[n % 2][:], hmh[e % 2][:, i, :],
                                            ALU.subtract).then_inc(hm_lo, 1)

                low(0), low(1), add(0), low(2), low(3), add(1), low(4), low(5), add(2), low(6), low(7), add(3), add(4)

        @block.tensor
        def _(pe):
            pe.wait_ge(const_loaded, 16 * 6)
            with pe.Fori(0, GROUPS) as g:
                pe.wait_ge(att_done, g + 1)
                pe.wait_ge(z_t, g + GROUP0)
                for t in range(TG):
                    for d in range(DC):
                        ins = nc.tensor.transpose(ps_o[0][:, t, d * P:(d + 1) * P], att[:, d, t * P:(t + 1) * P], ident[:])
                ins.then_inc(att_t, 1)
                pe.wait_ge(z_done, g + 1)
                for t in range(TG):
                    for c in range(DC):
                        ins = nc.tensor.transpose(ps_a[:, c, t * P:(t + 1) * P], zg[:, t, c * P:(c + 1) * P], ident[:])
                ins.then_inc(z_t, 1)
                pe.wait_ge(h2_f, g + 1)
                pe.wait_ge(logit_done, g + GROUP0)
                for t in range(TG):
                    for c in range(DC):
                        ins = nc.tensor.matmul(ps_h[:, 0, t * E:(t + 1) * E], h2f[:, c, t * P:(t + 1) * P], wg[:, c, :],
                                               start=(c == 0), stop=(c == DC - 1))
                ins.then_inc(gate_done, 1)
            pe.wait_ge(comb_out, 1)
            for t in range(TILES):
                at = ps_o[t // 8][0:E, :, :].rearrange("p t d -> p (t d)")
                ins = nc.tensor.transpose(at[:, (t % 8) * P:(t % 8 + 1) * P], comb[:, t * E:(t + 1) * E], ident[:])
            ins.then_inc(comb_tr, 1)
            pe.wait_ge(w_lo, 2)
            pe.wait_ge(h2_l, GROUPS)
            with pe.Fori(0, GROUPS) as g:
                def inner(e):
                    for i in range(IC):
                        n = e * IC + i
                        pe.wait_ge(gelu_done, g * HM + n + GELU0 - 1)
                        for q, (w, r) in enumerate(((w1h, h2h), (w1h, h2l), (w1l, h2h))):
                            for c in range(DC):
                                ins = nc.tensor.matmul(ps_h[:, n % 2, :], w[:, e, c, i * P:(i + 1) * P],
                                                       r[:, c, bass.ds(g * HALF, HALF)],
                                                       start=(q + c == 0), stop=(q == 2 and c == DC - 1))
                        ins.then_inc(hm_done, 1)

                def biases():
                    pe.wait_ge(comb_cut, g + 1)
                    pe.wait_ge(added, g * OUTS + ADD0)
                    for t in range(TG):
                        ins = nc.tensor.matmul(ps_o[0][:, t, :], comb_g[:, t * P:(t + 1) * P], b2_sb[:], start=True, stop=True)
                    ins.then_inc(out_done, 1)

                def outer(e):
                    pe.wait_ge(hm_lo, g * HM + (e + 1) * IC + GELU0)
                    pe.wait_ge(added, g * OUTS + e + ADD0)
                    for t in range(TG):
                        for q, (l, w) in enumerate(((hmh, w2h), (hmh, w2l), (hml, w2h))):
                            for i in range(IC):
                                ins = nc.tensor.matmul(ps_o[(e + 1) % 2][:, t, :], l[e % 2][:, i, t * P:(t + 1) * P],
                                                       w[:, e, i, :], start=(q + i == 0), stop=(q == 2 and i == IC - 1))
                    ins.then_inc(out_done, 1)

                inner(0), biases(), inner(1), outer(0), inner(2), outer(1), inner(3), outer(2), outer(3)


_CONSTS = ("ident", "identb", "mask", "rope")


def layer(nc, t, x2_d, h0_d, out):
    with ExitStack() as ctx:
        acc = ctx.enter_context(nc.sbuf_tensor("acc", [P, DC, TOK], F32))
        with ExitStack() as held:
            h1f = held.enter_context(nc.sbuf_tensor("h1f", [P, DC, TOK], F32))
            h1h = held.enter_context(nc.sbuf_tensor("h1h", [P, DC, TOK], F32R))
            h1l = held.enter_context(nc.sbuf_tensor("h1l", [P, DC, TOK], F32R))
            conv_layer(nc, t["x"], t["w_in_t"], t["w_out_t"], t["conv_par"], t["ln1"], t["ident"], x2_d, h0_d, h1h, h1l, h1f)
            attention(nc, t["w_qk"], t["w_v"], t["w_ov"], t["rope"], t["ident"], t["identb"], t["mask"], h1h, h1l, h1f, acc)
        experts(nc, t["ln2"], t["w_gate"], t["w1"], t["b1"], t["w2"], t["b2"], t["bo"], t["ident"], x2_d, h0_d, acc, out)


def kernel(**inputs):
    import ml_dtypes
    import numpy as np
    import concourse.bacc as bacc
    from concourse.bass_utils import run_bass_kernel_spmd as run

    a = {k[3:]: np.asarray(v) for k, v in inputs.items()}

    def per_partition(v, chunks):
        return v.reshape(chunks, P).T

    def head_cols(w, h):
        return w[:, h * HD:(h + 1) * HD].reshape(DC, P, HD).transpose(1, 0, 2).reshape(P, DC * HD)

    heads = [min(h, HEADS - 1) for h in range(HEADS + 1)]
    q_b, k_b, v_b = (per_partition(a[f"ffn_b{n}"], HEADS) for n in "qkv")
    w_qk = np.stack([np.concatenate([head_cols(a["ffn_wq"], h), head_cols(a["ffn_wk"], h), q_b[:, h:h + 1],
                                     k_b[:, h:h + 1]], 1) for h in heads])
    w_v = np.stack([head_cols(a["ffn_wv"], h) for h in heads])
    w_ov = np.stack([np.concatenate([a["ffn_wo"][h * HD:(h + 1) * HD], v_b[:, h:h + 1]], 1) for h in heads])
    par = np.stack([a["attn_conv_w"][:, 0, j] for j in range(TAPS)] + [a["attn_conv_b"], a["attn_D"]], 1)
    freq = (1.0 / np.power(np.float32(10000.0), np.arange(0, HD, 2, dtype=np.float32) / np.float32(HD))).astype(np.float32)
    angle = (np.arange(SEQ, dtype=np.float32)[:, None] * freq[None]).astype(np.float32).T
    cos, sin = np.cos(angle), np.sin(angle)
    rope = np.stack([np.concatenate([cos, cos]), np.concatenate([-sin, sin])], 1).astype(np.float32)
    mask = np.where(np.arange(2 * P)[None] <= np.arange(P)[:, None], 0.0, BIG)
    t = {
        "x": a["attn_x"].reshape(TOK, D),
        "w_in_t": a["attn_w_in"].T,
        "w_out_t": a["attn_w_out"].T,
        "conv_par": par.reshape(IB, P, TAPS + 2).transpose(1, 0, 2),
        "ln1": np.stack([per_partition(a["ffn_ln1_w"], DC), per_partition(a["ffn_ln1_b"], DC)], 1),
        "ln2": np.stack([per_partition(a["ffn_ln2_w"], DC), per_partition(a["ffn_ln2_b"], DC)], 1),
        "w_qk": w_qk, "w_v": w_v, "w_ov": w_ov, "rope": rope,
        "ident": np.eye(P, dtype=np.float32),
        "identb": np.eye(P).astype(ml_dtypes.bfloat16),
        "mask": mask.astype(ml_dtypes.bfloat16),
        "w_gate": a["ffn_w_gate"],
        "w1": a["ffn_we1"],
        "b1": a["ffn_be1"].reshape(EXPERTS, IC, P).transpose(2, 0, 1),
        "w2": a["ffn_we2"],
        "b2": a["ffn_be2"],
        "bo": per_partition(a["ffn_bo"], DC),
    }
    nc = bacc.Bacc("TRN2", target_bir_lowering=False, num_devices=1)
    arrays, aps = {}, {}
    for name, v in t.items():
        v = np.ascontiguousarray(v)
        arrays[name + "_dram"] = v
        aps[name] = nc.dram_tensor(name + "_dram", v.shape, mybir.dt.from_np(v.dtype), kind="ExternalInput").ap()
    x2_d = nc.dram_tensor("x2_scratch", (TOK, D), F32, kind="Internal").ap()
    h0_d = nc.dram_tensor("h0_scratch", (TOK, D), F32, kind="Internal").ap()
    out = nc.dram_tensor("out_dram", (TOK, D), F32, kind="ExternalOutput").ap()
    layer(nc, aps, x2_d, h0_d, out)
    r = run(nc, [arrays], core_ids=[0])
    return r.results[0]["out_dram"].reshape(BATCH, SEQ, D)
```

```python
from contextlib import ExitStack

import concourse.bass as bass
from concourse import mybir

F32 = mybir.dt.float32
F32R = mybir.dt.float32r
BF16 = mybir.dt.bfloat16
ALU = mybir.AluOpType
ACT = mybir.ActivationFunctionType
AX = mybir.AxisListType

P = 128
BATCH, SEQ, D = 2, 1024, 256
TOK = BATCH * SEQ
DC = D // P
DI = 512
IB = DI // P
TAPS = 4
HEADS, HD = 16, 128
EXPERTS, EI = 4, 256
IC = EI // P
HALF = SEQ // 2
TG = HALF // P
GROUPS = TOK // HALF
QB = SEQ // P
SCALE = float(HD) ** -0.5
EPS = 1e-5
BIG = -1e30

WQK = 4 * P + 2
WOV = D + 1


def scores_width(i):
    return max(256, (i + 1) * P)


def score_banks(i):
    return 1 if scores_width(i) <= 512 else 2


def spread(buf, i):
    nb = score_banks(i)
    return buf[:, 0:nb, 0:scores_width(i) // nb]


def packed(buf, i):
    return buf[:, 0:scores_width(i)].rearrange("p (a n) -> p a n", a=score_banks(i))


CHUNKS = [(i, j, min(4, i + 1 - j)) for i in range(QB) for j in range(0, i + 1, 4)]
NCH = len(CHUNKS)
FIRST_CHUNK = [min(c for c in range(NCH) if CHUNKS[c][0] == i) for i in range(QB)]
LAST_CHUNK = [max(c for c in range(NCH) if CHUNKS[c][0] == i) for i in range(QB)]
CHUNKS_TO_HALF = [LAST_CHUNK[3] + 1, NCH]

PERIOD = 64
AT = {
    "S": [0, 2, 9, 17, 36, 47, 49, 59],
    "T": [20, 27, 36, 37, 52, 59, 65, 76],
    "Q": [6, 17, 44, 56],
    "V": [25, 37],
    "O": [54, 84, 86],
    "W": [59, 74, 91, 111],
    "split_qk": [0],
    "split_o": [50],
}
LAG = {
    "S": {"max": 0, "exp": 4, "recip": 6, "norm": 1},
    "T": {"p_hi": 0, "p_lo": 0},
    "Q": {"q_cos": 0, "q_swap": 0, "q_sin": 0, "q_rope": 0, "q_hi": 12, "q_lo": 14},
    "V": {"v_hi": 3, "v_lo": 5},
    "O": {"o_hi": 0, "o_lo": 1},
    "W": {"acc": 0},
}
O_PIECES = [0, 1, 1]


def unit_order():
    placed = []
    for op, at in AT.items():
        for k, x in enumerate(at):
            parts = [(op, k)] if op != "T" else [("C", c) for c in range(FIRST_CHUNK[k], LAST_CHUNK[k] + 1)]
            for part, i in parts:
                placed.append((x, part, i))
                if (op, k) != ("O", 1):
                    placed += [(x + lag, what, O_PIECES[k] if op == "O" else i) for what, lag in LAG.get(op, {}).items()]
    order = sorted(range(len(placed)), key=lambda n: (placed[n][0] % PERIOD, n))
    return [(placed[n][1], placed[n][2], int(placed[n][0] // PERIOD)) for n in order]


UNIT = unit_order()
UNITS = HEADS * BATCH
MISC = [(op, k) for op, k, _ in UNIT if op in ("V", "Q", "W", "O") and (op, k) != ("O", 2)]
MISC_AGE = {(op, k): age for op, k, age in UNIT}


def bank_of(op, k):
    return MISC.index((op, k)) % 2


class Unit:

    def __init__(self, n, off):
        self.n, self.off, self.b = n, off, off % BATCH

    def count(self, each, k):
        return self.n * (2 * each) + (self.off * each + k)

    def head(self, more=0):
        return self.n + (self.off + more) // BATCH


def over_units(eng, work):
    def slots(n, off):
        for op, k, age in UNIT:
            last = off - age == UNITS - 1 and isinstance(n, int)
            if off < age and isinstance(n, int) or off == UNITS and not age:
                continue
            if last and (op[0] in "Qq" or op == "split_qk"):
                continue
            if op == "split_o" and (off - age) % 2 or op == "split_qk" and (off - age) % 2 == 0:
                continue
            work(op, k, Unit(n, off - age))

    slots(0, 0)
    with eng.Fori(0, (UNITS - 2) // 2) as n:
        slots(n, 1)
        slots(n, 2)
    slots(0, UNITS - 1)
    slots(0, UNITS)


def wait(eng, sem, value):
    if not isinstance(value, int) or value > 0:
        eng.wait_ge(sem, value)


CONV_PERIOD = 21.25
CONV_AT = {
    "stat": [-7.0, 36.0, 37.5],
    "aggr": [-2.0, 36.0, 38.5],
    "eps": [-1.5, 36.0, 40.0],
    "power": [-0.8, 40.7, 40.7],
    "norm": [-0.5, 37.0, 40.5],
    "turn": [0.5, 38.0],
    "x_hi": [4.0],
    "x_lo": [6.5],
    "in": [6.5, 6.8, 8.5, 12.3, 12.5, 14.3, 15.0, 17.8],
    "rows": [7.8, 13.8, 16.3, 20.8],
    "tap3": [8.3, 14.8, 17.8, 22.3],
    "tap0": [7.6, 15.6, 16.6, 22.1],
    "tap1": [9.4, 16.9, 18.9, 23.9],
    "tap2": [12.2, 18.7, 20.7, 27.2],
    "gate": [8.6, 15.1, 18.6, 24.1],
    "silu": [12.0, 19.0, 22.0, 28.0],
    "gated": [12.3, 19.8, 21.3, 27.8],
    "h_hi": [12.6, 21.1, 25.1, 28.6],
    "h_lo": [14.8, 20.8, 25.3, 25.8],
    "out": [28.6, 29.7],
    "x2": [34.2, 35.8],
    "h1_f": [44.0],
    "h1_h": [59.0],
    "h1_l": [65.5],
}
CONV_ORDER = [(op, k, g) for _, op, k, g in sorted(
    ((x + CONV_PERIOD * g, op, k, g) for op, at in CONV_AT.items() for k, x in enumerate(at) for g in range(GROUPS)),
    key=lambda o: o[0])]
TURNS = [(k, g) for op, k, g in CONV_ORDER if op == "turn"]


def conv_layer(nc, x, w_in_t, w_out_t, conv_par, ln1, ident_d, x2_d, h0_d, h1h, h1l, h1f):
    with ExitStack() as ctx:
        def sb(name, shape, dt=F32):
            return ctx.enter_context(nc.sbuf_tensor(name, shape, dt))

        def pb(name, shape, dt=F32):
            return ctx.enter_context(nc.psum_tensor(name, shape, dt))

        def sem(name):
            return ctx.enter_context(nc.semaphore("a_" + name))

        ident = sb("a_ident", [P, P])
        par = sb("a_par", [P, IB, TAPS + 2])
        lnp = sb("a_lnp", [P, 2, DC])
        wi = sb("wi", [P, DC, 2 * DI])
        wih = sb("wih", [P, DC, 2 * DI], F32R)
        wil = sb("wil", [P, DC, 2 * DI], F32R)
        wo = sb("wo", [P, IB, D])
        woh = sb("woh", [P, IB, D], F32R)
        wol = sb("wol", [P, IB, D], F32R)
        xs = [sb(f"xs{g}", [P, TG, D]) for g in range(GROUPS)]
        xn = sb("xn", [P, TG, D])
        xth = sb("xth", [P, DC, HALF], F32R)
        xtl = sb("xtl", [P, DC, HALF], F32R)
        xi = sb("xi", [P, IB, TAPS - 1 + SEQ])
        sg = sb("sg", [P, 2, HALF])
        cv = sb("cv", [P, 3, HALF])
        sx = sb("sx", [P, 2, HALF])
        hh = sb("hh", [P, IB, HALF], F32R)
        hl = sb("hl", [P, IB, HALF], F32R)
        h0 = sb("h0", [P, TG, D])
        zn = sb("zn", [P, TG, D])
        stats = [sb(f"a_stats{w}", [P, TG, 6]) for w in range(3)]
        mv = [sb(f"a_mv{w}", [P, TG, 2]) for w in range(3)]
        vare = [sb(f"a_vare{w}", [P, TG]) for w in range(3)]
        rstd = [sb(f"a_rstd{w}", [P, TG]) for w in range(3)]
        mark = sb("a_mark", [P, 1])
        power = sb("a_power", [P, TG])

        ps_t = pb("a_ps_t", [P, DC, HALF])
        ps_in = pb("a_ps_in", [P, 4, HALF])
        ps_out = pb("a_ps_out", [P, TG // 2, 2, D])

        wi_loaded, const_loaded, wo_loaded = sem("wi_loaded"), sem("const_loaded"), sem("wo_loaded")
        ident_loaded = sem("ident_loaded")
        wi_hi, wi_lo, wo_hi, wo_lo = sem("wi_hi"), sem("wi_lo"), sem("wo_hi"), sem("wo_lo")
        halo_zero, power_set = sem("halo_zero"), sem("power_set")
        x_loaded = [sem(f"x_loaded{g}") for g in range(GROUPS)]
        x2_stored, h0_stored = sem("x2_stored"), sem("h0_stored")
        stat_done = [sem(f"stat_done{w}") for w in range(3)]
        aggr_done = [sem(f"aggr_done{w}") for w in range(3)]
        eps_done = [sem(f"eps_done{w}") for w in range(3)]
        rstd_done = [sem(f"rstd_done{w}") for w in range(3)]
        norm_done = [sem(f"norm_done{w}") for w in range(3)]
        turned = [sem(f"turned{k}") for k in range(2)]
        x_hi, x_lo = sem("x_hi"), sem("x_lo")
        in_done = sem("in_done")
        rows_out = sem("rows_out")
        gate_out = sem("gate_out")
        tap_done = [sem(f"tap_done{j}") for j in range(TAPS)]
        silu_done, gated, h_hi, h_lo = sem("silu_done"), sem("gated"), sem("h_hi"), sem("h_lo")
        out_done, x2_done = sem("out_done"), sem("x2_done")
        h1_f, h1_h, h1_l = sem("h1_f"), sem("h1_h"), sem("h1_l")

        x_g = x.rearrange("(g t p) d -> g p t d", p=P, t=TG)
        x2_g = x2_d.rearrange("(g t p) d -> g p t d", p=P, t=TG)
        h0_g = h0_d.rearrange("(g t p) d -> g p t d", p=P, t=TG)
        block = ctx.enter_context(nc.Block())

        @block.sync
        def _(sp):
            sp.dma_start(xs[0][:], x_g[0]).then_inc(x_loaded[0], 16)
            sp.dma_start(wi[:], w_in_t.rearrange("(c p) n -> p c n", p=P)).then_inc(wi_loaded, 16)
            sp.dma_start(ident[:], ident_d).then_inc(ident_loaded, 16)
            sp.dma_start(par[:], conv_par).then_inc(const_loaded, 16)
            sp.dma_start(lnp[:], ln1).then_inc(const_loaded, 16)
            sp.dma_start(xs[1][:], x_g[1]).then_inc(x_loaded[1], 16)
            sp.dma_start(wo[:], w_out_t.rearrange("(c p) n -> p c n", p=P)).then_inc(wo_loaded, 16)
            for g in range(2, GROUPS):
                sp.dma_start(xs[g][:], x_g[g]).then_inc(x_loaded[g], 16)
            for g in range(GROUPS):
                sp.wait_ge(x2_done, 2 * g + 2)
                sp.dma_start(x2_g[g], xs[g][:]).then_inc(x2_stored, 16)
                sp.wait_ge(norm_done[1], g + 1)
                sp.dma_start(h0_g[g], h0[:]).then_inc(h0_stored, 16)
            sp.wait_ge(x2_stored, 16 * GROUPS)
            sp.wait_ge(h0_stored, 16 * GROUPS)

        @block.gpsimd
        def _(pool):
            nc.gpsimd.memset(power[:], -0.5).then_inc(power_set, 1)
            nc.gpsimd.memset(xi[:, :, 0:TAPS - 1], 0.0).then_inc(halo_zero, 1)
            pool.wait_ge(power_set, 1)
            for op, k, g in CONV_ORDER:
                if op == "power":
                    pool.wait_ge(eps_done[k], g + 1)
                    nc.gpsimd.tensor_tensor(rstd[k][:], vare[k][:], power[:], ALU.pow).then_inc(rstd_done[k], 1)
                    if (k, g) == (0, 0):
                        pool.wait_ge(wo_hi, 1)
                        nc.gpsimd.tensor_tensor(wol[:], wo[:], woh[:], ALU.subtract).then_inc(wo_lo, 1)
                elif op == "h_lo":
                    i = IB * g + k
                    pool.wait_ge(h_hi, i + 1)
                    nc.gpsimd.tensor_tensor(hl[:, k, :], cv[:, i % 3, :], hh[:, k, :], ALU.subtract).then_inc(h_lo, 1)
                elif op == "h1_l":
                    cols = slice(g * HALF, (g + 1) * HALF)
                    pool.wait_ge(h1_h, g + 1)
                    nc.gpsimd.tensor_tensor(h1l[:, :, cols], h1f[:, :, cols], h1h[:, :, cols],
                                            ALU.subtract).then_inc(h1_l, 1)

        @block.scalar
        def _(act):
            act.wait_ge(wi_loaded, 16)
            nc.scalar.activation(wih[:], wi[:], ACT.Copy).then_inc(wi_hi, 1)
            for op, k, g in CONV_ORDER:
                i = IB * g + k
                if op == "x_hi":
                    act.wait_ge(turned[0], g + 1)
                    if g > 0:
                        act.wait_ge(in_done, 2 * IB * g)
                    nc.scalar.activation(xth[:], ps_t[:], ACT.Copy).then_inc(x_hi, 1)
                    if g == 0:
                        act.wait_ge(wo_loaded, 16)
                        nc.scalar.activation(woh[:], wo[:], ACT.Copy).then_inc(wo_hi, 1)
                        act.wait_ge(const_loaded, 32)
                elif op == "rows":
                    act.wait_ge(in_done, 2 * i + 1)
                    lo = TAPS - 1 + (g % 2) * HALF
                    if g >= 2 and g % 2 == 0:
                        act.wait_ge(tap_done[2], i - IB + 1)
                    nc.scalar.activation(xi[:, k, lo:lo + HALF], ps_in[:, 2 * (i % 2), :], ACT.Copy).then_inc(rows_out, 1)
                elif op == "tap3":
                    if i >= 3:
                        act.wait_ge(h_lo, i - 2)
                    nc.scalar.activation(cv[:, i % 3, :], ps_in[:, 2 * (i % 2), :], ACT.Identity,
                                         bias=par[:, k, TAPS:TAPS + 1],
                                         scale=par[:, k, TAPS - 1:TAPS]).then_inc(tap_done[3], 1)
                elif op == "gate":
                    act.wait_ge(in_done, 2 * i + 2)
                    if i >= 2:
                        act.wait_ge(gated, i - 1)
                    nc.scalar.activation(sg[:, i % 2, :], ps_in[:, 2 * (i % 2) + 1, :], ACT.Silu).then_inc(gate_out, 1)
                elif op == "silu":
                    act.wait_ge(tap_done[2], i + 1)
                    if i >= 2:
                        act.wait_ge(gated, i - 1)
                    nc.scalar.activation(sx[:, i % 2, :], cv[:, i % 3, :], ACT.Silu).then_inc(silu_done, 1)
                elif op == "h_hi":
                    act.wait_ge(gated, i + 1)
                    if g > 0:
                        act.wait_ge(out_done, 2 * g)
                    nc.scalar.activation(hh[:, k, :], cv[:, i % 3, :], ACT.Copy).then_inc(h_hi, 1)
                elif op == "h1_f":
                    act.wait_ge(turned[1], g + 1)
                    for c in range(DC):
                        ins = nc.scalar.activation(h1f[:, c, g * HALF:(g + 1) * HALF], ps_t[:, c, :],
                                                   ACT.Identity, bias=lnp[:, 1, c:c + 1], scale=lnp[:, 0, c:c + 1])
                    ins.then_inc(h1_f, 1)
                elif op == "h1_h":
                    act.wait_ge(h1_f, g + 1)
                    cols = slice(g * HALF, (g + 1) * HALF)
                    nc.scalar.activation(h1h[:, :, cols], h1f[:, :, cols], ACT.Copy).then_inc(h1_h, 1)

        @block.vector
        def _(dve):
            for op, k, g in CONV_ORDER:
                i = IB * g + k
                if op == "stat":
                    src = (xs[g], xs[g], h0)[k]
                    if k == 0:
                        dve.wait_ge(x_loaded[g], 16)
                    elif k == 1:
                        dve.wait_ge(x2_done, 2 * g + 2)
                    else:
                        dve.wait_ge(norm_done[1], g + 1)
                    for t in range(TG):
                        nc.vector.bn_stats(stats[k][:, t, :], src[:, t, :]).then_inc(stat_done[k], 1)
                elif op == "aggr":
                    dve.wait_ge(stat_done[k], TG * g + TG)
                    nc.vector.memset(mark[:], 0.0)
                    for t in range(TG):
                        ins = nc.vector.bn_aggr(mv[k][:, t, :], stats[k][:, t, :])
                    ins.then_inc(aggr_done[k], 1)
                elif op == "eps":
                    dve.wait_ge(aggr_done[k], g + 1)
                    nc.vector.tensor_scalar(vare[k][:], mv[k][:, :, 1], EPS, None, ALU.add).then_inc(eps_done[k], 1)
                elif op == "norm":
                    src, dst = ((xs[g], xn), (xs[g], h0), (h0, zn))[k]
                    dve.wait_ge(rstd_done[k], g + 1)
                    if g > 0:
                        if k == 1:
                            dve.wait_ge(h0_stored, 16 * g)
                        else:
                            dve.wait_ge(turned[k // 2], g)
                    for t in range(TG):
                        ins = nc.vector.tensor_scalar(dst[:, t, :], src[:, t, :], mv[k][:, t, 0:1], rstd[k][:, t:t + 1],
                                                      ALU.subtract, ALU.mult)
                    ins.then_inc(norm_done[k], 1)
                    if (k, g) == (0, 0):
                        dve.wait_ge(wi_hi, 1)
                        nc.vector.tensor_tensor(wil[:], wi[:], wih[:], ALU.subtract).then_inc(wi_lo, 1)
                        dve.wait_ge(halo_zero, 1)
                        dve.wait_ge(const_loaded, 32)
                elif op == "x_lo":
                    dve.wait_ge(x_hi, g + 1)
                    nc.vector.tensor_tensor(xtl[:], ps_t[:], xth[:], ALU.subtract).then_inc(x_lo, 1)
                elif op in ("tap0", "tap1", "tap2"):
                    j = int(op[3])
                    dve.wait_ge(rows_out, i + 1)
                    dve.wait_ge(tap_done[j - 1 if j else 3], i + 1)
                    lo = (g % 2) * HALF + j
                    nc.vector.scalar_tensor_tensor(out=cv[:, i % 3, :], in0=xi[:, k, lo:lo + HALF], scalar=par[:, k, j:j + 1],
                                                   in1=cv[:, i % 3, :], op0=ALU.mult, op1=ALU.add).then_inc(tap_done[j], 1)
                elif op == "gated":
                    dve.wait_ge(silu_done, i + 1)
                    dve.wait_ge(gate_out, i + 1)
                    nc.vector.scalar_tensor_tensor(out=cv[:, i % 3, :], in0=sx[:, i % 2, :],
                                                   scalar=par[:, k, TAPS + 1:TAPS + 2], in1=sg[:, i % 2, :],
                                                   op0=ALU.mult, op1=ALU.mult).then_inc(gated, 1)
                elif op == "x2":
                    dve.wait_ge(out_done, 2 * g + k + 1)
                    rows = xs[g][:, 2 * k:2 * k + 2, :]
                    nc.vector.tensor_tensor(rows, ps_out[:, k], rows, ALU.add).then_inc(x2_done, 1)

        @block.tensor
        def _(pe):
            pe.wait_ge(ident_loaded, 16)
            for op, k, g in CONV_ORDER:
                if op == "turn":
                    n = TURNS.index((k, g))
                    if n > 0:
                        before, of = TURNS[n - 1]
                        pe.wait_ge((x_lo, h1_f)[before], of + 1)
                    pe.wait_ge(norm_done[2 * k], g + 1)
                    src = (xn, zn)[k]
                    for t in range(TG):
                        for c in range(DC):
                            ins = nc.tensor.transpose(ps_t[:, c, t * P:(t + 1) * P], src[:, t, c * P:(c + 1) * P], ident[:])
                    ins.then_inc(turned[k], 1)
                elif op == "in":
                    i = 2 * IB * g + k
                    n = (k // 2) * P + (k % 2) * DI
                    if i >= 4:
                        if k % 2 == 0:
                            pe.wait_ge(rows_out, i // 2 - 1)
                            pe.wait_ge(tap_done[3], i // 2 - 1)
                        else:
                            pe.wait_ge(gate_out, i // 2 - 1)
                    if k == 0:
                        pe.wait_ge(x_hi, g + 1)
                    if i == 0:
                        pe.wait_ge(wi_hi, 1)
                    for q, (w, r) in enumerate(((wih, xth), (wih, xtl), (wil, xth))):
                        if k == 0 and q == 1:
                            pe.wait_ge(x_lo, g + 1)
                        if i == 0 and q == 2:
                            pe.wait_ge(wi_lo, 1)
                        for c in range(DC):
                            ins = nc.tensor.matmul(ps_in[:, i % 4, :], w[:, c, n:n + P], r[:, c, :],
                                                   start=(q + c == 0), stop=(q == 2 and c == DC - 1))
                    ins.then_inc(in_done, 1)
                elif op == "out":
                    pe.wait_ge(h_lo, IB * (g + 1))
                    if g > 0:
                        pe.wait_ge(x2_done, 2 * (g - 1) + k + 1)
                    else:
                        pe.wait_ge(wo_lo, 1)
                    for t in range(2 * k, 2 * k + 2):
                        for q, (l, w) in enumerate(((hh, woh), (hh, wol), (hl, woh))):
                            for m in range(IB):
                                ins = nc.tensor.matmul(ps_out[:, k, t % 2, :], l[:, m, t * P:(t + 1) * P], w[:, m, :],
                                                       start=(q + m == 0), stop=(q == 2 and m == IB - 1))
                    ins.then_inc(out_done, 1)


def attention(nc, w_qk, w_v, w_ov, rope, ident_d, identb_d, mask_d, h1h, h1l, h1f, acc):
    with ExitStack() as ctx:
        def sb(name, shape, dt=F32):
            return ctx.enter_context(nc.sbuf_tensor(name, shape, dt))

        def pb(name, shape, dt=F32):
            return ctx.enter_context(nc.psum_tensor(name, shape, dt))

        def sem(name):
            return ctx.enter_context(nc.semaphore("b_" + name))

        ident = sb("b_ident", [P, P])
        identb = sb("b_identb", [P, P], BF16)
        mask = sb("b_mask", [P, 2 * P], BF16)
        cos_sin = sb("b_cos_sin", [P, 2, SEQ])
        wqk = sb("b_wqk", [P, WQK])
        wqkh = sb("b_wqkh", [P, 4, P], F32R)
        wqkl = sb("b_wqkl", [P, 4, P], F32R)
        bqk = sb("b_bqk", [P, 2])
        wv = sb("b_wv", [P, DC, P])
        wov = sb("b_wov", [P, WOV])
        woh = sb("b_woh", [P, D], F32R)
        wol = sb("b_wol", [P, D], F32R)
        bv = sb("b_bv", [P, 1])
        qkh = [sb(f"b_qkh{b}", [P, 2, SEQ], F32R) for b in range(BATCH)]
        qkl = [sb(f"b_qkl{b}", [P, 2, SEQ], F32R) for b in range(BATCH)]
        rot = sb("b_rot", [P, 2, HALF])
        swp = sb("b_swp", [P, 2, HALF])
        vh = sb("b_vh", [P, QB, HD], F32R)
        vl = sb("b_vl", [P, QB, HD], F32R)
        prob = [sb(f"b_prob{i}", [P, SEQ]) for i in range(4)]
        pth = [sb(f"b_pth{f}", [P, 4 * f + 4, HALF], F32R) for f in range(2)]
        ptl = [sb(f"b_ptl{f}", [P, 4 * f + 4, HALF], F32R) for f in range(2)]
        oh = [sb(f"b_oh{f}", [P, HALF], F32R) for f in range(2)]
        ol = [sb(f"b_ol{f}", [P, HALF], F32R) for f in range(2)]
        nmax = sb("b_nmax", [P, BATCH, QB])
        rsum = sb("b_rsum", [P, BATCH, QB])
        rinv = sb("b_rinv", [P, BATCH, QB])

        ps_s = [pb(f"b_ps_s{i}", [P, 2, HALF]) for i in range(2)]
        ps_t = pb("b_ps_t", [P, 2, HALF])
        ps_m = pb("b_ps_m", [P, 2, HALF])

        const_loaded = sem("const_loaded")
        qk_loaded = sem("qk_loaded")
        v_loaded = sem("v_loaded")
        ov_loaded = sem("ov_loaded")
        zeroed = sem("zeroed")
        wqk_hi, wqk_lo = sem("wqk_hi"), sem("wqk_lo")
        wo_hi, wo_lo = sem("wo_hi"), sem("wo_lo")
        s_done, max_done, exp_done = sem("s_done"), sem("max_done"), sem("exp_done")
        recip_done, norm_done = sem("recip_done"), sem("norm_done")
        t_done, p_hi, p_lo = sem("t_done"), sem("p_hi"), sem("p_lo")
        q_done, q_cos, q_swap, q_sin = sem("q_done"), sem("q_cos"), sem("q_swap"), sem("q_sin")
        q_rope, q_hi, q_lo = sem("q_rope"), sem("q_hi"), sem("q_lo")
        v_done, v_hi, v_lo = sem("v_done"), sem("v_hi"), sem("v_lo")
        o_done, o_hi, o_lo = sem("o_done"), sem("o_hi"), sem("o_lo")
        w_done, acc_done = sem("w_done"), sem("acc_done")

        block = ctx.enter_context(nc.Block())

        def piece(k):
            return k % 2, k // 2

        @block.sync
        def _(sp):
            sp.dma_start(wqk[:], w_qk[0]).then_inc(qk_loaded, 16)
            sp.dma_start(cos_sin[:], rope).then_inc(const_loaded, 16)
            sp.dma_start(wv[:], w_v[0].rearrange("p (c n) -> p c n", c=DC)).then_inc(v_loaded, 16)
            sp.dma_start(wov[:], w_ov[0]).then_inc(ov_loaded, 16)
            sp.dma_start(ident[:], ident_d).then_inc(const_loaded, 16)
            sp.dma_start(identb[:], identb_d).then_inc(const_loaded, 16)
            sp.dma_start(mask[:], mask_d).then_inc(const_loaded, 16)
            with sp.Fori(0, HEADS - 1) as h:
                sp.wait_ge(wqk_lo, h + 1)
                sp.dma_start(wqk[:], w_qk[h + 1]).then_inc(qk_loaded, 16)
                sp.wait_ge(wo_lo, h + 1)
                sp.dma_start(wov[:], w_ov[h + 1]).then_inc(ov_loaded, 16)
                sp.wait_ge(v_done, h * 4 + 4)
                sp.dma_start(wv[:], w_v[h + 1].rearrange("p (c n) -> p c n", c=DC)).then_inc(v_loaded, 16)

        @block.gpsimd
        def _(pool):
            nc.gpsimd.memset(acc[:], 0.0).then_inc(zeroed, 1)
            for f in range(2):
                nc.gpsimd.memset(pth[f][:, 4 * f + 3, 2 * P:3 * P].bitcast(F32), 0.0).then_inc(zeroed, 1)
                nc.gpsimd.memset(ptl[f][:, 4 * f + 3, 2 * P:3 * P].bitcast(F32), 0.0).then_inc(zeroed, 1)
            pool.wait_ge(const_loaded, 16 * 4)

            def sin(k, n):
                half = piece(k)[1]
                pool.wait_ge(q_swap, n)
                nc.gpsimd.tensor_tensor(swp[:, k % 2, :], swp[:, k % 2, :], cos_sin[:, 1, half * HALF:(half + 1) * HALF],
                                        ALU.mult).then_inc(q_sin, 1)

            def rotate(k, n):
                pool.wait_ge(q_sin, n)
                nc.gpsimd.tensor_tensor(rot[:, k % 2, :], rot[:, k % 2, :], swp[:, k % 2, :], ALU.add).then_inc(q_rope, 1)

            for k in range(4):
                sin(k, k + 1)
                rotate(k, k + 1)

            def work(op, k, u):
                if op == "norm":
                    pool.wait_ge(recip_done, u.count(8, k + 1))
                    row = prob[k % 4][:, 0:(k + 1) * P]
                    nc.gpsimd.tensor_tensor(row, row, rinv[:, u.b, k:k + 1].to_broadcast([P, (k + 1) * P]),
                                            ALU.mult).then_inc(norm_done, 1)
                elif op == "q_sin":
                    sin(k, u.count(4, k + 5))
                elif op == "q_rope":
                    rotate(k, u.count(4, k + 5))

            over_units(pool, work)

        @block.scalar
        def _(act):
            def split_qk(loaded):
                act.wait_ge(qk_loaded, loaded)
                nc.scalar.activation(wqkh[:, 0:2, :], wqk[:, 0:2 * P].rearrange("p (c n) -> p c n", c=2), ACT.Copy,
                                     scale=SCALE)
                nc.scalar.activation(wqkh[:, 2:4, :], wqk[:, 2 * P:4 * P].rearrange("p (c n) -> p c n", c=2),
                                     ACT.Copy).then_inc(wqk_hi, 1)

            def swap(k, n, bank):
                which = piece(k)[0]
                act.wait_ge(q_cos, n)
                wait(act, q_rope, n - 2)
                lo, hi = slice(0, HD // 2), slice(HD // 2, HD)
                for to, of in ((lo, hi), (hi, lo)):
                    ins = nc.scalar.activation(swp[to, k % 2, :], ps_m[of, bank, :], ACT.Identity,
                                               bias=bqk[of, which:which + 1])
                ins.then_inc(q_swap, 1)

            def high(k, n, dst):
                which, half = piece(k)
                act.wait_ge(q_rope, n)
                nc.scalar.activation(dst[:, which, half * HALF:(half + 1) * HALF], rot[:, k % 2, :],
                                     ACT.Copy).then_inc(q_hi, 1)

            split_qk(16)
            for k in range(4):
                swap(k, k + 1, k % 2)
                high(k, k + 1, qkh[0])

            def work(op, k, u):
                if op == "split_o":
                    act.wait_ge(ov_loaded, u.head() * 16 + 16)
                    wait(act, w_done, u.count(4, 0))
                    nc.scalar.activation(woh[:], wov[:, 0:D], ACT.Copy).then_inc(wo_hi, 1)
                elif op == "split_qk":
                    act.wait_ge(q_done, u.count(4, 4))
                    split_qk(u.head(1) * 16 + 16)
                elif op == "exp":
                    act.wait_ge(max_done, u.count(8, k + 1))
                    n = LAST_CHUNK[k - 4] + 1 if k >= 4 else LAST_CHUNK[k + 4] + 1 - NCH
                    wait(act, t_done, u.count(NCH, n))
                    nc.scalar.activation(packed(prob[k % 4], k), spread(ps_s[k % 2], k), ACT.Exp,
                                         bias=nmax[:, u.b, k:k + 1], accum_out=rsum[:, u.b, k:k + 1]).then_inc(exp_done, 1)
                elif op == "p_hi":
                    i, j, n = CHUNKS[k]
                    act.wait_ge(t_done, u.count(NCH, k + 1))
                    nc.scalar.activation(pth[i // 4][:, j:j + n, (i % 4) * P:(i % 4 + 1) * P],
                                         ps_t[:, k % 2, 0:n * P].rearrange("p (n q) -> p n q", n=n),
                                         ACT.Copy).then_inc(p_hi, 1)
                elif op == "q_swap":
                    swap(k, u.count(4, k + 5), bank_of("Q", k))
                elif op == "q_hi":
                    high(k, u.count(4, k + 5), qkh[1 - u.b])
                elif op == "v_hi":
                    act.wait_ge(v_done, u.count(2, k + 1))
                    nc.scalar.activation(vh[:, 4 * k:4 * k + 4, :],
                                         ps_m[:, bank_of("V", k), :].rearrange("p (n d) -> p n d", n=4),
                                         ACT.Copy).then_inc(v_hi, 1)
                elif op == "o_hi":
                    act.wait_ge(o_done, u.count(2, k + 1))
                    act.wait_ge(wo_lo, u.head() + 1)
                    nc.scalar.activation(oh[k][:], ps_m[:, bank_of("O", k), :], ACT.Identity,
                                         bias=bv[:, 0:1]).then_inc(o_hi, 1)

            over_units(act, work)

        @block.vector
        def _(dve):
            def split_qk(n):
                dve.wait_ge(wqk_hi, n)
                nc.vector.scalar_tensor_tensor(out=wqkl[:, 0:2, :], in0=wqk[:, 0:2 * P].rearrange("p (c n) -> p c n", c=2),
                                               scalar=SCALE, in1=wqkh[:, 0:2, :], op0=ALU.mult, op1=ALU.subtract)
                nc.vector.tensor_tensor(wqkl[:, 2:4, :], wqk[:, 2 * P:4 * P].rearrange("p (c n) -> p c n", c=2),
                                        wqkh[:, 2:4, :], ALU.subtract)
                nc.vector.tensor_scalar(bqk[:, 0:1], wqk[:, 4 * P:4 * P + 1], SCALE, None, ALU.mult)
                nc.vector.tensor_copy(bqk[:, 1:2], wqk[:, 4 * P + 1:4 * P + 2]).then_inc(wqk_lo, 1)

            def times_cos(k, n, bank):
                which, half = piece(k)
                dve.wait_ge(q_done, n)
                nc.vector.scalar_tensor_tensor(out=rot[:, k % 2, :], in0=ps_m[:, bank, :], scalar=bqk[:, which:which + 1],
                                               in1=cos_sin[:, 0, half * HALF:(half + 1) * HALF],
                                               op0=ALU.add, op1=ALU.mult).then_inc(q_cos, 1)

            def low(k, n, hi, lo):
                which, half = piece(k)
                cols = slice(half * HALF, (half + 1) * HALF)
                dve.wait_ge(q_hi, n)
                nc.vector.tensor_tensor(lo[:, which, cols], rot[:, k % 2, :], hi[:, which, cols],
                                        ALU.subtract).then_inc(q_lo, 1)

            split_qk(1)
            dve.wait_ge(wqk_lo, 1)
            dve.wait_ge(const_loaded, 16 * 4)
            dve.wait_ge(zeroed, 1)
            for k in range(4):
                times_cos(k, k + 1, k % 2)
                low(k, k + 1, qkh[0], qkl[0])

            def work(op, k, u):
                if op == "split_o":
                    dve.wait_ge(wo_hi, u.head() + 1)
                    nc.vector.tensor_tensor(wol[:], wov[:, 0:D], woh[:], ALU.subtract)
                    nc.vector.tensor_copy(bv[:], wov[:, D:D + 1]).then_inc(wo_lo, 1)
                elif op == "split_qk":
                    dve.wait_ge(q_swap, u.count(4, 4))
                    split_qk(u.head(1) + 1)
                    dve.wait_ge(wqk_lo, u.head(1) + 1)
                elif op == "max":
                    dve.wait_ge(s_done, u.count(8, k + 1))
                    nc.vector.tensor_reduce(nmax[:, u.b, k:k + 1], spread(ps_s[k % 2], k), AX.XY, ALU.max,
                                            negate=True).then_inc(max_done, 1)
                elif op == "recip":
                    dve.wait_ge(exp_done, u.count(8, k + 1))
                    nc.vector.reciprocal(rinv[:, u.b, k:k + 1], rsum[:, u.b, k:k + 1]).then_inc(recip_done, 1)
                elif op == "p_lo":
                    i, j, n = CHUNKS[k]
                    f, q = i // 4, slice((i % 4) * P, (i % 4 + 1) * P)
                    dve.wait_ge(p_hi, u.count(NCH, k + 1))
                    nc.vector.tensor_tensor(ptl[f][:, j:j + n, q],
                                            ps_t[:, k % 2, 0:n * P].rearrange("p (n q) -> p n q", n=n),
                                            pth[f][:, j:j + n, q], ALU.subtract).then_inc(p_lo, 1)
                elif op == "q_cos":
                    times_cos(k, u.count(4, k + 5), bank_of("Q", k))
                elif op == "q_lo":
                    low(k, u.count(4, k + 5), qkh[1 - u.b], qkl[1 - u.b])
                elif op == "v_lo":
                    dve.wait_ge(v_hi, u.count(2, k + 1))
                    nc.vector.tensor_tensor(vl[:, 4 * k:4 * k + 4, :],
                                            ps_m[:, bank_of("V", k), :].rearrange("p (n d) -> p n d", n=4),
                                            vh[:, 4 * k:4 * k + 4, :], ALU.subtract).then_inc(v_lo, 1)
                elif op == "o_lo":
                    dve.wait_ge(o_hi, u.count(2, k + 1))
                    nc.vector.scalar_tensor_tensor(out=ol[k][:], in0=ps_m[:, bank_of("O", k), :], scalar=bv[:, 0:1],
                                                   in1=oh[k][:], op0=ALU.add, op1=ALU.subtract).then_inc(o_lo, 1)
                elif op == "acc":
                    dve.wait_ge(w_done, u.count(4, k + 1))
                    t = u.b * SEQ + (k // 2) * HALF
                    to = acc[:, k % 2, t:t + HALF]
                    nc.vector.tensor_tensor(to, ps_m[:, bank_of("W", k), :], to, ALU.add).then_inc(acc_done, 1)

            over_units(dve, work)

        @block.tensor
        def _(pe):
            def project(k, batch, bank):
                which, half = piece(k)
                t = batch * SEQ + half * HALF
                for q, (w, r) in enumerate(((wqkh, h1h), (wqkh, h1l), (wqkl, h1h))):
                    for c in range(DC):
                        ins = nc.tensor.matmul(ps_m[:, bank, :], w[:, 2 * which + c, :], r[:, c, t:t + HALF],
                                               start=(q + c == 0), stop=(q == 2 and c == DC - 1))
                ins.then_inc(q_done, 1)

            def bank_free(op, k, u):
                m, off = MISC.index((op, k)), u.off + MISC_AGE[op, k]
                while True:
                    m, off = (m - 2) % len(MISC), off - (m < 2)
                    before, i = MISC[m]
                    v = Unit(u.n, off - MISC_AGE[before, i])
                    if not isinstance(u.n, int):
                        break
                    if off < 0:
                        return
                    if 0 <= v.off < UNITS - (before == "Q"):
                        break
                sem, each, more = {"V": (v_lo, 2, 1), "Q": (q_swap, 4, 5), "O": (o_lo, 2, 1), "W": (acc_done, 4, 1)}[before]
                pe.wait_ge(sem, v.count(each, i + more))

            pe.wait_ge(wqk_lo, 1)
            for k in range(4):
                if k >= 2:
                    pe.wait_ge(q_swap, k - 1)
                project(k, 0, k % 2)
            pe.wait_ge(const_loaded, 16 * 4)
            pe.wait_ge(zeroed, 5)
            pe.wait_ge(q_swap, 4)

            def work(op, k, u):
                if op in ("V", "Q", "O", "W") and (op, k) != ("O", 2):
                    bank_free(op, k, u)
                if op == "S":
                    pe.wait_ge(q_lo, u.count(4, 2 if k < 4 else 4))
                    wait(pe, exp_done, u.count(8, k - 1))
                    nb = score_banks(k)
                    w = scores_width(k) // nb
                    q = slice(k * P, (k + 1) * P)
                    for n, (l, r) in enumerate(((qkh, qkh), (qkh, qkl), (qkl, qkh))):
                        for g in range(nb):
                            nc.tensor.matmul(ps_s[k % 2][:, g, 0:w], l[u.b][:, 0, q], r[u.b][:, 1, g * w:(g + 1) * w],
                                             start=(n == 0), stop=(n == 2 and g < nb - 1))
                    mw = 2 * P if k == 0 else P
                    nc.tensor.matmul(ps_s[k % 2][:, nb - 1, w - mw:w], identb[:], mask[:, 0:mw],
                                     start=False, stop=True).then_inc(s_done, 1)
                elif op == "C":
                    i, j, n = CHUNKS[k]
                    pe.wait_ge(norm_done, u.count(8, i + 1))
                    wait(pe, p_lo, u.count(NCH, k - 1))
                    for a in range(n):
                        ins = nc.tensor.transpose(ps_t[:, k % 2, a * P:(a + 1) * P],
                                                  prob[i % 4][:, (j + a) * P:(j + a + 1) * P], ident[:])
                    ins.then_inc(t_done, 1)
                elif op == "V":
                    pe.wait_ge(v_loaded, u.head() * 16 + 16)
                    for a in range(4):
                        t = u.b * SEQ + (4 * k + a) * P
                        for c in range(DC):
                            ins = nc.tensor.matmul(ps_m[:, bank_of(op, k), a * HD:(a + 1) * HD], h1f[:, c, t:t + P],
                                                   wv[:, c, :], start=(c == 0), stop=(c == DC - 1))
                    ins.then_inc(v_done, 1)
                elif op == "Q":
                    pe.wait_ge(wqk_lo, u.head(1) + 1)
                    project(k, 1 - u.b, bank_of(op, k))
                elif op == "O":
                    f = min(k, 1)
                    pe.wait_ge(p_lo, u.count(NCH, CHUNKS_TO_HALF[f]))
                    pe.wait_ge(v_lo, u.count(2, f + 1))
                    last = 4 * f + 3
                    for j in range(4 if k == 2 else 0, 8 if k == 2 else 4):
                        q0 = min(max(0, j - 4 * f) * P, HALF - 2 * P)
                        for n, (l, r) in enumerate(((vh, pth), (vh, ptl), (vl, pth))):
                            ins = nc.tensor.matmul(ps_m[:, bank_of(op, f), q0:HALF], l[:, j, :], r[f][:, j, q0:HALF],
                                                   start=(j == 0 and n == 0), stop=(j == last and n == 2))
                    if k != 1:
                        ins.then_inc(o_done, 1)
                elif op == "W":
                    f, d = k // 2, slice((k % 2) * P, (k % 2 + 1) * P)
                    pe.wait_ge(o_lo, u.count(2, f + 1))
                    pe.wait_ge(wo_lo, u.head() + 1)
                    for n, (l, r) in enumerate(((woh, oh), (woh, ol), (wol, oh))):
                        ins = nc.tensor.matmul(ps_m[:, bank_of(op, k), :], l[:, d], r[f][:], start=(n == 0), stop=(n == 2))
                    ins.then_inc(w_done, 1)

            over_units(pe, work)


EXPERT_PERIOD = 27
EXPERT_AT = {
    "att": [0], "turn_att": [1.2], "h": [2.2], "base": [3.5],
    "stat": [3.5], "aggr": [5], "eps": [5.3], "power": [5.5], "norm": [6],
    "turn_z": [7], "h2_f": [8], "gate": [9], "h2_h": [9.5], "h2_l": [10],
    "route": [11], "turn_comb": [17.5], "comb_out": [18],
    "inner": [13, 14.3, 18.7, 20, 24.4, 25.7, 30.1, 31.4],
    "gelu": [14.3, 15.6, 20, 21.3, 25.7, 27, 31.4, 32.7],
    "hm_hi": [14.9, 16.2, 20.6, 21.9, 26.3, 27.6, 32, 33.3],
    "hm_lo": [15.5, 16.8, 21.2, 22.5, 26.9, 28.2, 32.6, 33.9],
    "outer": [21.3, 27.1, 32.8, 42.6], "bias": [24], "add": [24.4, 30.2, 35.9, 45.7, 25.8],
}
EXPERT_ORDER = [(op, k, int(x // EXPERT_PERIOD)) for x, op, k in sorted(
    ((x, op, k) for op, at in EXPERT_AT.items() for k, x in enumerate(at)), key=lambda o: o[0] % EXPERT_PERIOD)]
ADDS = sorted(range(EXPERTS + 1), key=lambda k: EXPERT_AT["add"][k])


class Group:

    def __init__(self, n, off):
        self.n, self.off = n, off
        self.first = isinstance(n, int) and off == 0

    def count(self, each, k):
        return self.n * each + (self.off * each + k)

    def cols(self, size):
        if isinstance(self.n, int):
            return slice(self.off * size, (self.off + 1) * size)
        return bass.ds(self.n * size + self.off * size, size)


def over_expert_groups(eng, work):
    def slots(n, off):
        for op, k, age in EXPERT_ORDER:
            if isinstance(n, int) and not 0 <= off - age < GROUPS:
                continue
            work(op, k, Group(n, off - age))

    slots(0, 0)
    slots(0, 1)
    with eng.Fori(0, GROUPS - 2) as n:
        slots(n, 2)
    slots(0, GROUPS)


def experts(nc, ln2, w_gate, w1, b1, w2, b2, bo, earlier_d, ident_d, x2_d, h0_d, acc, out):
    with ExitStack() as ctx:
        def sb(name, shape, dt=F32):
            return ctx.enter_context(nc.sbuf_tensor(name, shape, dt))

        def pb(name, shape, dt=F32):
            return ctx.enter_context(nc.psum_tensor(name, shape, dt))

        def sem(name):
            return ctx.enter_context(nc.semaphore("c_" + name))

        E = EXPERTS
        TILES = TOK // P
        HM = E * IC
        ident = sb("c_ident", [P, P])
        lnp = sb("c_lnp", [P, 2, DC])
        wg = sb("c_wg", [P, DC, E])
        bo_sb = sb("c_bo", [P, DC])
        b1_sb = sb("c_b1", [P, E, IC])
        b2_sb = sb("c_b2", [E, D])
        earlier = sb("c_earlier", [P, E, E])
        w1f = sb("c_w1f", [P, E, DC, EI])
        w1h = sb("c_w1h", [P, E, DC, EI], F32R)
        w1l = sb("c_w1l", [P, E, DC, EI], F32R)
        w2f = sb("c_w2f", [P, E, IC, D])
        w2h = sb("c_w2h", [P, E, IC, D], F32R)
        w2l = sb("c_w2l", [P, E, IC, D], F32R)
        att = sb("c_att", [P, DC, HALF])
        h0 = sb("c_h0", [P, TG, D])
        x2 = sb("c_x2", [P, TG, D])
        hg = sb("c_hg", [P, TG, D])
        zg = sb("c_zg", [P, TG, D])
        h2f = sb("c_h2f", [P, DC, HALF])
        h2h = sb("c_h2h", [P, DC, TOK], F32R)
        h2l = sb("c_h2l", [P, DC, TOK], F32R)
        total = sb("c_total", [P, TILES, D])
        stats = sb("c_stats", [P, TG, 6])
        mv = sb("c_mv", [P, TG, 2])
        rstd = sb("c_rstd", [P, TG])
        vare = sb("c_vare", [P, TG])
        mark = sb("c_mark", [P, 1])
        power = sb("c_power", [P, TG])
        most = sb("c_most", [P, TG])
        less = sb("c_less", [P, TG, E])
        prob = sb("c_prob", [P, TG, E])
        inv = sb("c_inv", [P, TG])
        above = sb("c_above", [P, TG, E, E])
        equal = sb("c_equal", [P, TG, E, E])
        rank = sb("c_rank", [P, TG, E])
        comb_g = sb("c_comb_g", [P, TG, E])
        comb = sb("c_comb", [P, TILES * E])
        comb_t = sb("c_comb_t", [E, HALF])
        hmf = [sb(f"c_hmf{i}", [P, HALF]) for i in range(2)]
        hmh = [sb(f"c_hmh{i}", [P, IC, HALF], F32R) for i in range(2)]
        hml = [sb(f"c_hml{i}", [P, IC, HALF], F32R) for i in range(2)]

        ps_a = pb("c_ps_a", [P, DC, HALF])
        ps_rows = ps_a[:].rearrange("p c (a d) -> p (c a) d", a=HALF // D)
        ps_logit = ps_a[:, 0, 0:TG * E].rearrange("p (t e) -> p t e", e=E)
        ps_h = pb("c_ps_h", [P, 2, HALF])
        ps_o = [pb(f"c_ps_o{i}", [P, TG, D]) for i in range(2)]

        const_loaded, w1_loaded, w2_loaded = sem("const_loaded"), sem("w1_loaded"), sem("w2_loaded")
        h0_loaded, x2_loaded = sem("h0_loaded"), sem("x2_loaded")
        att_done, att_turned = sem("att_done"), sem("att_turned")
        h_done, base_done = sem("h_done"), sem("base_done")
        stat_done, aggr_done, eps_done, rstd_done = sem("stat_done"), sem("aggr_done"), sem("eps_done"), sem("rstd_done")
        power_set, z_done, z_turned = sem("power_set"), sem("z_done"), sem("z_turned")
        h2_f, h2_h, h2_l = sem("h2_f"), sem("h2_h"), sem("h2_l")
        gate_done, route, route_exp = sem("gate_done"), sem("route"), sem("route_exp")
        comb_done, comb_turned, comb_out = sem("comb_done"), sem("comb_turned"), sem("comb_out")
        w1_hi, w1_lo, w2_hi, w2_lo = sem("w1_hi"), sem("w1_lo"), sem("w2_hi"), sem("w2_lo")
        hm_done, gelu_done, hm_hi, hm_lo = sem("hm_done"), sem("gelu_done"), sem("hm_hi"), sem("hm_lo")
        outer_done, bias_done, added = sem("outer_done"), sem("bias_done"), sem("added")
        stored = sem("stored")

        h0_g = h0_d.rearrange("(g t p) d -> g p t d", p=P, t=TG)
        x2_g = x2_d.rearrange("(g t p) d -> g p t d", p=P, t=TG)
        out_g = out.rearrange("(g t p) d -> g p t d", p=P, t=TG)
        ROUTE = 17
        EXPS = [2, 11]
        block = ctx.enter_context(nc.Block())

        @block.sync
        def _(sp):
            sp.dma_start(h0[:], h0_g[0]).then_inc(h0_loaded, 16)
            for dst, src in ((bo_sb, bo), (ident, ident_d)):
                sp.dma_start(dst[:], src).then_inc(const_loaded, 16)
            sp.dma_start(x2[:], x2_g[0]).then_inc(x2_loaded, 16)
            sp.dma_start(w1f[:], w1.rearrange("e (c p) i -> p e c i", p=P)).then_inc(w1_loaded, 16)
            for dst, src in ((lnp, ln2), (wg, w_gate.rearrange("(c p) e -> p c e", p=P)), (b1_sb, b1), (b2_sb, b2),
                             (earlier, earlier_d)):
                sp.dma_start(dst[:], src).then_inc(const_loaded, 16)
            sp.dma_start(w2f[:], w2.rearrange("e (c p) d -> p e c d", p=P)).then_inc(w2_loaded, 16)
            with sp.Fori(0, GROUPS - 1) as g:
                sp.wait_ge(h_done, g + 1)
                sp.dma_start(h0[:], h0_g[g + 1]).then_inc(h0_loaded, 16)
                sp.wait_ge(base_done, g + 1)
                sp.dma_start(x2[:], x2_g[g + 1]).then_inc(x2_loaded, 16)
                sp.wait_ge(added, g * len(ADDS) + len(ADDS))
                sp.dma_start(out_g[g], total[:, bass.ds(g * TG, TG), :]).then_inc(stored, 16)
            sp.wait_ge(added, GROUPS * len(ADDS))
            sp.dma_start(out_g[GROUPS - 1], total[:, (GROUPS - 1) * TG:GROUPS * TG, :]).then_inc(stored, 16)
            sp.wait_ge(stored, 16 * GROUPS)

        @block.gpsimd
        def _(pool):
            nc.gpsimd.memset(power[:], -0.5).then_inc(power_set, 1)
            pool.wait_ge(power_set, 1)

            def work(op, k, g):
                if op == "power":
                    pool.wait_ge(eps_done, g.count(1, 1))
                    nc.gpsimd.tensor_tensor(rstd[:], vare[:], power[:], ALU.pow).then_inc(rstd_done, 1)
                    if g.first:
                        pool.wait_ge(w2_hi, 1)
                        nc.gpsimd.tensor_tensor(w2l[:], w2f[:], w2h[:], ALU.subtract).then_inc(w2_lo, 1)
                elif op == "base":
                    pool.wait_ge(h_done, g.count(1, 1))
                    pool.wait_ge(x2_loaded, g.count(16, 16))
                    nc.gpsimd.tensor_tensor(total[:, g.cols(TG), :], x2[:], hg[:], ALU.add).then_inc(base_done, 1)
                elif op == "hm_lo":
                    e, i = k // IC, k % IC
                    pool.wait_ge(hm_hi, g.count(HM, k + 1))
                    nc.gpsimd.tensor_tensor(hml[e % 2][:, i, :], hmf[k % 2][:], hmh[e % 2][:, i, :],
                                            ALU.subtract).then_inc(hm_lo, 1)

            over_expert_groups(pool, work)

        @block.scalar
        def _(act):
            def work(op, k, g):
                if op == "att":
                    if g.first:
                        act.wait_ge(const_loaded, 16 * 7)
                    wait(act, att_turned, g.count(1, 0))
                    for d in range(DC):
                        ins = nc.scalar.activation(att[:, d, :], acc[:, d, g.cols(HALF)], ACT.Identity, bias=bo_sb[:, d:d + 1])
                    ins.then_inc(att_done, 1)
                    if g.first:
                        act.wait_ge(w1_loaded, 16)
                        nc.scalar.activation(w1h[:], w1f[:], ACT.Copy).then_inc(w1_hi, 1)
                        act.wait_ge(w2_loaded, 16)
                        nc.scalar.activation(w2h[:], w2f[:], ACT.Copy).then_inc(w2_hi, 1)
                elif op == "h2_f":
                    act.wait_ge(z_turned, g.count(1, 1))
                    wait(act, gate_done, g.count(1, 0))
                    wait(act, h2_l, g.count(1, 0))
                    for c in range(DC):
                        ins = nc.scalar.activation(h2f[:, c, :], ps_a[:, c, :], ACT.Identity, bias=lnp[:, 1, c:c + 1],
                                                   scale=lnp[:, 0, c:c + 1])
                    ins.then_inc(h2_f, 1)
                elif op == "h2_h":
                    act.wait_ge(h2_f, g.count(1, 1))
                    nc.scalar.activation(h2h[:, :, g.cols(HALF)], h2f[:], ACT.Copy).then_inc(h2_h, 1)
                elif op == "route":
                    for step, dst in zip(EXPS, (prob, rank)):
                        act.wait_ge(route, g.count(ROUTE, step))
                        nc.scalar.activation(dst[:], less[:], ACT.Exp).then_inc(route_exp, 1)
                elif op == "comb_out":
                    act.wait_ge(comb_turned, g.count(1, 1))
                    wait(act, bias_done, g.count(1, 0))
                    nc.scalar.activation(comb_t[:], ps_a[0:E, 0, :], ACT.Copy).then_inc(comb_out, 1)
                elif op == "gelu":
                    e, i = k // IC, k % IC
                    act.wait_ge(hm_done, g.count(HM, k + 1))
                    wait(act, hm_lo, g.count(HM, k - 1))
                    nc.scalar.activation(hmf[k % 2][:], ps_h[:, k % 2, :], ACT.Gelu,
                                         bias=b1_sb[:, e, i:i + 1]).then_inc(gelu_done, 1)
                elif op == "hm_hi":
                    e, i = k // IC, k % IC
                    act.wait_ge(gelu_done, g.count(HM, k + 1))
                    wait(act, outer_done, g.count(E, e - 1))
                    nc.scalar.activation(hmh[e % 2][:, i, :], hmf[k % 2][:], ACT.Copy).then_inc(hm_hi, 1)

            over_expert_groups(act, work)

        @block.vector
        def _(dve):
            def routing(g):
                steps = [0]

                def then(ins):
                    steps[0] += 1
                    ins.then_inc(route, 1)

                def after():
                    dve.wait_ge(route, g.count(ROUTE, steps[0]))

                def bc(a):
                    return a[:, :].unsqueeze(2).to_broadcast([P, TG, E])

                then(nc.vector.tensor_reduce(most[:], ps_logit, AX.X, ALU.max)), after()
                then(nc.vector.tensor_tensor(less[:], ps_logit, bc(most), ALU.subtract)), after()
                dve.wait_ge(route_exp, g.count(2, 1))
                then(nc.vector.tensor_reduce(most[:], prob[:], AX.X, ALU.add)), after()
                then(nc.vector.reciprocal(inv[:], most[:])), after()
                then(nc.vector.tensor_tensor(prob[:], prob[:], bc(inv), ALU.mult)), after()
                one = prob[:].unsqueeze(3).to_broadcast([P, TG, E, E])
                other = prob[:].unsqueeze(2).to_broadcast([P, TG, E, E])
                then(nc.vector.tensor_tensor(above[:], other, one, ALU.is_gt))
                then(nc.vector.tensor_tensor(equal[:], other, one, ALU.is_equal))
                then(nc.vector.tensor_reduce(most[:], prob[:], AX.X, ALU.max)), after()
                then(nc.vector.tensor_tensor(equal[:], equal[:], earlier[:].unsqueeze(1).to_broadcast([P, TG, E, E]),
                                             ALU.mult)), after()
                then(nc.vector.tensor_tensor(above[:], above[:], equal[:], ALU.add))
                then(nc.vector.tensor_tensor(less[:], prob[:], bc(most), ALU.subtract)), after()
                assert steps[0] == EXPS[1]
                then(nc.vector.tensor_reduce(prob[:], above[:], AX.X, ALU.add)), after()
                dve.wait_ge(route_exp, g.count(2, 2))
                then(nc.vector.scalar_tensor_tensor(out=rank[:], in0=prob[:], scalar=1.5, in1=rank[:],
                                                    op0=ALU.is_lt, op1=ALU.mult)), after()
                then(nc.vector.tensor_reduce(most[:], rank[:], AX.X, ALU.add)), after()
                then(nc.vector.reciprocal(inv[:], most[:])), after()
                wait(dve, comb_turned, g.count(1, 0))
                then(nc.vector.tensor_tensor(comb_g[:], rank[:], bc(inv), ALU.mult)), after()
                then(nc.vector.tensor_copy(comb[:, g.cols(TG * E)].rearrange("p (t e) -> p t e", e=E), comb_g[:])), after()
                assert steps[0] == ROUTE

            def work(op, k, g):
                if op == "h":
                    dve.wait_ge(h0_loaded, g.count(16, 16))
                    dve.wait_ge(att_turned, g.count(1, 1))
                    wait(dve, base_done, g.count(1, 0))
                    for r in range(2):
                        rows = slice(2 * r, 2 * r + 2)
                        ins = nc.vector.tensor_tensor(hg[:, rows, :], ps_rows[:, rows, :], h0[:, rows, :], ALU.add)
                    ins.then_inc(h_done, 1)
                elif op == "stat":
                    dve.wait_ge(h_done, g.count(1, 1))
                    for t in range(TG):
                        nc.vector.bn_stats(stats[:, t, :], hg[:, t, :]).then_inc(stat_done, 1)
                elif op == "aggr":
                    dve.wait_ge(stat_done, g.count(TG, TG))
                    nc.vector.memset(mark[:], 0.0)
                    for t in range(TG):
                        ins = nc.vector.bn_aggr(mv[:, t, :], stats[:, t, :])
                    ins.then_inc(aggr_done, 1)
                elif op == "eps":
                    dve.wait_ge(aggr_done, g.count(1, 1))
                    nc.vector.tensor_scalar(vare[:], mv[:, :, 1], EPS, None, ALU.add).then_inc(eps_done, 1)
                elif op == "norm":
                    dve.wait_ge(rstd_done, g.count(1, 1))
                    wait(dve, z_turned, g.count(1, 0))
                    for t in range(TG):
                        ins = nc.vector.tensor_scalar(zg[:, t, :], hg[:, t, :], mv[:, t, 0:1], rstd[:, t:t + 1],
                                                      ALU.subtract, ALU.mult)
                    ins.then_inc(z_done, 1)
                    if g.first:
                        dve.wait_ge(w1_hi, 1)
                        nc.vector.tensor_tensor(w1l[:], w1f[:], w1h[:], ALU.subtract).then_inc(w1_lo, 1)
                        dve.wait_ge(const_loaded, 16 * 7)
                elif op == "h2_l":
                    dve.wait_ge(h2_h, g.count(1, 1))
                    nc.vector.tensor_tensor(h2l[:, :, g.cols(HALF)], h2f[:], h2h[:, :, g.cols(HALF)],
                                            ALU.subtract).then_inc(h2_l, 1)
                elif op == "route":
                    dve.wait_ge(gate_done, g.count(1, 1))
                    routing(g)
                elif op == "add":
                    if k == E:
                        dve.wait_ge(bias_done, g.count(1, 1))
                    else:
                        dve.wait_ge(outer_done, g.count(E, k + 1))
                    dve.wait_ge(base_done, g.count(1, 1))
                    wait(dve, added, g.count(len(ADDS), ADDS.index(k)))
                    for t in range(TG):
                        to = total[:, g.cols(TG), :][:, t, :]
                        if k == E:
                            ins = nc.vector.tensor_tensor(to, ps_rows[:, t, :], to, ALU.add)
                        else:
                            one = t * E + k
                            ins = nc.vector.scalar_tensor_tensor(
                                out=to, in0=ps_o[k % 2][:, t, :], scalar=comb[:, g.cols(TG * E)][:, one:one + 1], in1=to,
                                op0=ALU.mult, op1=ALU.add)
                    ins.then_inc(added, 1)

            over_expert_groups(dve, work)

        @block.tensor
        def _(pe):
            pe.wait_ge(const_loaded, 16 * 7)

            def work(op, k, g):
                if op == "turn_att":
                    pe.wait_ge(att_done, g.count(1, 1))
                    wait(pe, added, g.count(len(ADDS), ADDS.index(E) + 1 - len(ADDS)))
                    for t in range(TG):
                        for d in range(DC):
                            ins = nc.tensor.transpose(ps_rows[:, t, d * P:(d + 1) * P], att[:, d, t * P:(t + 1) * P], ident[:])
                    ins.then_inc(att_turned, 1)
                elif op == "turn_z":
                    pe.wait_ge(z_done, g.count(1, 1))
                    for t in range(TG):
                        for c in range(DC):
                            ins = nc.tensor.transpose(ps_a[:, c, t * P:(t + 1) * P], zg[:, t, c * P:(c + 1) * P], ident[:])
                    ins.then_inc(z_turned, 1)
                elif op == "gate":
                    pe.wait_ge(h2_f, g.count(1, 1))
                    for t in range(TG):
                        for c in range(DC):
                            ins = nc.tensor.matmul(ps_a[:, 0, t * E:(t + 1) * E], h2f[:, c, t * P:(t + 1) * P], wg[:, c, :],
                                                   start=(c == 0), stop=(c == DC - 1))
                    ins.then_inc(gate_done, 1)
                elif op == "turn_comb":
                    pe.wait_ge(route, g.count(ROUTE, ROUTE))
                    for t in range(TG):
                        ins = nc.tensor.transpose(ps_a[0:E, 0, t * P:(t + 1) * P], comb_g[:, t, :], ident[:])
                    ins.then_inc(comb_turned, 1)
                elif op == "bias":
                    pe.wait_ge(comb_out, g.count(1, 1))
                    for t in range(TG):
                        ins = nc.tensor.matmul(ps_rows[:, t, :], comb_t[:, t * P:(t + 1) * P], b2_sb[:], start=True, stop=True)
                    ins.then_inc(bias_done, 1)
                elif op == "inner":
                    e, i = k // IC, k % IC
                    if g.first and k == 0:
                        pe.wait_ge(w1_lo, 1)
                    if k == 0:
                        pe.wait_ge(h2_l, g.count(1, 1))
                    wait(pe, gelu_done, g.count(HM, k - 1))
                    for q, (w, r) in enumerate(((w1h, h2h), (w1h, h2l), (w1l, h2h))):
                        for c in range(DC):
                            ins = nc.tensor.matmul(ps_h[:, k % 2, :], w[:, e, c, i * P:(i + 1) * P], r[:, c, g.cols(HALF)],
                                                   start=(q + c == 0), stop=(q == 2 and c == DC - 1))
                    ins.then_inc(hm_done, 1)
                elif op == "outer":
                    if g.first and k == 0:
                        pe.wait_ge(w2_lo, 1)
                    pe.wait_ge(hm_lo, g.count(HM, (k + 1) * IC))
                    if k >= 2:
                        pe.wait_ge(added, g.count(len(ADDS), ADDS.index(k - 2) + 1))
                    else:
                        wait(pe, added, g.count(len(ADDS), ADDS.index(k + 2) + 1 - len(ADDS)))
                    for t in range(TG):
                        for q, (l, w) in enumerate(((hmh, w2h), (hmh, w2l), (hml, w2h))):
                            for i in range(IC):
                                ins = nc.tensor.matmul(ps_o[k % 2][:, t, :], l[k % 2][:, i, t * P:(t + 1) * P],
                                                       w[:, k, i, :], start=(q + i == 0), stop=(q == 2 and i == IC - 1))
                    ins.then_inc(outer_done, 1)

            over_expert_groups(pe, work)


def layer(nc, t, x2_d, h0_d, out):
    with ExitStack() as ctx:
        acc = ctx.enter_context(nc.sbuf_tensor("acc", [P, DC, TOK], F32))
        with ExitStack() as held:
            h1f = held.enter_context(nc.sbuf_tensor("h1f", [P, DC, TOK], F32))
            h1h = held.enter_context(nc.sbuf_tensor("h1h", [P, DC, TOK], F32R))
            h1l = held.enter_context(nc.sbuf_tensor("h1l", [P, DC, TOK], F32R))
            conv_layer(nc, t["x"], t["w_in_t"], t["w_out_t"], t["conv_par"], t["ln1"], t["ident"], x2_d, h0_d, h1h, h1l, h1f)
            attention(nc, t["w_qk"], t["w_v"], t["w_ov"], t["rope"], t["ident"], t["identb"], t["mask"], h1h, h1l, h1f, acc)
        experts(nc, t["ln2"], t["w_gate"], t["w1"], t["b1"], t["w2"], t["b2"], t["bo"], t["earlier"], t["ident"], x2_d, h0_d, acc, out)


def kernel(**inputs):
    import ml_dtypes
    import numpy as np
    import concourse.bacc as bacc
    from concourse.bass_utils import run_bass_kernel_spmd as run

    a = {k[3:]: np.asarray(v) for k, v in inputs.items()}

    def per_partition(v, chunks):
        return v.reshape(chunks, P).T

    def head_cols(w, h):
        return w[:, h * HD:(h + 1) * HD].reshape(DC, P, HD).transpose(1, 0, 2).reshape(P, DC * HD)

    heads = range(HEADS)
    q_b, k_b, v_b = (per_partition(a[f"ffn_b{n}"], HEADS) for n in "qkv")
    w_qk = np.stack([np.concatenate([head_cols(a["ffn_wq"], h), head_cols(a["ffn_wk"], h), q_b[:, h:h + 1],
                                     k_b[:, h:h + 1]], 1) for h in heads])
    w_v = np.stack([head_cols(a["ffn_wv"], h) for h in heads])
    w_ov = np.stack([np.concatenate([a["ffn_wo"][h * HD:(h + 1) * HD], v_b[:, h:h + 1]], 1) for h in heads])
    par = np.stack([a["attn_conv_w"][:, 0, j] for j in range(TAPS)] + [a["attn_conv_b"], a["attn_D"]], 1)
    freq = (1.0 / np.power(np.float32(10000.0), np.arange(0, HD, 2, dtype=np.float32) / np.float32(HD))).astype(np.float32)
    angle = (np.arange(SEQ, dtype=np.float32)[:, None] * freq[None]).astype(np.float32).T
    cos, sin = np.cos(angle), np.sin(angle)
    rope = np.stack([np.concatenate([cos, cos]), np.concatenate([-sin, sin])], 1).astype(np.float32)
    mask = np.where(np.arange(2 * P)[None] <= np.arange(P)[:, None], 0.0, BIG)
    t = {
        "x": a["attn_x"].reshape(TOK, D),
        "w_in_t": a["attn_w_in"].T,
        "w_out_t": a["attn_w_out"].T,
        "conv_par": par.reshape(IB, P, TAPS + 2).transpose(1, 0, 2),
        "ln1": np.stack([per_partition(a["ffn_ln1_w"], DC), per_partition(a["ffn_ln1_b"], DC)], 1),
        "ln2": np.stack([per_partition(a["ffn_ln2_w"], DC), per_partition(a["ffn_ln2_b"], DC)], 1),
        "w_qk": w_qk, "w_v": w_v, "w_ov": w_ov, "rope": rope,
        "ident": np.eye(P, dtype=np.float32),
        "identb": np.eye(P).astype(ml_dtypes.bfloat16),
        "mask": mask.astype(ml_dtypes.bfloat16),
        "w_gate": a["ffn_w_gate"],
        "w1": a["ffn_we1"],
        "b1": a["ffn_be1"].reshape(EXPERTS, IC, P).transpose(2, 0, 1),
        "w2": a["ffn_we2"],
        "b2": a["ffn_be2"],
        "bo": per_partition(a["ffn_bo"], DC),
        "earlier": np.broadcast_to(np.tri(EXPERTS, k=-1, dtype=np.float32), (P, EXPERTS, EXPERTS)),
    }
    nc = bacc.Bacc("TRN2", target_bir_lowering=False, num_devices=1)
    arrays, aps = {}, {}
    for name, v in t.items():
        v = np.ascontiguousarray(v)
        arrays[name + "_dram"] = v
        aps[name] = nc.dram_tensor(name + "_dram", v.shape, mybir.dt.from_np(v.dtype), kind="ExternalInput").ap()
    x2_d = nc.dram_tensor("x2_scratch", (TOK, D), F32, kind="Internal").ap()
    h0_d = nc.dram_tensor("h0_scratch", (TOK, D), F32, kind="Internal").ap()
    out = nc.dram_tensor("out_dram", (TOK, D), F32, kind="ExternalOutput").ap()
    layer(nc, aps, x2_d, h0_d, out)
    r = run(nc, [arrays], core_ids=[0])
    return r.results[0]["out_dram"].reshape(BATCH, SEQ, D)
```

```python
from contextlib import ExitStack

import concourse.bass as bass
from concourse import mybir

F32 = mybir.dt.float32
F32R = mybir.dt.float32r
ALU = mybir.AluOpType
ACT = mybir.ActivationFunctionType
AX = mybir.AxisListType

P = 128
BATCH, SEQ, D = 2, 1024, 256
TOK = BATCH * SEQ
DC = D // P
DI = 512
IB = DI // P
TAPS = 4
HEADS, HD = 16, 128
EXPERTS, EI = 4, 256
IC = EI // P
HALF = SEQ // 2
TG = HALF // P
GROUPS = TOK // HALF
QB = SEQ // P
SCALE = float(HD) ** -0.5
EPS = 1e-5
BIG = -1e30

WQK = 4 * P + 2
WOV = D + 1


def scores_width(i):
    return max(256, (i + 1) * P)


def score_banks(i):
    return 1 if scores_width(i) <= 512 else 2


def spread(buf, i):
    nb = score_banks(i)
    return buf[:, 0:nb, 0:(i + 1) * P // nb]


def diagonal(buf, i):
    nb = score_banks(i)
    w = (i + 1) * P // nb
    return buf[:, nb - 1, w - P:w]


def packed(buf, i):
    return buf[:, 0:(i + 1) * P].rearrange("p (a n) -> p a n", a=score_banks(i))


CHUNKS = [(i, j, min(4, i + 1 - j)) for i in range(QB) for j in range(0, i + 1, 4)]
NCH = len(CHUNKS)
FIRST_CHUNK = [min(c for c in range(NCH) if CHUNKS[c][0] == i) for i in range(QB)]
LAST_CHUNK = [max(c for c in range(NCH) if CHUNKS[c][0] == i) for i in range(QB)]
CHUNKS_TO_HALF = [LAST_CHUNK[3] + 1, NCH]

PERIOD = 64
AT = {
    "S": [2.5, 4.6, 12.2, 18.5, 25.2, 37.7, 39.1, 57.8],
    "T": [23.6, 23.7, 46.9, 51.3, 55.3, 64.4, 75.2, 78],
    "Q": [13.4, 20.2, 34.4, 42.9],
    "V": [52.9, 67.1],
    "O": [64.5, 88.4, 96.3],
    "W": [67.3, 76.9, 119.4, 125.8],
    "split_qk": [6.5],
    "split_o": [63.2],
}
LAG = {
    "S": {
        "masked": [0, 5.7, 8.3, 10.5, 11.1, 8.5, 11, 1.5],
        "max": [2.7, 6.5, 10.6, 13, 14, 11.5, 15.1, 1.5],
        "exp": [5.8, 9.3, 20.6, 17.3, 14.2, 8.6, 23.8, 10.3],
        "recip": [8.5, 8.3, 21, 24.6, 21.8, 14.1, 22.1, 13],
        "norm": [11.9, 16.2, 26.2, 32.8, 27.9, 18.6, 32.3, 13.9],
    },
    "T": {
        "p_hi": [4.1, 17.6, 1, 2.2, 3.4, 0.3, 0, 6.5],
        "p_lo": [18, 24.3, 5.1, 0.9, 3.4, 0.9, 0.7, 5],
    },
    "Q": {
        "q_cos": [2.5, 6.1, 8.4, 8.7],
        "q_swap": [7.2, 13.2, 8.8, 12.7],
        "q_sin": [10.5, 16.1, 23.3, 15.9],
        "q_rope": [17.7, 18.6, 23.7, 22.1],
        "q_hi": [25, 25.5, 36.2, 44.5],
        "q_lo": [29.4, 29.9, 37.2, 44.6],
    },
    "V": {
        "v_hi": [4.6, 7.6],
        "v_lo": [4.3, 6.6],
    },
    "O": {
        "o_hi": [5.5, 0, 9.8],
        "o_lo": [2.2, 0, 12.4],
    },
    "W": {
        "acc": [7.4, 0.8, 2.7, 0.6],
    },
}
O_PIECES = [0, 1, 1]


def unit_order():
    placed = []
    for op, at in AT.items():
        for k, x in enumerate(at):
            parts = [(op, k)] if op != "T" else [("C", c) for c in range(FIRST_CHUNK[k], LAST_CHUNK[k] + 1)]
            for part, i in parts:
                placed.append((x, part, i))
                if (op, k) != ("O", 1):
                    placed += [(x + lag[k], what, O_PIECES[k] if op == "O" else i) for what, lag in LAG.get(op, {}).items()]
    order = sorted(range(len(placed)), key=lambda n: (placed[n][0] % PERIOD, n))
    return [(placed[n][1], placed[n][2], int(placed[n][0] // PERIOD)) for n in order]


UNIT = unit_order()
UNITS = HEADS * BATCH
MISC = [(op, k) for op, k, _ in UNIT if op in ("V", "Q", "W", "O") and (op, k) != ("O", 2)]
MISC_AGE = {(op, k): age for op, k, age in UNIT}


def bank_of(op, k):
    return MISC.index((op, k)) % 2


class Unit:

    def __init__(self, n, off):
        self.n, self.off, self.b = n, off, off % BATCH

    def count(self, each, k):
        return self.n * (2 * each) + (self.off * each + k)

    def head(self, more=0):
        return self.n + (self.off + more) // BATCH


def over_units(eng, work):
    def slots(n, off):
        for op, k, age in UNIT:
            last = off - age == UNITS - 1 and isinstance(n, int)
            if off < age and isinstance(n, int) or off == UNITS and not age:
                continue
            if last and (op[0] in "Qq" or op == "split_qk"):
                continue
            if op == "split_o" and (off - age) % 2 or op == "split_qk" and (off - age) % 2 == 0:
                continue
            work(op, k, Unit(n, off - age))

    slots(0, 0)
    slots(0, 1)
    with eng.Fori(0, (UNITS - 4) // 2) as n:
        slots(n, 2)
        slots(n, 3)
    slots(0, UNITS - 2)
    slots(0, UNITS - 1)
    slots(0, UNITS)


def wait(eng, sem, value):
    if not isinstance(value, int) or value > 0:
        eng.wait_ge(sem, value)


CONV_PERIOD = 21.5
CONV_AT = {
    "stat": [-10, 36, 37.5],
    "aggr": [-1.5, 36, 37.5],
    "eps": [-1.5, 36.5, 38.5],
    "power": [-9.3, 28.2, 31.2],
    "norm": [1, 37, 41.5],
    "turn": [4, 40.5],
    "x_hi": [5],
    "x_lo": [5],
    "in": [6.5, 6.8, 11, 12.3, 14.5, 14.8, 17, 20.8],
    "rows": [7.3, 13.8, 15.8, 22.3],
    "tap3": [8.8, 15.3, 20.3, 22.8],
    "tap0": [7.6, 15.1, 18.6, 24.1],
    "tap1": [7.9, 16.4, 21.4, 24.9],
    "tap2": [8.7, 19.7, 22.2, 25.7],
    "gate": [10.6, 18.6, 20.1, 26.1],
    "silu": [13.5, 22, 24, 27.5],
    "gated": [12.8, 23.3, 24.8, 27.3],
    "h_hi": [14.1, 26.1, 27.1, 28.1],
    "h_lo": [10.8, 18.3, 20.3, 25.3],
    "out": [29.1, 30.2],
    "x2": [30.7, 35.3],
    "h1_f": [46.5],
    "h1_h": [54],
    "h1_l": [50],
}
FIRST_QK_AT = {
    "split_qk": [74.5],
    "q": [85.5, 90.1, 106.5, 114.6],
    "q_cos": [92, 99.5, 112, 130.5],
    "q_swap": [105.5, 108, 125.5, 129.5],
    "q_sin": [91.5, 100.5, 115, 123.5],
    "q_rope": [93, 112, 118.5, 135],
    "q_hi": [109.5, 114.5, 136.5, 156.5],
    "q_lo": [111.5, 120.5, 132, 138.5],
}
CONV_ORDER = [(op, k, g) for _, op, k, g in sorted(
    [(x + CONV_PERIOD * g, op, k, g) for op, at in CONV_AT.items() for k, x in enumerate(at) for g in range(GROUPS)]
    + [(x, op, k, 0) for op, at in FIRST_QK_AT.items() for k, x in enumerate(at)], key=lambda o: o[0])]
TURNS = [(op, k, g) for op, k, g in CONV_ORDER if op in ("turn", "q")]


def conv_layer(nc, sh, x, w_in_t, w_out_t, conv_par, ln1, x2_d, h0_d, h1h, h1l, h1f, acc):
    with ExitStack() as ctx:
        def sb(name, shape, dt=F32):
            return ctx.enter_context(nc.sbuf_tensor(name, shape, dt))

        def pb(name, shape, dt=F32):
            return ctx.enter_context(nc.psum_tensor(name, shape, dt))

        def sem(name):
            return ctx.enter_context(nc.semaphore("a_" + name))

        par = sb("a_par", [P, IB, TAPS + 2])
        lnp = sb("a_lnp", [P, 2, DC])
        wi = sb("wi", [P, DC, 2 * DI])
        qk = sh.qk
        qk.rot, qk.swp = (wi[:, c, :].rearrange("p (a n) -> p a n", a=2) for c in range(2))
        wih = sb("wih", [P, DC, 2 * DI], F32R)
        wil = sb("wil", [P, DC, 2 * DI], F32R)
        wo = sb("wo", [P, IB, D])
        woh = sb("woh", [P, IB, D], F32R)
        wol = sb("wol", [P, IB, D], F32R)
        xs = [acc[:, g // 2, (g % 2) * TG * D:(g % 2 + 1) * TG * D].rearrange("p (t d) -> p t d", t=TG)
              for g in range(GROUPS)]
        xn = sb("xn", [P, TG, D])
        xth = sb("xth", [P, DC, HALF], F32R)
        xtl = sb("xtl", [P, DC, HALF], F32R)
        xi = sb("xi", [P, IB, TAPS - 1 + SEQ])
        sg = sb("sg", [P, 2, HALF])
        cv = sb("cv", [P, 3, HALF])
        sx = sb("sx", [P, 2, HALF])
        hh = sb("hh", [P, IB, HALF], F32R)
        hl = sb("hl", [P, IB, HALF], F32R)
        h0 = sb("h0", [P, TG, D])
        zn = sb("zn", [P, TG, D])
        stats = [sb(f"a_stats{w}", [P, TG, 6]) for w in range(3)]
        mv = [sb(f"a_mv{w}", [P, TG, 2]) for w in range(3)]
        vare = [sb(f"a_vare{w}", [P, TG]) for w in range(3)]
        rstd = [sb(f"a_rstd{w}", [P, TG]) for w in range(3)]
        mark = sb("a_mark", [P, 1])
        power = sb("a_power", [P, TG])

        ps_t = pb("a_ps_t", [P, DC, HALF])
        ps_in = pb("a_ps_in", [P, 4, HALF])
        ps_out = pb("a_ps_out", [P, TG // 2, 2, D])

        wi_loaded, const_loaded, wo_loaded = sem("wi_loaded"), sem("const_loaded"), sem("wo_loaded")
        wi_hi, wi_lo, wo_hi, wo_lo = sem("wi_hi"), sem("wi_lo"), sem("wo_hi"), sem("wo_lo")
        halo_zero, power_set = sem("halo_zero"), sem("power_set")
        x_loaded = [sem(f"x_loaded{g}") for g in range(GROUPS)]
        x2_stored, h0_stored = sem("x2_stored"), sem("h0_stored")
        stat_done = [sem(f"stat_done{w}") for w in range(3)]
        aggr_done = [sem(f"aggr_done{w}") for w in range(3)]
        eps_done = [sem(f"eps_done{w}") for w in range(3)]
        rstd_done = [sem(f"rstd_done{w}") for w in range(3)]
        norm_done = [sem(f"norm_done{w}") for w in range(3)]
        turned = [sem(f"turned{k}") for k in range(2)]
        x_hi, x_lo = sem("x_hi"), sem("x_lo")
        in_done = sem("in_done")
        rows_out = sem("rows_out")
        gate_out = sem("gate_out")
        tap_done = [sem(f"tap_done{j}") for j in range(TAPS)]
        silu_done, gated, h_hi, h_lo = sem("silu_done"), sem("gated"), sem("h_hi"), sem("h_lo")
        out_done, x2_done = sem("out_done"), sem("x2_done")
        h1_f, h1_h, h1_l = sem("h1_f"), sem("h1_h"), sem("h1_l")

        x_g = x.rearrange("(g t p) d -> g p t d", p=P, t=TG)
        x2_g = x2_d.rearrange("(g t p) d -> g p t d", p=P, t=TG)
        h0_g = h0_d.rearrange("(g t p) d -> g p t d", p=P, t=TG)
        block = ctx.enter_context(nc.Block())

        @block.sync
        def _(sp):
            sp.dma_start(xs[0], x_g[0]).then_inc(x_loaded[0], 16)
            sp.dma_start(wi[:], w_in_t.rearrange("(c p) n -> p c n", p=P)).then_inc(wi_loaded, 16)
            sp.dma_start(sh.ident[:], sh.ident_d).then_inc(sh.ident_loaded, 16)
            sp.dma_start(par[:], conv_par).then_inc(const_loaded, 16)
            sp.dma_start(lnp[:], ln1).then_inc(const_loaded, 16)
            sp.dma_start(xs[1], x_g[1]).then_inc(x_loaded[1], 16)
            sp.dma_start(wo[:], w_out_t.rearrange("(c p) n -> p c n", p=P)).then_inc(wo_loaded, 16)
            for g in range(2, GROUPS):
                sp.dma_start(xs[g], x_g[g]).then_inc(x_loaded[g], 16)
            sp.dma_start(qk.wqk[:], qk.w_qk[0]).then_inc(qk.qk_loaded, 16)
            sp.dma_start(qk.cos_sin[:], qk.rope).then_inc(sh.tables_loaded, 16)
            sp.dma_start(sh.mask[:], sh.mask_d).then_inc(sh.tables_loaded, 16)
            sp.dma_start(sh.wv[:], sh.w_v[0].rearrange("p (c n) -> p c n", c=DC)).then_inc(sh.v_loaded, 16)
            sp.dma_start(sh.wov[:], sh.w_ov[0]).then_inc(sh.ov_loaded, 16)
            for dst, src in sh.expert_constants:
                sp.dma_start(dst[:], src).then_inc(sh.expert_loaded, 16)
            for g in range(GROUPS):
                sp.wait_ge(x2_done, 2 * g + 2)
                sp.dma_start(x2_g[g], xs[g]).then_inc(x2_stored, 16)
                sp.wait_ge(norm_done[1], g + 1)
                sp.dma_start(h0_g[g], h0[:]).then_inc(h0_stored, 16)
            sp.wait_ge(x2_stored, 16 * GROUPS)
            sp.wait_ge(h0_stored, 16 * GROUPS)

        @block.gpsimd
        def _(pool):
            nc.gpsimd.memset(power[:], -0.5).then_inc(power_set, 1)
            nc.gpsimd.memset(xi[:, :, 0:TAPS - 1], 0.0).then_inc(halo_zero, 1)
            pool.wait_ge(power_set, 1)
            for op, k, g in CONV_ORDER:
                if op == "power":
                    pool.wait_ge(eps_done[k], g + 1)
                    nc.gpsimd.tensor_tensor(rstd[k][:], vare[k][:], power[:], ALU.pow).then_inc(rstd_done[k], 1)
                    if (k, g) == (0, 0):
                        pool.wait_ge(wo_hi, 1)
                        nc.gpsimd.tensor_tensor(wol[:], wo[:], woh[:], ALU.subtract).then_inc(wo_lo, 1)
                elif op == "h_lo":
                    i = IB * g + k
                    pool.wait_ge(h_hi, i + 1)
                    nc.gpsimd.tensor_tensor(hl[:, k, :], cv[:, i % 3, :], hh[:, k, :], ALU.subtract).then_inc(h_lo, 1)
                elif op == "q_sin":
                    if k == 0:
                        pool.wait_ge(sh.tables_loaded, 16 * 2)
                    qk.times_sin(pool, k, k + 1)
                elif op == "q_rope":
                    qk.rotate(pool, k, k + 1)
                elif op == "h1_l":
                    cols = slice(g * HALF, (g + 1) * HALF)
                    pool.wait_ge(h1_h, g + 1)
                    nc.gpsimd.tensor_tensor(h1l[:, :, cols], h1f[:, :, cols], h1h[:, :, cols],
                                            ALU.subtract).then_inc(h1_l, 1)

        @block.scalar
        def _(act):
            act.wait_ge(wi_loaded, 16)
            nc.scalar.activation(wih[:], wi[:], ACT.Copy).then_inc(wi_hi, 1)
            for op, k, g in CONV_ORDER:
                i = IB * g + k
                if op == "x_hi":
                    act.wait_ge(turned[0], g + 1)
                    if g > 0:
                        act.wait_ge(in_done, 2 * IB * g)
                    nc.scalar.activation(xth[:], ps_t[:], ACT.Copy).then_inc(x_hi, 1)
                    if g == 0:
                        act.wait_ge(wo_loaded, 16)
                        nc.scalar.activation(woh[:], wo[:], ACT.Copy).then_inc(wo_hi, 1)
                        act.wait_ge(const_loaded, 32)
                elif op == "rows":
                    act.wait_ge(in_done, 2 * i + 1)
                    lo = TAPS - 1 + (g % 2) * HALF
                    if g >= 2 and g % 2 == 0:
                        act.wait_ge(tap_done[2], i - IB + 1)
                    nc.scalar.activation(xi[:, k, lo:lo + HALF], ps_in[:, 2 * (i % 2), :], ACT.Copy).then_inc(rows_out, 1)
                elif op == "tap3":
                    act.wait_ge(in_done, 2 * i + 1)
                    if i >= 3:
                        act.wait_ge(h_lo, i - 2)
                    nc.scalar.activation(cv[:, i % 3, :], ps_in[:, 2 * (i % 2), :], ACT.Identity,
                                         bias=par[:, k, TAPS:TAPS + 1],
                                         scale=par[:, k, TAPS - 1:TAPS]).then_inc(tap_done[3], 1)
                elif op == "gate":
                    act.wait_ge(in_done, 2 * i + 2)
                    if i >= 2:
                        act.wait_ge(gated, i - 1)
                    nc.scalar.activation(sg[:, i % 2, :], ps_in[:, 2 * (i % 2) + 1, :], ACT.Silu).then_inc(gate_out, 1)
                elif op == "silu":
                    act.wait_ge(tap_done[2], i + 1)
                    if i >= 2:
                        act.wait_ge(gated, i - 1)
                    nc.scalar.activation(sx[:, i % 2, :], cv[:, i % 3, :], ACT.Silu).then_inc(silu_done, 1)
                elif op == "h_hi":
                    act.wait_ge(gated, i + 1)
                    if g > 0:
                        act.wait_ge(out_done, 2 * g)
                    nc.scalar.activation(hh[:, k, :], cv[:, i % 3, :], ACT.Copy).then_inc(h_hi, 1)
                elif op == "h1_f":
                    act.wait_ge(turned[1], g + 1)
                    for c in range(DC):
                        ins = nc.scalar.activation(h1f[:, c, g * HALF:(g + 1) * HALF], ps_t[:, c, :],
                                                   ACT.Identity, bias=lnp[:, 1, c:c + 1], scale=lnp[:, 0, c:c + 1])
                    ins.then_inc(h1_f, 1)
                elif op == "split_qk":
                    qk.split_high(act, 16)
                elif op == "q_swap":
                    act.wait_ge(wi_lo, 1)
                    qk.swap(act, k, k + 1, ps_t[:, k % 2, :])
                elif op == "q_hi":
                    qk.high(act, k, k + 1, qk.first_h)
                elif op == "h1_h":
                    act.wait_ge(h1_f, g + 1)
                    cols = slice(g * HALF, (g + 1) * HALF)
                    nc.scalar.activation(h1h[:, :, cols], h1f[:, :, cols], ACT.Copy).then_inc(h1_h, 1)

        @block.vector
        def _(dve):
            for op, k, g in CONV_ORDER:
                i = IB * g + k
                if op == "stat":
                    src = (xs[g], xs[g], h0)[k]
                    if k == 0:
                        dve.wait_ge(x_loaded[g], 16)
                    elif k == 1:
                        dve.wait_ge(x2_done, 2 * g + 2)
                    else:
                        dve.wait_ge(norm_done[1], g + 1)
                    for t in range(TG):
                        nc.vector.bn_stats(stats[k][:, t, :], src[:, t, :]).then_inc(stat_done[k], 1)
                elif op == "aggr":
                    dve.wait_ge(stat_done[k], TG * g + TG)
                    nc.vector.memset(mark[:], 0.0)
                    for t in range(TG):
                        ins = nc.vector.bn_aggr(mv[k][:, t, :], stats[k][:, t, :])
                    ins.then_inc(aggr_done[k], 1)
                elif op == "eps":
                    dve.wait_ge(aggr_done[k], g + 1)
                    nc.vector.tensor_scalar(vare[k][:], mv[k][:, :, 1], EPS, None, ALU.add).then_inc(eps_done[k], 1)
                elif op == "norm":
                    src, dst = ((xs[g], xn), (xs[g], h0), (h0, zn))[k]
                    dve.wait_ge(rstd_done[k], g + 1)
                    if g > 0:
                        if k == 1:
                            dve.wait_ge(h0_stored, 16 * g)
                        else:
                            dve.wait_ge(turned[k // 2], g)
                    for t in range(TG):
                        ins = nc.vector.tensor_scalar(dst[:, t, :], src[:, t, :], mv[k][:, t, 0:1], rstd[k][:, t:t + 1],
                                                      ALU.subtract, ALU.mult)
                    ins.then_inc(norm_done[k], 1)
                    if (k, g) == (0, 0):
                        dve.wait_ge(wi_hi, 1)
                        nc.vector.tensor_tensor(wil[:], wi[:], wih[:], ALU.subtract).then_inc(wi_lo, 1)
                        dve.wait_ge(halo_zero, 1)
                        dve.wait_ge(const_loaded, 32)
                elif op == "x_lo":
                    dve.wait_ge(x_hi, g + 1)
                    nc.vector.tensor_tensor(xtl[:], ps_t[:], xth[:], ALU.subtract).then_inc(x_lo, 1)
                elif op in ("tap0", "tap1", "tap2"):
                    j = int(op[3])
                    dve.wait_ge(rows_out, i + 1)
                    dve.wait_ge(tap_done[j - 1 if j else 3], i + 1)
                    lo = (g % 2) * HALF + j
                    nc.vector.scalar_tensor_tensor(out=cv[:, i % 3, :], in0=xi[:, k, lo:lo + HALF], scalar=par[:, k, j:j + 1],
                                                   in1=cv[:, i % 3, :], op0=ALU.mult, op1=ALU.add).then_inc(tap_done[j], 1)
                elif op == "gated":
                    dve.wait_ge(silu_done, i + 1)
                    dve.wait_ge(gate_out, i + 1)
                    nc.vector.scalar_tensor_tensor(out=cv[:, i % 3, :], in0=sx[:, i % 2, :],
                                                   scalar=par[:, k, TAPS + 1:TAPS + 2], in1=sg[:, i % 2, :],
                                                   op0=ALU.mult, op1=ALU.mult).then_inc(gated, 1)
                elif op == "split_qk":
                    qk.split_low(dve, 1)
                elif op == "q_cos":
                    if k == 0:
                        dve.wait_ge(wi_lo, 1)
                        dve.wait_ge(qk.wqk_lo, 1)
                        dve.wait_ge(sh.tables_loaded, 16 * 2)
                    wait(dve, qk.q_lo, k - 1)
                    qk.times_cos(dve, k, k + 1, ps_t[:, k % 2, :])
                elif op == "q_lo":
                    qk.low(dve, k, k + 1, qk.first_h, qk.first_l)
                elif op == "x2":
                    dve.wait_ge(out_done, 2 * g + k + 1)
                    rows = xs[g][:, 2 * k:2 * k + 2, :]
                    nc.vector.tensor_tensor(rows, ps_out[:, k], rows, ALU.add).then_inc(x2_done, 1)

        @block.tensor
        def _(pe):
            pe.wait_ge(sh.ident_loaded, 16)
            for op, k, g in CONV_ORDER:
                if op in ("turn", "q"):
                    n = TURNS.index((op, k, g))
                    turns = [(i, of) for what, i, of in TURNS[:n] if what == "turn"]
                    if turns:
                        before, of = turns[-1]
                        pe.wait_ge((x_lo, h1_f)[before], of + 1)
                    pieces = n - len(turns) - (op == "q" and k % 2)
                    wait(pe, qk.q_swap, pieces)
                if op == "q":
                    if k == 0:
                        pe.wait_ge(qk.wqk_lo, 1)
                    pe.wait_ge(h1_l, k // 2 + 1)
                    qk.project(k, 0, ps_t[:, k % 2, :], h1h, h1l)
                elif op == "turn":
                    pe.wait_ge(norm_done[2 * k], g + 1)
                    src = (xn, zn)[k]
                    for t in range(TG):
                        for c in range(DC):
                            ins = nc.tensor.transpose(ps_t[:, c, t * P:(t + 1) * P], src[:, t, c * P:(c + 1) * P], sh.ident[:])
                    ins.then_inc(turned[k], 1)
                elif op == "in":
                    i = 2 * IB * g + k
                    n = (k // 2) * P + (k % 2) * DI
                    if i >= 4:
                        if k % 2 == 0:
                            pe.wait_ge(rows_out, i // 2 - 1)
                            pe.wait_ge(tap_done[3], i // 2 - 1)
                        else:
                            pe.wait_ge(gate_out, i // 2 - 1)
                    if k == 0:
                        pe.wait_ge(x_hi, g + 1)
                    if i == 0:
                        pe.wait_ge(wi_hi, 1)
                    for q, (w, r) in enumerate(((wih, xth), (wih, xtl), (wil, xth))):
                        if k == 0 and q == 1:
                            pe.wait_ge(x_lo, g + 1)
                        if i == 0 and q == 2:
                            pe.wait_ge(wi_lo, 1)
                        for c in range(DC):
                            ins = nc.tensor.matmul(ps_in[:, i % 4, :], w[:, c, n:n + P], r[:, c, :],
                                                   start=(q + c == 0), stop=(q == 2 and c == DC - 1))
                    ins.then_inc(in_done, 1)
                elif op == "out":
                    pe.wait_ge(h_lo, IB * (g + 1))
                    if g > 0:
                        pe.wait_ge(x2_done, 2 * (g - 1) + k + 1)
                    else:
                        pe.wait_ge(wo_lo, 1)
                    for t in range(2 * k, 2 * k + 2):
                        for q, (l, w) in enumerate(((hh, woh), (hh, wol), (hl, woh))):
                            for m in range(IB):
                                ins = nc.tensor.matmul(ps_out[:, k, t % 2, :], l[:, m, t * P:(t + 1) * P], w[:, m, :],
                                                       start=(q + m == 0), stop=(q == 2 and m == IB - 1))
                    ins.then_inc(out_done, 1)


class QueriesKeys:

    def __init__(self, nc, ctx, t):
        def sb(name, shape, dt=F32):
            return ctx.enter_context(nc.sbuf_tensor(name, shape, dt))

        def sem(name):
            return ctx.enter_context(nc.semaphore(name))

        self.nc = nc
        self.cos_sin, self.rope = sb("cos_sin", [P, 2, SEQ]), t["rope"]
        self.wqk, self.w_qk, self.qk_loaded = sb("wqk", [P, WQK]), t["w_qk"], sem("qk_loaded")
        self.wqkh = sb("wqkh", [P, 4, P], F32R)
        self.wqkl = sb("wqkl", [P, 4, P], F32R)
        self.bqk = sb("bqk", [P, 2])
        self.first_h = sb("qkh0", [P, 2, SEQ], F32R)
        self.first_l = sb("qkl0", [P, 2, SEQ], F32R)
        self.rot = self.swp = None
        self.wqk_hi, self.wqk_lo = sem("wqk_hi"), sem("wqk_lo")
        self.q_done, self.q_cos, self.q_swap, self.q_sin = sem("q_done"), sem("q_cos"), sem("q_swap"), sem("q_sin")
        self.q_rope, self.q_hi, self.q_lo = sem("q_rope"), sem("q_hi"), sem("q_lo")

    @staticmethod
    def piece(k):
        return k % 2, k // 2

    def split_high(self, act, loaded):
        nc, wqk, wqkh = self.nc, self.wqk, self.wqkh
        act.wait_ge(self.qk_loaded, loaded)
        nc.scalar.activation(wqkh[:, 0:2, :], wqk[:, 0:2 * P].rearrange("p (c n) -> p c n", c=2), ACT.Copy, scale=SCALE)
        nc.scalar.activation(wqkh[:, 2:4, :], wqk[:, 2 * P:4 * P].rearrange("p (c n) -> p c n", c=2),
                             ACT.Copy).then_inc(self.wqk_hi, 1)

    def split_low(self, dve, n):
        nc, wqk, wqkh, wqkl, bqk = self.nc, self.wqk, self.wqkh, self.wqkl, self.bqk
        dve.wait_ge(self.wqk_hi, n)
        nc.vector.scalar_tensor_tensor(out=wqkl[:, 0:2, :], in0=wqk[:, 0:2 * P].rearrange("p (c n) -> p c n", c=2),
                                       scalar=SCALE, in1=wqkh[:, 0:2, :], op0=ALU.mult, op1=ALU.subtract)
        nc.vector.tensor_tensor(wqkl[:, 2:4, :], wqk[:, 2 * P:4 * P].rearrange("p (c n) -> p c n", c=2),
                                wqkh[:, 2:4, :], ALU.subtract)
        nc.vector.tensor_scalar(bqk[:, 0:1], wqk[:, 4 * P:4 * P + 1], SCALE, None, ALU.mult)
        nc.vector.tensor_copy(bqk[:, 1:2], wqk[:, 4 * P + 1:4 * P + 2]).then_inc(self.wqk_lo, 1)

    def project(self, k, batch, ps, h1h, h1l):
        which, half = self.piece(k)
        t = batch * SEQ + half * HALF
        for q, (w, r) in enumerate(((self.wqkh, h1h), (self.wqkh, h1l), (self.wqkl, h1h))):
            for c in range(DC):
                ins = self.nc.tensor.matmul(ps, w[:, 2 * which + c, :], r[:, c, t:t + HALF],
                                            start=(q + c == 0), stop=(q == 2 and c == DC - 1))
        ins.then_inc(self.q_done, 1)

    def times_cos(self, dve, k, n, ps):
        which, half = self.piece(k)
        dve.wait_ge(self.q_done, n)
        self.nc.vector.scalar_tensor_tensor(out=self.rot[:, k % 2, :], in0=ps, scalar=self.bqk[:, which:which + 1],
                                            in1=self.cos_sin[:, 0, half * HALF:(half + 1) * HALF],
                                            op0=ALU.add, op1=ALU.mult).then_inc(self.q_cos, 1)

    def swap(self, act, k, n, ps):
        which = self.piece(k)[0]
        act.wait_ge(self.q_cos, n)
        wait(act, self.q_rope, n - 2)
        lo, hi = slice(0, HD // 2), slice(HD // 2, HD)
        for to, of in ((lo, hi), (hi, lo)):
            ins = self.nc.scalar.activation(self.swp[to, k % 2, :], ps[of, :], ACT.Identity,
                                            bias=self.bqk[of, which:which + 1])
        ins.then_inc(self.q_swap, 1)

    def times_sin(self, pool, k, n):
        half = self.piece(k)[1]
        pool.wait_ge(self.q_swap, n)
        self.nc.gpsimd.tensor_tensor(self.swp[:, k % 2, :], self.swp[:, k % 2, :],
                                     self.cos_sin[:, 1, half * HALF:(half + 1) * HALF], ALU.mult).then_inc(self.q_sin, 1)

    def rotate(self, pool, k, n):
        pool.wait_ge(self.q_sin, n)
        self.nc.gpsimd.tensor_tensor(self.rot[:, k % 2, :], self.rot[:, k % 2, :], self.swp[:, k % 2, :],
                                     ALU.add).then_inc(self.q_rope, 1)

    def high(self, act, k, n, dst):
        which, half = self.piece(k)
        act.wait_ge(self.q_rope, n)
        self.nc.scalar.activation(dst[:, which, half * HALF:(half + 1) * HALF], self.rot[:, k % 2, :],
                                  ACT.Copy).then_inc(self.q_hi, 1)

    def low(self, dve, k, n, hi, lo):
        which, half = self.piece(k)
        cols = slice(half * HALF, (half + 1) * HALF)
        dve.wait_ge(self.q_hi, n)
        self.nc.vector.tensor_tensor(lo[:, which, cols], self.rot[:, k % 2, :], hi[:, which, cols],
                                     ALU.subtract).then_inc(self.q_lo, 1)


def attention(nc, sh, w1, x2_d, h0_d, h1h, h1l, h1f, acc):
    with ExitStack() as ctx:
        def sb(name, shape, dt=F32):
            return ctx.enter_context(nc.sbuf_tensor(name, shape, dt))

        def pb(name, shape, dt=F32):
            return ctx.enter_context(nc.psum_tensor(name, shape, dt))

        def sem(name):
            return ctx.enter_context(nc.semaphore("b_" + name))

        ident, mask, wv, wov = sh.ident, sh.mask, sh.wv, sh.wov
        w_v, w_ov = sh.w_v, sh.w_ov
        v_loaded, ov_loaded, tables_loaded = sh.v_loaded, sh.ov_loaded, sh.tables_loaded
        qk = sh.qk
        wqk_lo, q_done, q_swap, q_lo = qk.wqk_lo, qk.q_done, qk.q_swap, qk.q_lo
        woh = sb("b_woh", [P, D], F32R)
        wol = sb("b_wol", [P, D], F32R)
        bv = sb("b_bv", [P, 1])
        qkh = [qk.first_h, sb("b_qkh1", [P, 2, SEQ], F32R)]
        qkl = [qk.first_l, sb("b_qkl1", [P, 2, SEQ], F32R)]
        qk.rot, qk.swp = sb("b_rot", [P, 2, HALF]), sb("b_swp", [P, 2, HALF])
        vh = sb("b_vh", [P, QB, HD], F32R)
        vl = sb("b_vl", [P, QB, HD], F32R)
        prob = [sb(f"b_prob{i}", [P, SEQ]) for i in range(4)]
        pth = [sb(f"b_pth{f}", [P, 4 * f + 4, HALF], F32R) for f in range(2)]
        ptl = [sb(f"b_ptl{f}", [P, 4 * f + 4, HALF], F32R) for f in range(2)]
        oh = [sb(f"b_oh{f}", [P, HALF], F32R) for f in range(2)]
        ol = [sb(f"b_ol{f}", [P, HALF], F32R) for f in range(2)]
        nmax = sb("b_nmax", [P, BATCH, QB])
        rsum = sb("b_rsum", [P, BATCH, QB])
        rinv = sb("b_rinv", [P, BATCH, QB])

        ps_s = [pb(f"b_ps_s{i}", [P, 2, HALF]) for i in range(2)]
        ps_t = pb("b_ps_t", [P, 2, HALF])
        ps_m = pb("b_ps_m", [P, 2, HALF])

        zeroed = sem("zeroed")
        wo_hi, wo_lo = sem("wo_hi"), sem("wo_lo")
        masked = sem("masked")
        s_done, max_done, exp_done = sem("s_done"), sem("max_done"), sem("exp_done")
        recip_done, norm_done = sem("recip_done"), sem("norm_done")
        t_done, p_hi, p_lo = sem("t_done"), sem("p_hi"), sem("p_lo")
        v_done, v_hi, v_lo = sem("v_done"), sem("v_hi"), sem("v_lo")
        o_done, o_hi, o_lo = sem("o_done"), sem("o_hi"), sem("o_lo")
        w_done, acc_done = sem("w_done"), sem("acc_done")

        block = ctx.enter_context(nc.Block())

        @block.sync
        def _(sp):
            with sp.Fori(0, HEADS - 1) as h:
                sp.wait_ge(wqk_lo, h + 1)
                sp.dma_start(qk.wqk[:], qk.w_qk[h + 1]).then_inc(qk.qk_loaded, 16)
                sp.wait_ge(wo_lo, h + 1)
                sp.dma_start(wov[:], w_ov[h + 1]).then_inc(ov_loaded, 16)
                sp.wait_ge(v_done, h * 4 + 4)
                sp.dma_start(wv[:], w_v[h + 1].rearrange("p (c n) -> p c n", c=DC)).then_inc(v_loaded, 16)
            sp.wait_ge(v_done, 2 * UNITS)
            sp.dma_start(sh.h0[:], h0_d[0:HALF].rearrange("(t p) d -> p t d", p=P)).then_inc(sh.h0_loaded, 16)
            sp.dma_start(sh.x2[:], x2_d[0:HALF].rearrange("(t p) d -> p t d", p=P)).then_inc(sh.x2_loaded, 16)
            sp.dma_start(sh.w1f[:], w1.rearrange("e (c p) i -> p e c i", p=P)).then_inc(sh.w1_loaded, 16)

        @block.gpsimd
        def _(pool):
            nc.gpsimd.memset(acc[:], 0.0).then_inc(zeroed, 1)
            for f in range(2):
                nc.gpsimd.memset(pth[f][:, 4 * f + 3, 2 * P:3 * P].bitcast(F32), 0.0).then_inc(zeroed, 1)
                nc.gpsimd.memset(ptl[f][:, 4 * f + 3, 2 * P:3 * P].bitcast(F32), 0.0).then_inc(zeroed, 1)
            def work(op, k, u):
                if op == "norm":
                    pool.wait_ge(recip_done, u.count(8, k + 1))
                    row = prob[k % 4][:, 0:(k + 1) * P]
                    nc.gpsimd.tensor_tensor(row, row, rinv[:, u.b, k:k + 1].to_broadcast([P, (k + 1) * P]),
                                            ALU.mult).then_inc(norm_done, 1)
                elif op == "q_sin":
                    qk.times_sin(pool, k, u.count(4, k + 5))
                elif op == "q_rope":
                    qk.rotate(pool, k, u.count(4, k + 5))

            over_units(pool, work)

        @block.scalar
        def _(act):
            def work(op, k, u):
                if op == "split_o":
                    act.wait_ge(ov_loaded, u.head() * 16 + 16)
                    wait(act, w_done, u.count(4, 0))
                    nc.scalar.activation(woh[:], wov[:, 0:D], ACT.Copy).then_inc(wo_hi, 1)
                elif op == "split_qk":
                    act.wait_ge(q_done, u.count(4, 4))
                    qk.split_high(act, u.head(1) * 16 + 16)
                elif op == "exp":
                    act.wait_ge(max_done, u.count(8, k + 1))
                    n = LAST_CHUNK[k - 4] + 1 if k >= 4 else LAST_CHUNK[k + 4] + 1 - NCH
                    wait(act, t_done, u.count(NCH, n))
                    nc.scalar.activation(packed(prob[k % 4], k), spread(ps_s[k % 2], k), ACT.Exp,
                                         bias=nmax[:, u.b, k:k + 1], accum_out=rsum[:, u.b, k:k + 1]).then_inc(exp_done, 1)
                elif op == "p_hi":
                    i, j, n = CHUNKS[k]
                    act.wait_ge(t_done, u.count(NCH, k + 1))
                    nc.scalar.activation(pth[i // 4][:, j:j + n, (i % 4) * P:(i % 4 + 1) * P],
                                         ps_t[:, k % 2, 0:n * P].rearrange("p (n q) -> p n q", n=n),
                                         ACT.Copy).then_inc(p_hi, 1)
                elif op == "q_swap":
                    qk.swap(act, k, u.count(4, k + 5), ps_m[:, bank_of("Q", k), :])
                elif op == "q_hi":
                    qk.high(act, k, u.count(4, k + 5), qkh[1 - u.b])
                elif op == "v_hi":
                    act.wait_ge(v_done, u.count(2, k + 1))
                    nc.scalar.activation(vh[:, 4 * k:4 * k + 4, :],
                                         ps_m[:, bank_of("V", k), :].rearrange("p (n d) -> p n d", n=4),
                                         ACT.Copy).then_inc(v_hi, 1)
                elif op == "o_hi":
                    act.wait_ge(o_done, u.count(2, k + 1))
                    act.wait_ge(wo_lo, u.head() + 1)
                    nc.scalar.activation(oh[k][:], ps_m[:, bank_of("O", k), :], ACT.Identity,
                                         bias=bv[:, 0:1]).then_inc(o_hi, 1)

            over_units(act, work)

        @block.vector
        def _(dve):
            dve.wait_ge(zeroed, 1)
            dve.wait_ge(tables_loaded, 16 * 2)

            def work(op, k, u):
                if op == "split_o":
                    dve.wait_ge(wo_hi, u.head() + 1)
                    nc.vector.tensor_tensor(wol[:], wov[:, 0:D], woh[:], ALU.subtract)
                    nc.vector.tensor_copy(bv[:], wov[:, D:D + 1]).then_inc(wo_lo, 1)
                elif op == "split_qk":
                    dve.wait_ge(q_swap, u.count(4, 4))
                    qk.split_low(dve, u.head(1) + 1)
                    dve.wait_ge(wqk_lo, u.head(1) + 1)
                elif op == "masked":
                    dve.wait_ge(s_done, u.count(8, k + 1))
                    nc.vector.tensor_tensor(diagonal(ps_s[k % 2], k), diagonal(ps_s[k % 2], k), mask[:],
                                            ALU.add).then_inc(masked, 1)
                elif op == "max":
                    dve.wait_ge(masked, u.count(8, k + 1))
                    nc.vector.tensor_reduce(nmax[:, u.b, k:k + 1], spread(ps_s[k % 2], k), AX.XY, ALU.max,
                                            negate=True).then_inc(max_done, 1)
                elif op == "recip":
                    dve.wait_ge(exp_done, u.count(8, k + 1))
                    nc.vector.reciprocal(rinv[:, u.b, k:k + 1], rsum[:, u.b, k:k + 1]).then_inc(recip_done, 1)
                elif op == "p_lo":
                    i, j, n = CHUNKS[k]
                    f, q = i // 4, slice((i % 4) * P, (i % 4 + 1) * P)
                    dve.wait_ge(p_hi, u.count(NCH, k + 1))
                    nc.vector.tensor_tensor(ptl[f][:, j:j + n, q],
                                            ps_t[:, k % 2, 0:n * P].rearrange("p (n q) -> p n q", n=n),
                                            pth[f][:, j:j + n, q], ALU.subtract).then_inc(p_lo, 1)
                elif op == "q_cos":
                    dve.wait_ge(q_lo, u.count(4, k + 3))
                    qk.times_cos(dve, k, u.count(4, k + 5), ps_m[:, bank_of("Q", k), :])
                elif op == "q_lo":
                    qk.low(dve, k, u.count(4, k + 5), qkh[1 - u.b], qkl[1 - u.b])
                elif op == "v_lo":
                    dve.wait_ge(v_hi, u.count(2, k + 1))
                    nc.vector.tensor_tensor(vl[:, 4 * k:4 * k + 4, :],
                                            ps_m[:, bank_of("V", k), :].rearrange("p (n d) -> p n d", n=4),
                                            vh[:, 4 * k:4 * k + 4, :], ALU.subtract).then_inc(v_lo, 1)
                elif op == "o_lo":
                    dve.wait_ge(o_hi, u.count(2, k + 1))
                    nc.vector.scalar_tensor_tensor(out=ol[k][:], in0=ps_m[:, bank_of("O", k), :], scalar=bv[:, 0:1],
                                                   in1=oh[k][:], op0=ALU.add, op1=ALU.subtract).then_inc(o_lo, 1)
                elif op == "acc":
                    dve.wait_ge(w_done, u.count(4, k + 1))
                    t = u.b * SEQ + (k // 2) * HALF
                    to = acc[:, k % 2, t:t + HALF]
                    nc.vector.tensor_tensor(to, ps_m[:, bank_of("W", k), :], to, ALU.add).then_inc(acc_done, 1)

            over_units(dve, work)

        @block.tensor
        def _(pe):
            def bank_free(op, k, u):
                m, off = MISC.index((op, k)), u.off + MISC_AGE[op, k]
                while True:
                    m, off = (m - 2) % len(MISC), off - (m < 2)
                    before, i = MISC[m]
                    v = Unit(u.n, off - MISC_AGE[before, i])
                    if not isinstance(u.n, int):
                        break
                    if off < 0:
                        return
                    if 0 <= v.off < UNITS - (before == "Q"):
                        break
                sem, each, more = {"V": (v_lo, 2, 1), "Q": (q_swap, 4, 5), "O": (o_lo, 2, 1), "W": (acc_done, 4, 1)}[before]
                pe.wait_ge(sem, v.count(each, i + more))

            pe.wait_ge(zeroed, 5)

            def work(op, k, u):
                if op in ("V", "Q", "O", "W") and (op, k) != ("O", 2):
                    bank_free(op, k, u)
                if op == "S":
                    pe.wait_ge(q_lo, u.count(4, 2 if k < 4 else 4))
                    wait(pe, exp_done, u.count(8, k - 1))
                    nb = score_banks(k)
                    w = scores_width(k) // nb
                    q = slice(k * P, (k + 1) * P)
                    for n, (l, r) in enumerate(((qkh, qkh), (qkh, qkl), (qkl, qkh))):
                        for g in range(nb):
                            ins = nc.tensor.matmul(ps_s[k % 2][:, g, 0:w], l[u.b][:, 0, q], r[u.b][:, 1, g * w:(g + 1) * w],
                                                   start=(n == 0), stop=(n == 2))
                    ins.then_inc(s_done, 1)
                elif op == "C":
                    i, j, n = CHUNKS[k]
                    pe.wait_ge(norm_done, u.count(8, i + 1))
                    wait(pe, p_lo, u.count(NCH, k - 1))
                    for a in range(n):
                        ins = nc.tensor.transpose(ps_t[:, k % 2, a * P:(a + 1) * P],
                                                  prob[i % 4][:, (j + a) * P:(j + a + 1) * P], ident[:])
                    ins.then_inc(t_done, 1)
                elif op == "V":
                    pe.wait_ge(v_loaded, u.head() * 16 + 16)
                    for a in range(4):
                        t = u.b * SEQ + (4 * k + a) * P
                        for c in range(DC):
                            ins = nc.tensor.matmul(ps_m[:, bank_of(op, k), a * HD:(a + 1) * HD], h1f[:, c, t:t + P],
                                                   wv[:, c, :], start=(c == 0), stop=(c == DC - 1))
                    ins.then_inc(v_done, 1)
                elif op == "Q":
                    pe.wait_ge(wqk_lo, u.head(1) + 1)
                    qk.project(k, 1 - u.b, ps_m[:, bank_of(op, k), :], h1h, h1l)
                elif op == "O":
                    f = min(k, 1)
                    pe.wait_ge(p_lo, u.count(NCH, CHUNKS_TO_HALF[f]))
                    pe.wait_ge(v_lo, u.count(2, f + 1))
                    last = 4 * f + 3
                    for j in range(4 if k == 2 else 0, 8 if k == 2 else 4):
                        q0 = min(max(0, j - 4 * f) * P, HALF - 2 * P)
                        for n, (l, r) in enumerate(((vh, pth), (vh, ptl), (vl, pth))):
                            ins = nc.tensor.matmul(ps_m[:, bank_of(op, f), q0:HALF], l[:, j, :], r[f][:, j, q0:HALF],
                                                   start=(j == 0 and n == 0), stop=(j == last and n == 2))
                    if k != 1:
                        ins.then_inc(o_done, 1)
                elif op == "W":
                    f, d = k // 2, slice((k % 2) * P, (k % 2 + 1) * P)
                    pe.wait_ge(o_lo, u.count(2, f + 1))
                    pe.wait_ge(wo_lo, u.head() + 1)
                    for n, (l, r) in enumerate(((woh, oh), (woh, ol), (wol, oh))):
                        ins = nc.tensor.matmul(ps_m[:, bank_of(op, k), :], l[:, d], r[f][:], start=(n == 0), stop=(n == 2))
                    ins.then_inc(w_done, 1)

            over_units(pe, work)


EXPERT_PERIOD = 26.75
EXPERT_AT = {
    "att": [0],
    "turn_att": [1.7],
    "h": [5.2],
    "base": [10],
    "stat": [5.5],
    "aggr": [7],
    "eps": [7.3],
    "power": [1.5],
    "norm": [7.5],
    "turn_z": [7],
    "h2_f": [9.5],
    "gate": [12.5],
    "h2_h": [9.5],
    "h2_l": [11.5],
    "route": [11.5],
    "turn_comb": [23],
    "comb_out": [23.5],
    "inner": [15, 15.8, 19.7, 22, 24.9, 28.7, 30.1, 33.4],
    "gelu": [16.3, 17.6, 20, 22.8, 28.2, 30, 30.4, 34.7],
    "hm_hi": [17.4, 18.7, 20.1, 25.4, 28.8, 31.1, 32, 36.8],
    "hm_lo": [12, 16.3, 17.7, 23.5, 27.9, 30.7, 32.6, 35.4],
    "outer": [23.3, 32.1, 36.8, 43.1],
    "bias": [23.5],
    "add": [23.4, 35.2, 38.4, 43.7, 30.8],
}
EXPERT_ORDER = [(op, k, int(x // EXPERT_PERIOD)) for x, op, k in sorted(
    ((x, op, k) for op, at in EXPERT_AT.items() for k, x in enumerate(at)), key=lambda o: o[0] % EXPERT_PERIOD)]
ADDS = sorted(range(EXPERTS + 1), key=lambda k: EXPERT_AT["add"][k])


class Group:

    def __init__(self, n, off):
        self.n, self.off = n, off
        self.first = isinstance(n, int) and off == 0

    def count(self, each, k):
        return self.n * each + (self.off * each + k)

    def cols(self, size):
        if isinstance(self.n, int):
            return slice(self.off * size, (self.off + 1) * size)
        return bass.ds(self.n * size + self.off * size, size)


def over_expert_groups(eng, work):
    def slots(n, off):
        for op, k, age in EXPERT_ORDER:
            if isinstance(n, int) and not 0 <= off - age < GROUPS:
                continue
            work(op, k, Group(n, off - age))

    slots(0, 0)
    slots(0, 1)
    with eng.Fori(0, GROUPS - 2) as n:
        slots(n, 2)
    slots(0, GROUPS)


def experts(nc, sh, w2, x2_d, h0_d, acc, out):
    with ExitStack() as ctx:
        def sb(name, shape, dt=F32):
            return ctx.enter_context(nc.sbuf_tensor(name, shape, dt))

        def pb(name, shape, dt=F32):
            return ctx.enter_context(nc.psum_tensor(name, shape, dt))

        def sem(name):
            return ctx.enter_context(nc.semaphore("c_" + name))

        E = EXPERTS
        TILES = TOK // P
        HM = E * IC
        ident, lnp, wg, bo_sb, b1_sb, b2_sb, earlier = sh.ident, sh.lnp, sh.wg, sh.bo, sh.b1, sh.b2, sh.earlier
        w1f, h0, x2 = sh.w1f, sh.h0, sh.x2
        h0_loaded, x2_loaded, w1_loaded = sh.h0_loaded, sh.x2_loaded, sh.w1_loaded
        w2f = sb("c_w2f", [P, E, IC, D])
        w1h = sb("c_w1h", [P, E, DC, EI], F32R)
        w1l = sb("c_w1l", [P, E, DC, EI], F32R)
        w2h = sb("c_w2h", [P, E, IC, D], F32R)
        w2l = sb("c_w2l", [P, E, IC, D], F32R)
        att = sb("c_att", [P, DC, HALF])
        hg = sb("c_hg", [P, TG, D])
        zg = sb("c_zg", [P, TG, D])
        h2f = sb("c_h2f", [P, DC, HALF])
        h2h = sb("c_h2h", [P, DC, TOK], F32R)
        h2l = sb("c_h2l", [P, DC, TOK], F32R)
        total = sb("c_total", [P, TILES, D])
        stats = sb("c_stats", [P, TG, 6])
        mv = sb("c_mv", [P, TG, 2])
        rstd = sb("c_rstd", [P, TG])
        vare = sb("c_vare", [P, TG])
        mark = sb("c_mark", [P, 1])
        power = sb("c_power", [P, TG])
        most = sb("c_most", [P, TG])
        less = sb("c_less", [P, TG, E])
        prob = sb("c_prob", [P, TG, E])
        inv = sb("c_inv", [P, TG])
        above = sb("c_above", [P, TG, E, E])
        equal = sb("c_equal", [P, TG, E, E])
        rank = sb("c_rank", [P, TG, E])
        comb_g = sb("c_comb_g", [P, TG, E])
        comb = sb("c_comb", [P, TILES * E])
        comb_t = sb("c_comb_t", [E, HALF])
        hmf = [sb(f"c_hmf{i}", [P, HALF]) for i in range(2)]
        hmh = [sb(f"c_hmh{i}", [P, IC, HALF], F32R) for i in range(2)]
        hml = [sb(f"c_hml{i}", [P, IC, HALF], F32R) for i in range(2)]

        ps_a = pb("c_ps_a", [P, DC, HALF])
        ps_rows = ps_a[:].rearrange("p c (a d) -> p (c a) d", a=HALF // D)
        ps_logit = ps_a[:, 0, 0:TG * E].rearrange("p (t e) -> p t e", e=E)
        ps_h = pb("c_ps_h", [P, 2, HALF])
        ps_o = [pb(f"c_ps_o{i}", [P, TG, D]) for i in range(2)]

        att_done, att_turned = sem("att_done"), sem("att_turned")
        h_done, base_done = sem("h_done"), sem("base_done")
        w2_loaded = sem("w2_loaded")
        stat_done, aggr_done, eps_done, rstd_done = sem("stat_done"), sem("aggr_done"), sem("eps_done"), sem("rstd_done")
        power_set, z_done, z_turned = sem("power_set"), sem("z_done"), sem("z_turned")
        h2_f, h2_h, h2_l = sem("h2_f"), sem("h2_h"), sem("h2_l")
        gate_done, route, route_exp = sem("gate_done"), sem("route"), sem("route_exp")
        comb_done, comb_turned, comb_out = sem("comb_done"), sem("comb_turned"), sem("comb_out")
        w1_hi, w1_lo, w2_hi, w2_lo = sem("w1_hi"), sem("w1_lo"), sem("w2_hi"), sem("w2_lo")
        hm_done, gelu_done, hm_hi, hm_lo = sem("hm_done"), sem("gelu_done"), sem("hm_hi"), sem("hm_lo")
        outer_done, bias_done, added = sem("outer_done"), sem("bias_done"), sem("added")
        stored = sem("stored")

        h0_g = h0_d.rearrange("(g t p) d -> g p t d", p=P, t=TG)
        x2_g = x2_d.rearrange("(g t p) d -> g p t d", p=P, t=TG)
        out_g = out.rearrange("(g t p) d -> g p t d", p=P, t=TG)
        ROUTE = 17
        EXPS = [2, 11]
        block = ctx.enter_context(nc.Block())

        @block.sync
        def _(sp):
            sp.dma_start(w2f[:], w2.rearrange("e (c p) d -> p e c d", p=P)).then_inc(w2_loaded, 16)
            with sp.Fori(0, GROUPS - 1) as g:
                sp.wait_ge(h_done, g + 1)
                sp.dma_start(h0[:], h0_g[g + 1]).then_inc(h0_loaded, 16)
                sp.wait_ge(base_done, g + 1)
                sp.dma_start(x2[:], x2_g[g + 1]).then_inc(x2_loaded, 16)
                sp.wait_ge(added, g * len(ADDS) + len(ADDS))
                sp.dma_start(out_g[g], total[:, bass.ds(g * TG, TG), :]).then_inc(stored, 16)
            sp.wait_ge(added, GROUPS * len(ADDS))
            sp.dma_start(out_g[GROUPS - 1], total[:, (GROUPS - 1) * TG:GROUPS * TG, :]).then_inc(stored, 16)
            sp.wait_ge(stored, 16 * GROUPS)

        @block.gpsimd
        def _(pool):
            nc.gpsimd.memset(power[:], -0.5).then_inc(power_set, 1)
            pool.wait_ge(power_set, 1)

            def work(op, k, g):
                if op == "power":
                    pool.wait_ge(eps_done, g.count(1, 1))
                    nc.gpsimd.tensor_tensor(rstd[:], vare[:], power[:], ALU.pow).then_inc(rstd_done, 1)
                    if g.first:
                        pool.wait_ge(w2_hi, 1)
                        nc.gpsimd.tensor_tensor(w2l[:], w2f[:], w2h[:], ALU.subtract).then_inc(w2_lo, 1)
                elif op == "base":
                    pool.wait_ge(h_done, g.count(1, 1))
                    pool.wait_ge(x2_loaded, g.count(16, 16))
                    nc.gpsimd.tensor_tensor(total[:, g.cols(TG), :], x2[:], hg[:], ALU.add).then_inc(base_done, 1)
                elif op == "hm_lo":
                    e, i = k // IC, k % IC
                    pool.wait_ge(hm_hi, g.count(HM, k + 1))
                    nc.gpsimd.tensor_tensor(hml[e % 2][:, i, :], hmf[k % 2][:], hmh[e % 2][:, i, :],
                                            ALU.subtract).then_inc(hm_lo, 1)

            over_expert_groups(pool, work)

        @block.scalar
        def _(act):
            def work(op, k, g):
                if op == "att":
                    if g.first:
                        act.wait_ge(sh.expert_loaded, 16 * len(sh.expert_constants))
                    wait(act, att_turned, g.count(1, 0))
                    for d in range(DC):
                        ins = nc.scalar.activation(att[:, d, :], acc[:, d, g.cols(HALF)], ACT.Identity, bias=bo_sb[:, d:d + 1])
                    ins.then_inc(att_done, 1)
                    if g.first:
                        act.wait_ge(w1_loaded, 16)
                        nc.scalar.activation(w1h[:], w1f[:], ACT.Copy).then_inc(w1_hi, 1)
                        act.wait_ge(w2_loaded, 16)
                        nc.scalar.activation(w2h[:], w2f[:], ACT.Copy).then_inc(w2_hi, 1)
                elif op == "h2_f":
                    act.wait_ge(z_turned, g.count(1, 1))
                    wait(act, gate_done, g.count(1, 0))
                    wait(act, h2_l, g.count(1, 0))
                    for c in range(DC):
                        ins = nc.scalar.activation(h2f[:, c, :], ps_a[:, c, :], ACT.Identity, bias=lnp[:, 1, c:c + 1],
                                                   scale=lnp[:, 0, c:c + 1])
                    ins.then_inc(h2_f, 1)
                elif op == "h2_h":
                    act.wait_ge(h2_f, g.count(1, 1))
                    nc.scalar.activation(h2h[:, :, g.cols(HALF)], h2f[:], ACT.Copy).then_inc(h2_h, 1)
                elif op == "route":
                    for step, dst in zip(EXPS, (prob, rank)):
                        act.wait_ge(route, g.count(ROUTE, step))
                        nc.scalar.activation(dst[:], less[:], ACT.Exp).then_inc(route_exp, 1)
                elif op == "comb_out":
                    act.wait_ge(comb_turned, g.count(1, 1))
                    wait(act, bias_done, g.count(1, 0))
                    nc.scalar.activation(comb_t[:], ps_a[0:E, 0, :], ACT.Copy).then_inc(comb_out, 1)
                elif op == "gelu":
                    e, i = k // IC, k % IC
                    act.wait_ge(hm_done, g.count(HM, k + 1))
                    wait(act, hm_lo, g.count(HM, k - 1))
                    nc.scalar.activation(hmf[k % 2][:], ps_h[:, k % 2, :], ACT.Gelu,
                                         bias=b1_sb[:, e, i:i + 1]).then_inc(gelu_done, 1)
                elif op == "hm_hi":
                    e, i = k // IC, k % IC
                    act.wait_ge(gelu_done, g.count(HM, k + 1))
                    wait(act, outer_done, g.count(E, e - 1))
                    nc.scalar.activation(hmh[e % 2][:, i, :], hmf[k % 2][:], ACT.Copy).then_inc(hm_hi, 1)

            over_expert_groups(act, work)

        @block.vector
        def _(dve):
            def routing(g):
                steps = [0]

                def then(ins):
                    steps[0] += 1
                    ins.then_inc(route, 1)

                def after():
                    dve.wait_ge(route, g.count(ROUTE, steps[0]))

                def bc(a):
                    return a[:, :].unsqueeze(2).to_broadcast([P, TG, E])

                then(nc.vector.tensor_reduce(most[:], ps_logit, AX.X, ALU.max)), after()
                then(nc.vector.tensor_tensor(less[:], ps_logit, bc(most), ALU.subtract)), after()
                dve.wait_ge(route_exp, g.count(2, 1))
                then(nc.vector.tensor_reduce(most[:], prob[:], AX.X, ALU.add)), after()
                then(nc.vector.reciprocal(inv[:], most[:])), after()
                then(nc.vector.tensor_tensor(prob[:], prob[:], bc(inv), ALU.mult)), after()
                one = prob[:].unsqueeze(3).to_broadcast([P, TG, E, E])
                other = prob[:].unsqueeze(2).to_broadcast([P, TG, E, E])
                then(nc.vector.tensor_tensor(above[:], other, one, ALU.is_gt))
                then(nc.vector.tensor_tensor(equal[:], other, one, ALU.is_equal))
                then(nc.vector.tensor_reduce(most[:], prob[:], AX.X, ALU.max)), after()
                then(nc.vector.tensor_tensor(equal[:], equal[:], earlier[:].unsqueeze(1).to_broadcast([P, TG, E, E]),
                                             ALU.mult)), after()
                then(nc.vector.tensor_tensor(above[:], above[:], equal[:], ALU.add))
                then(nc.vector.tensor_tensor(less[:], prob[:], bc(most), ALU.subtract)), after()
                assert steps[0] == EXPS[1]
                then(nc.vector.tensor_reduce(prob[:], above[:], AX.X, ALU.add)), after()
                dve.wait_ge(route_exp, g.count(2, 2))
                then(nc.vector.scalar_tensor_tensor(out=rank[:], in0=prob[:], scalar=1.5, in1=rank[:],
                                                    op0=ALU.is_lt, op1=ALU.mult)), after()
                then(nc.vector.tensor_reduce(most[:], rank[:], AX.X, ALU.add)), after()
                then(nc.vector.reciprocal(inv[:], most[:])), after()
                wait(dve, comb_turned, g.count(1, 0))
                then(nc.vector.tensor_tensor(comb_g[:], rank[:], bc(inv), ALU.mult)), after()
                then(nc.vector.tensor_copy(comb[:, g.cols(TG * E)].rearrange("p (t e) -> p t e", e=E), comb_g[:])), after()
                assert steps[0] == ROUTE

            def work(op, k, g):
                if op == "h":
                    dve.wait_ge(h0_loaded, g.count(16, 16))
                    dve.wait_ge(att_turned, g.count(1, 1))
                    wait(dve, base_done, g.count(1, 0))
                    for r in range(2):
                        rows = slice(2 * r, 2 * r + 2)
                        ins = nc.vector.tensor_tensor(hg[:, rows, :], ps_rows[:, rows, :], h0[:, rows, :], ALU.add)
                    ins.then_inc(h_done, 1)
                elif op == "stat":
                    dve.wait_ge(h_done, g.count(1, 1))
                    for t in range(TG):
                        nc.vector.bn_stats(stats[:, t, :], hg[:, t, :]).then_inc(stat_done, 1)
                elif op == "aggr":
                    dve.wait_ge(stat_done, g.count(TG, TG))
                    nc.vector.memset(mark[:], 0.0)
                    for t in range(TG):
                        ins = nc.vector.bn_aggr(mv[:, t, :], stats[:, t, :])
                    ins.then_inc(aggr_done, 1)
                elif op == "eps":
                    dve.wait_ge(aggr_done, g.count(1, 1))
                    nc.vector.tensor_scalar(vare[:], mv[:, :, 1], EPS, None, ALU.add).then_inc(eps_done, 1)
                elif op == "norm":
                    dve.wait_ge(rstd_done, g.count(1, 1))
                    wait(dve, z_turned, g.count(1, 0))
                    for t in range(TG):
                        ins = nc.vector.tensor_scalar(zg[:, t, :], hg[:, t, :], mv[:, t, 0:1], rstd[:, t:t + 1],
                                                      ALU.subtract, ALU.mult)
                    ins.then_inc(z_done, 1)
                    if g.first:
                        dve.wait_ge(w1_hi, 1)
                        nc.vector.tensor_tensor(w1l[:], w1f[:], w1h[:], ALU.subtract).then_inc(w1_lo, 1)
                        dve.wait_ge(sh.expert_loaded, 16 * len(sh.expert_constants))
                elif op == "h2_l":
                    dve.wait_ge(h2_h, g.count(1, 1))
                    nc.vector.tensor_tensor(h2l[:, :, g.cols(HALF)], h2f[:], h2h[:, :, g.cols(HALF)],
                                            ALU.subtract).then_inc(h2_l, 1)
                elif op == "route":
                    dve.wait_ge(gate_done, g.count(1, 1))
                    routing(g)
                elif op == "add":
                    if k == E:
                        dve.wait_ge(bias_done, g.count(1, 1))
                    else:
                        dve.wait_ge(outer_done, g.count(E, k + 1))
                    dve.wait_ge(base_done, g.count(1, 1))
                    wait(dve, added, g.count(len(ADDS), ADDS.index(k)))
                    for t in range(TG):
                        to = total[:, g.cols(TG), :][:, t, :]
                        if k == E:
                            ins = nc.vector.tensor_tensor(to, ps_rows[:, t, :], to, ALU.add)
                        else:
                            one = t * E + k
                            ins = nc.vector.scalar_tensor_tensor(
                                out=to, in0=ps_o[k % 2][:, t, :], scalar=comb[:, g.cols(TG * E)][:, one:one + 1], in1=to,
                                op0=ALU.mult, op1=ALU.add)
                    ins.then_inc(added, 1)

            over_expert_groups(dve, work)

        @block.tensor
        def _(pe):
            pe.wait_ge(sh.expert_loaded, 16 * len(sh.expert_constants))

            def work(op, k, g):
                if op == "turn_att":
                    pe.wait_ge(att_done, g.count(1, 1))
                    wait(pe, added, g.count(len(ADDS), ADDS.index(E) + 1 - len(ADDS)))
                    for t in range(TG):
                        for d in range(DC):
                            ins = nc.tensor.transpose(ps_rows[:, t, d * P:(d + 1) * P], att[:, d, t * P:(t + 1) * P], ident[:])
                    ins.then_inc(att_turned, 1)
                elif op == "turn_z":
                    pe.wait_ge(z_done, g.count(1, 1))
                    for t in range(TG):
                        for c in range(DC):
                            ins = nc.tensor.transpose(ps_a[:, c, t * P:(t + 1) * P], zg[:, t, c * P:(c + 1) * P], ident[:])
                    ins.then_inc(z_turned, 1)
                elif op == "gate":
                    pe.wait_ge(h2_f, g.count(1, 1))
                    for t in range(TG):
                        for c in range(DC):
                            ins = nc.tensor.matmul(ps_a[:, 0, t * E:(t + 1) * E], h2f[:, c, t * P:(t + 1) * P], wg[:, c, :],
                                                   start=(c == 0), stop=(c == DC - 1))
                    ins.then_inc(gate_done, 1)
                elif op == "turn_comb":
                    pe.wait_ge(route, g.count(ROUTE, ROUTE))
                    for t in range(TG):
                        ins = nc.tensor.transpose(ps_a[0:E, 0, t * P:(t + 1) * P], comb_g[:, t, :], ident[:])
                    ins.then_inc(comb_turned, 1)
                elif op == "bias":
                    pe.wait_ge(comb_out, g.count(1, 1))
                    for t in range(TG):
                        ins = nc.tensor.matmul(ps_rows[:, t, :], comb_t[:, t * P:(t + 1) * P], b2_sb[:], start=True, stop=True)
                    ins.then_inc(bias_done, 1)
                elif op == "inner":
                    e, i = k // IC, k % IC
                    if g.first and k == 0:
                        pe.wait_ge(w1_lo, 1)
                    if k == 0:
                        pe.wait_ge(h2_l, g.count(1, 1))
                    wait(pe, gelu_done, g.count(HM, k - 1))
                    for q, (w, r) in enumerate(((w1h, h2h), (w1h, h2l), (w1l, h2h))):
                        for c in range(DC):
                            ins = nc.tensor.matmul(ps_h[:, k % 2, :], w[:, e, c, i * P:(i + 1) * P], r[:, c, g.cols(HALF)],
                                                   start=(q + c == 0), stop=(q == 2 and c == DC - 1))
                    ins.then_inc(hm_done, 1)
                elif op == "outer":
                    if g.first and k == 0:
                        pe.wait_ge(w2_lo, 1)
                    pe.wait_ge(hm_lo, g.count(HM, (k + 1) * IC))
                    if k >= 2:
                        pe.wait_ge(added, g.count(len(ADDS), ADDS.index(k - 2) + 1))
                    else:
                        wait(pe, added, g.count(len(ADDS), ADDS.index(k + 2) + 1 - len(ADDS)))
                    for t in range(TG):
                        for q, (l, w) in enumerate(((hmh, w2h), (hmh, w2l), (hml, w2h))):
                            for i in range(IC):
                                ins = nc.tensor.matmul(ps_o[k % 2][:, t, :], l[k % 2][:, i, t * P:(t + 1) * P],
                                                       w[:, k, i, :], start=(q + i == 0), stop=(q == 2 and i == IC - 1))
                    ins.then_inc(outer_done, 1)

            over_expert_groups(pe, work)


class Shared:

    def __init__(self, nc, ctx, t, h1f):
        def sb(name, shape, dt=F32):
            return ctx.enter_context(nc.sbuf_tensor(name, shape, dt))

        def sem(name):
            return ctx.enter_context(nc.semaphore(name))

        self.ident, self.ident_d, self.ident_loaded = sb("ident", [P, P]), t["ident"], sem("ident_loaded")
        self.mask, self.mask_d = sb("mask", [P, P]), t["mask"]
        self.qk = QueriesKeys(nc, ctx, t)
        self.tables_loaded = sem("tables_loaded")
        self.wv, self.w_v, self.v_loaded = sb("wv", [P, DC, P]), t["w_v"], sem("v_loaded")
        self.wov, self.w_ov, self.ov_loaded = sb("wov", [P, WOV]), t["w_ov"], sem("ov_loaded")
        self.lnp = sb("ln2", [P, 2, DC])
        self.wg = sb("w_gate", [P, DC, EXPERTS])
        self.bo = sb("bo", [P, DC])
        self.b1 = sb("b1", [P, EXPERTS, IC])
        self.b2 = sb("b2", [EXPERTS, D])
        self.earlier = sb("earlier", [P, EXPERTS, EXPERTS])
        self.expert_constants = ((self.lnp, t["ln2"]), (self.wg, t["w_gate"].rearrange("(c p) e -> p c e", p=P)),
                                 (self.bo, t["bo"]), (self.b1, t["b1"]), (self.b2, t["b2"]), (self.earlier, t["earlier"]))
        self.expert_loaded = sem("expert_loaded")
        self.w1f = h1f[:, 0, :].rearrange("p (e c i) -> p e c i", e=EXPERTS, c=DC)
        rows = h1f[:, 1, :].rearrange("p (r t d) -> p r t d", r=2, t=TG)
        self.h0, self.x2 = rows[:, 0], rows[:, 1]
        self.w1_loaded, self.h0_loaded, self.x2_loaded = sem("w1_loaded"), sem("h0_loaded"), sem("x2_loaded")


def layer(nc, t, x2_d, h0_d, out):
    with ExitStack() as ctx:
        acc = ctx.enter_context(nc.sbuf_tensor("acc", [P, DC, TOK], F32))
        h1f = ctx.enter_context(nc.sbuf_tensor("h1f", [P, DC, TOK], F32))
        sh = Shared(nc, ctx, t, h1f)
        with ExitStack() as held:
            h1h = held.enter_context(nc.sbuf_tensor("h1h", [P, DC, TOK], F32R))
            h1l = held.enter_context(nc.sbuf_tensor("h1l", [P, DC, TOK], F32R))
            conv_layer(nc, sh, t["x"], t["w_in_t"], t["w_out_t"], t["conv_par"], t["ln1"], x2_d, h0_d, h1h, h1l, h1f, acc)
            attention(nc, sh, t["w1"], x2_d, h0_d, h1h, h1l, h1f, acc)
        experts(nc, sh, t["w2"], x2_d, h0_d, acc, out)


def kernel(**inputs):
    import numpy as np
    import concourse.bacc as bacc
    from concourse.bass_utils import run_bass_kernel_spmd as run

    a = {k[3:]: np.asarray(v) for k, v in inputs.items()}

    def per_partition(v, chunks):
        return v.reshape(chunks, P).T

    def head_cols(w, h):
        return w[:, h * HD:(h + 1) * HD].reshape(DC, P, HD).transpose(1, 0, 2).reshape(P, DC * HD)

    heads = range(HEADS)
    q_b, k_b, v_b = (per_partition(a[f"ffn_b{n}"], HEADS) for n in "qkv")
    w_qk = np.stack([np.concatenate([head_cols(a["ffn_wq"], h), head_cols(a["ffn_wk"], h), q_b[:, h:h + 1],
                                     k_b[:, h:h + 1]], 1) for h in heads])
    w_v = np.stack([head_cols(a["ffn_wv"], h) for h in heads])
    w_ov = np.stack([np.concatenate([a["ffn_wo"][h * HD:(h + 1) * HD], v_b[:, h:h + 1]], 1) for h in heads])
    par = np.stack([a["attn_conv_w"][:, 0, j] for j in range(TAPS)] + [a["attn_conv_b"], a["attn_D"]], 1)
    freq = (1.0 / np.power(np.float32(10000.0), np.arange(0, HD, 2, dtype=np.float32) / np.float32(HD))).astype(np.float32)
    angle = (np.arange(SEQ, dtype=np.float32)[:, None] * freq[None]).astype(np.float32).T
    cos, sin = np.cos(angle), np.sin(angle)
    rope = np.stack([np.concatenate([cos, cos]), np.concatenate([-sin, sin])], 1).astype(np.float32)
    mask = np.where(np.arange(P)[None] <= np.arange(P)[:, None], 0.0, BIG)
    t = {
        "x": a["attn_x"].reshape(TOK, D),
        "w_in_t": a["attn_w_in"].T,
        "w_out_t": a["attn_w_out"].T,
        "conv_par": par.reshape(IB, P, TAPS + 2).transpose(1, 0, 2),
        "ln1": np.stack([per_partition(a["ffn_ln1_w"], DC), per_partition(a["ffn_ln1_b"], DC)], 1),
        "ln2": np.stack([per_partition(a["ffn_ln2_w"], DC), per_partition(a["ffn_ln2_b"], DC)], 1),
        "w_qk": w_qk, "w_v": w_v, "w_ov": w_ov, "rope": rope,
        "ident": np.eye(P, dtype=np.float32),
        "mask": mask.astype(np.float32),
        "w_gate": a["ffn_w_gate"],
        "w1": a["ffn_we1"],
        "b1": a["ffn_be1"].reshape(EXPERTS, IC, P).transpose(2, 0, 1),
        "w2": a["ffn_we2"],
        "b2": a["ffn_be2"],
        "bo": per_partition(a["ffn_bo"], DC),
        "earlier": np.broadcast_to(np.tri(EXPERTS, k=-1, dtype=np.float32), (P, EXPERTS, EXPERTS)),
    }
    nc = bacc.Bacc("TRN2", target_bir_lowering=False, num_devices=1)
    arrays, aps = {}, {}
    for name, v in t.items():
        v = np.ascontiguousarray(v)
        arrays[name + "_dram"] = v
        aps[name] = nc.dram_tensor(name + "_dram", v.shape, mybir.dt.from_np(v.dtype), kind="ExternalInput").ap()
    x2_d = nc.dram_tensor("x2_scratch", (TOK, D), F32, kind="Internal").ap()
    h0_d = nc.dram_tensor("h0_scratch", (TOK, D), F32, kind="Internal").ap()
    out = nc.dram_tensor("out_dram", (TOK, D), F32, kind="ExternalOutput").ap()
    layer(nc, aps, x2_d, h0_d, out)
    r = run(nc, [arrays], core_ids=[0])
    return r.results[0]["out_dram"].reshape(BATCH, SEQ, D)
```
